# Optimizing a Trainium2 kernel written in Bass

```python
import numpy as np
import jax
import jax.numpy as jnp

def _softmax(x, axis=-1):
    return jax.nn.softmax(x, axis=axis)

def _gelu(x):
    return jax.nn.gelu(x, approximate=True)

def _silu(x):
    return jax.nn.silu(x)

def _sigmoid(x):
    return jax.nn.sigmoid(x)

def _layernorm(x, axis=-1, eps=1e-05):
    m = jnp.mean(x, axis=axis, keepdims=True)
    v = jnp.var(x, axis=axis, keepdims=True)
    return (x - m) / jnp.sqrt(v + eps)

def _scatter_add(tgt, idx, src, axis=0):
    return tgt.at[idx].add(src)

def _segment_sum(src, seg, n):
    return jax.ops.segment_sum(src, seg, n)
kernel_name = 'mk_gnn_ffn_d1_gnn_r8_565415'

def setup_inputs(seed: int=0):
    np.random.seed(seed)
    _w = jnp.asarray

    def _rec_inputs():
        import jax
        import jax.numpy as jnp
        _gk = jax.random.key(seed)
        x = 0.0001755 + 0.9998 * jax.random.normal(jax.random.fold_in(_gk, 1), (6250, 256), jnp.float32)
        src = jax.random.randint(jax.random.fold_in(_gk, 2), (100000,), 0, 6250, jnp.int32)
        dst = jax.random.randint(jax.random.fold_in(_gk, 3), (100000,), 0, 6250, jnp.int32)
        _o = jnp.argsort(dst, stable=True)
        src = src[_o]
        dst = dst[_o]
        edge_attr_64 = jax.random.uniform(jax.random.fold_in(_gk, 11), (100000, 64), jnp.float32, 0.0, 1)
        return (x, src, dst, edge_attr_64)
    x, src, dst, edge_attr_64 = _rec_inputs()

    def _L0_gnn_setup():
        import jax, jax.numpy as jnp
        import numpy as np
        N, E, HID, NRBF = (1250, 40000, 256, 64)
        key = jax.random.key(seed)
        ks = jax.random.split(key, 12)

        def lin(k, fin, fout):
            bound = 1.0 / np.sqrt(fin)
            kw, kb = jax.random.split(k)
            W = jax.random.uniform(kw, (fin, fout), jnp.float32, -bound, bound)
            b = jax.random.uniform(kb, (fout,), jnp.float32, -bound, bound)
            return (W, b)
        W1, b1 = lin(ks[0], NRBF, HID)
        W2, b2 = lin(ks[1], HID, HID)
        U1, c1 = lin(ks[2], 2 * HID, HID)
        U2, c2 = lin(ks[3], HID, HID)
        h = jax.random.normal(ks[4], (N, HID), jnp.float32)
        edge_index = jax.random.randint(ks[5], (2, E), 0, N, jnp.int64)
        rbf = jax.random.uniform(ks[6], (E, NRBF), jnp.float32)
        return {'h': h, 'edge_index': edge_index, 'rbf': rbf, 'W1': W1, 'b1': b1, 'W2': W2, 'b2': b2, 'U1': U1, 'c1': c1, 'U2': U2, 'c2': c2}
    _L0_gnn_all = _L0_gnn_setup()
    _L0_gnn_in = {k: v for k, v in _L0_gnn_all.items() if k in ('W1', 'b1', 'W2', 'b2', 'U1', 'c1', 'U2', 'c2')}
    del _L0_gnn_all

    def _L0_ffn_setup():
        import jax, jax.numpy as jnp
        import numpy as np
        B, T, D, H, E = (16, 512, 256, 512, 8)
        key = jax.random.key(seed)
        ks = jax.random.split(key, 5)
        x = jax.random.normal(ks[0], (B, T, D), dtype=jnp.float32)
        gate_w = jax.random.normal(ks[1], (D, E), dtype=jnp.float32) * 0.02
        gate_b = jnp.zeros((E,), dtype=jnp.float32)
        W1 = jax.random.normal(ks[2], (E, D, H), dtype=jnp.float32) * 0.02
        b1 = jnp.zeros((E, H), dtype=jnp.float32)
        W2 = jax.random.normal(ks[3], (E, H, D), dtype=jnp.float32) * 0.02
        b2 = jnp.zeros((E, D), dtype=jnp.float32)
        return {'x': x, 'gate_w': gate_w, 'gate_b': gate_b, 'W1': W1, 'b1': b1, 'W2': W2, 'b2': b2}
    _L0_ffn_all = _L0_ffn_setup()
    _L0_ffn_in = {k: v for k, v in _L0_ffn_all.items() if k in ('gate_w', 'gate_b', 'W1', 'b1', 'W2', 'b2')}
    del _L0_ffn_all
    return {'x': x, 'src': src, 'dst': dst, 'edge_attr_64': edge_attr_64, 'L0_gnn_W1': _L0_gnn_in['W1'], 'L0_gnn_b1': _L0_gnn_in['b1'], 'L0_gnn_W2': _L0_gnn_in['W2'], 'L0_gnn_b2': _L0_gnn_in['b2'], 'L0_gnn_U1': _L0_gnn_in['U1'], 'L0_gnn_c1': _L0_gnn_in['c1'], 'L0_gnn_U2': _L0_gnn_in['U2'], 'L0_gnn_c2': _L0_gnn_in['c2'], 'L0_ffn_gate_w': _L0_ffn_in['gate_w'], 'L0_ffn_gate_b': _L0_ffn_in['gate_b'], 'L0_ffn_W1': _L0_ffn_in['W1'], 'L0_ffn_b1': _L0_ffn_in['b1'], 'L0_ffn_W2': _L0_ffn_in['W2'], 'L0_ffn_b2': _L0_ffn_in['b2']}

def reference(x, src, dst, edge_attr_64, L0_gnn_W1, L0_gnn_b1, L0_gnn_W2, L0_gnn_b2, L0_gnn_U1, L0_gnn_c1, L0_gnn_U2, L0_gnn_c2, L0_ffn_gate_w, L0_ffn_gate_b, L0_ffn_W1, L0_ffn_b1, L0_ffn_W2, L0_ffn_b2):
    import jax
    import jax.numpy as jnp

    def _L0_gnn_ref(h, edge_index, rbf, W1, b1, W2, b2, U1, c1, U2, c2):
        import jax, jax.numpy as jnp
        import numpy as np
        N, E, HID, NRBF = (1250, 40000, 256, 64)
        src, dst = (edge_index[0], edge_index[1])
        gate = jax.nn.sigmoid(jax.nn.silu(rbf @ W1 + b1) @ W2 + b2)
        msg = gate * h[src]
        aggr = jax.ops.segment_sum(msg, dst, num_segments=h.shape[0])
        upd = jax.nn.silu(jnp.concatenate([h, aggr], axis=-1) @ U1 + c1) @ U2 + c2
        return h + upd

    def _L0_ffn_ref(x, gate_w, gate_b, W1, b1, W2, b2):
        import jax, jax.numpy as jnp
        import numpy as np
        B, T, D, H, E = (16, 512, 256, 512, 8)
        Bb, Tt, Dd = x.shape
        Ee = gate_w.shape[1]
        xf = x.reshape(-1, Dd)
        N = xf.shape[0]
        logits = xf @ gate_w + gate_b
        probs = jax.nn.softmax(logits, axis=-1)
        top2_vals, top2_idx = jax.lax.top_k(probs, 2)
        cw = jnp.zeros((N, Ee), dtype=xf.dtype).at[jnp.arange(N)[:, None], top2_idx].add(top2_vals)

        def step(acc, params):
            w1, bb1, w2, bb2, we = params
            h = jax.nn.gelu(xf @ w1 + bb1, approximate=False)
            y = h @ w2 + bb2
            return (acc + we[:, None] * y, None)
        out, _ = jax.lax.scan(step, jnp.zeros_like(xf), (W1, b1, W2, b2, cw.T))
        return out.reshape(Bb, Tt, Dd)
    edge_index = jnp.stack([src, dst])
    x = x + _L0_gnn_ref(_layernorm(x, axis=-1), edge_index, edge_attr_64, L0_gnn_W1, L0_gnn_b1, L0_gnn_W2, L0_gnn_b2, L0_gnn_U1, L0_gnn_c1, L0_gnn_U2, L0_gnn_c2)
    x = x + _L0_ffn_ref(_layernorm(x, axis=-1)[None], L0_ffn_gate_w, L0_ffn_gate_b, L0_ffn_W1, L0_ffn_b1, L0_ffn_W2, L0_ffn_b2)[0]
    return x

_drawn_inputs = setup_inputs


def setup_inputs(seed=0):
    import zlib

    import numpy as np

    out = dict(_drawn_inputs(seed))
    spreads = {'L0_ffn_gate_b': (0.0, 0.8), 'L0_ffn_b1': (0.0, 0.8), 'L0_ffn_b2': (0.0, 0.629)}
    factors = {'edge_attr_64': 8.0,
     'L0_gnn_W1': 7.979,
     'L0_gnn_b1': 8.0,
     'L0_gnn_W2': 7.794,
     'L0_gnn_b2': 33.288,
     'L0_gnn_c1': 8.0,
     'L0_gnn_c2': 3.114,
     'L0_ffn_gate_w': 3.997,
     'L0_ffn_W1': 5.742,
     'L0_ffn_W2': 5.398}
    for name, (base, spread) in spreads.items():
        noise = np.random.default_rng([zlib.crc32(name.encode()), seed]).standard_normal(out[name].shape)
        drawn = base * np.exp(spread * noise) if base else spread * noise
        out[name] = jnp.asarray(drawn.astype(out[name].dtype))
    for name, factor in factors.items():
        out[name] = (out[name] * factor).astype(out[name].dtype)
    return out
```

```python
import concourse.bass as bass
import numpy as np
from concourse import mybir
from contextlib import ExitStack

F32 = mybir.dt.float32
F32R = mybir.dt.float32r
I32 = mybir.dt.int32
ALU = mybir.AluOpType
ACT = mybir.ActivationFunctionType
AX = mybir.AxisListType

P = 128
N_NODES = 6250
N_EDGES = 100000
D = 256
DC = D // P
NRBF = 64
NT = -(-N_NODES // P)
NPAD = NT * P
SUP = 512
ST = SUP // P
NS = -(-N_EDGES // SUP)
EPAD = NS * SUP
HALF_S = NS // 2
WIN = 64
AW = NPAD + WIN
GT = 7
NG = NT // GT
GN = GT * P
GH = GN // 2
NE = 8
H = 512
HC = H // P
XB = 512
XT = XB // P
LIST = NPAD + XB
MOST = -(-NPAD // XB)
ALL = 2 * NPAD // XB + NE
CLEAR = -(-ALL * XB // (NG * P))
RES = CLEAR * NG * P
EPS = 1e-5


class Alloc:

    def __init__(self, nc, ctx, stage):
        self.nc, self.ctx, self.stage = nc, ctx, stage

    def sb(self, name, shape, dt=F32):
        return self.ctx.enter_context(self.nc.sbuf_tensor(f"{self.stage}_{name}", shape, dt))

    def ps(self, name, shape):
        return self.ctx.enter_context(self.nc.psum_tensor(f"{self.stage}_{name}", shape, F32))

    def sem(self, name):
        return self.ctx.enter_context(self.nc.semaphore(f"{self.stage}_{name}"))


def inverse_root(dve, chain, r, root, v):
    chain(dve.reciprocal(r, root))
    chain(dve.tensor_tensor(root, r, r, ALU.mult))
    chain(dve.tensor_tensor(root, root, v, ALU.mult))
    chain(dve.tensor_scalar(root, root, -0.5, 1.5, ALU.mult, ALU.add))
    chain(dve.tensor_tensor(r, r, root, ALU.mult))


def normalise(nc, x, half_h, dst_rows, seg_scratch, seg_table):
    with ExitStack() as ctx:
        a = Alloc(nc, ctx, "norm")
        xin = [a.sb(f"x{i}", [P, GT, D]) for i in range(2)]
        hout = [a.sb(f"h{i}", [P, GT, D]) for i in range(2)]
        stats = a.sb("stats", [P, GT, nc.vector.BN_STATS_DIM])
        mv = a.sb("mean_var", [P, GT, nc.vector.BN_AGGR_DIM])
        rstd = a.sb("rstd", [P, GT])
        var = a.sb("var", [P, GT])
        std = a.sb("std", [P, GT])
        rows = a.sb("dst_rows", [HALF_S, 2, SUP], I32)
        rows_f = a.sb("dst_rows_f", [HALF_S, 2, SUP])
        span = a.sb("span", [HALF_S, 2, 2])
        span_i = a.sb("span_i", [HALF_S, 2, 2], I32)
        flat = a.sb("flat", [1, NS, 2], I32)
        flat_f = a.sb("flat_f", [1, NS])
        zeros = a.sb("zeros", [1, NS])
        upto = a.sb("upto", [1, NS])
        table = a.sb("table", [1, NS, 4], I32)
        x_in = [a.sem(f"x_in{i}") for i in range(2)]
        h_out = [a.sem(f"h_out{i}") for i in range(2)]
        h_ready = a.sem("h_ready")
        rows_in = a.sem("rows_in")
        span_ready = a.sem("span_ready")
        span_out = a.sem("span_out")
        flat_in = a.sem("flat_in")
        table_ready = a.sem("table_ready")
        table_out = a.sem("table_out")
        step = a.sem("vector_step")
        var_ready = a.sem("var_ready")
        std_ready = a.sem("std_ready")
        x_v = x.rearrange("(g t p) d -> g p t d", p=P, t=GT)
        h_v = half_h.rearrange("(g t p) d -> g p t d", p=P, t=GT)
        block = ctx.enter_context(nc.Block())

        @block.sync
        def _(sp):
            sp.dma_start(rows[:], dst_rows).then_inc(rows_in, 16)
            for g in range(NG):
                if g >= 2:
                    sp.wait_ge(h_ready, g - 1)
                sp.dma_start(xin[g % 2][:], x_v[g]).then_inc(x_in[g % 2], 16)

        @block.scalar
        def _(act):
            act.wait_ge(span_ready, 1)
            act.dma_start(seg_scratch.rearrange("(a p) c -> p a c", a=2), span_i[:]).then_inc(span_out, 16)
            act.wait_ge(span_out, 16)
            act.dma_start(flat[:], seg_scratch.rearrange("(o s) c -> o s c", o=1)).then_inc(flat_in, 16)
            for g in range(NG):
                act.wait_ge(var_ready, g + 1)
                nc.scalar.activation(std[:], var[:], ACT.Sqrt).then_inc(std_ready, 1)
                act.wait_ge(h_ready, g + 1)
                act.dma_start(h_v[g], hout[g % 2][:]).then_inc(h_out[g % 2], 16)
                if g == 1:
                    act.wait_ge(table_ready, 1)
                    act.dma_start(seg_table, table[:]).then_inc(table_out, 16)
            act.wait_ge(table_out, 16)
            act.wait_ge(h_out[0], 16 * ((NG + 1) // 2))
            act.wait_ge(h_out[1], 16 * (NG // 2))

        @block.vector
        def _(dve):
            n = [0]

            def link(ins):
                n[0] += 1
                ins.then_inc(step, 1)
                dve.wait_ge(step, n[0])

            def spans():
                dve.wait_ge(rows_in, 16)
                link(nc.vector.tensor_copy(rows_f[:], rows[:]))
                nc.vector.tensor_reduce(span[:, :, 0:1], rows_f[:], AX.X, ALU.min)
                link(nc.vector.tensor_reduce(span[:, :, 1:2], rows_f[:], AX.X, ALU.max))
                link(nc.vector.tensor_tensor(span[:, :, 1:2], span[:, :, 1:2], span[:, :, 0:1], ALU.subtract))
                link(nc.vector.tensor_copy(span_i[:], span[:]))
                nc.vector.tensor_scalar(span_i[:, :, 1:2], span_i[:, :, 1:2], WIN.bit_length() - 1, None,
                                        ALU.logical_shift_right).then_inc(span_ready, 1)

            def window_table():
                link(nc.vector.memset(zeros[:], 0.0))
                link(nc.vector.memset(table[:], 0))
                dve.wait_ge(flat_in, 16)
                link(nc.vector.tensor_copy(flat_f[:], flat[:, :, 1]))
                link(nc.vector.tensor_tensor_scan(upto[:], flat_f[:], zeros[:], 0.0, ALU.add, ALU.add))
                link(nc.vector.tensor_tensor(upto[:], upto[:], flat_f[:], ALU.subtract))
                nc.vector.tensor_copy(table[:, :, 0:2], flat[:])
                nc.vector.tensor_copy(table[:, :, 2], upto[:]).then_inc(table_ready, 1)

            spans()
            for g in range(NG):
                dve.wait_ge(x_in[g % 2], 16 * (g // 2 + 1))
                if g >= 2:
                    dve.wait_ge(h_out[g % 2], 16 * (g // 2))
                for t in range(GT):
                    last = nc.vector.bn_stats(stats[:, t, :], xin[g % 2][:, t, :])
                link(last)
                for t in range(GT):
                    last = nc.vector.bn_aggr(mv[:, t, :], stats[:, t, :])
                link(last)
                nc.vector.tensor_scalar(var[:], mv[:, :, 1], EPS, 4.0, ALU.add, ALU.mult).then_inc(var_ready, 1)
                dve.wait_ge(std_ready, g + 1)
                inverse_root(nc.vector, link, rstd[:], std[:], var[:])
                for t in range(GT):
                    last = nc.vector.tensor_scalar(hout[g % 2][:, t, :], xin[g % 2][:, t, :], mv[:, t, 0:1],
                                                   rstd[:, t:t + 1], ALU.subtract, ALU.mult)
                last.then_inc(h_ready, 1)
                if g == 0:
                    window_table()


def split_weight(dve, chain, hi, lo, w):
    chain(dve.tensor_copy(hi, w))
    chain(dve.tensor_tensor(lo, w, hi.bitcast(F32), ALU.subtract))


def edges(nc, aggr, rbf, src_cols, dst_cols, half_h, seg_table, w1, b1, w2, b2):
    with ExitStack() as ctx:
        a = Alloc(nc, ctx, "edge")
        w1f = a.sb("w1f", [P, D])
        w1hi, w1lo = a.sb("w1hi", [P, D], F32R), a.sb("w1lo", [P, D], F32R)
        w2f = a.sb("w2f", [P, DC, D])
        w2hi, w2lo = a.sb("w2hi", [P, DC, D], F32R), a.sb("w2lo", [P, DC, D], F32R)
        b1c = a.sb("b1c", [P, DC])
        b2f = a.sb("b2f", [1, D])
        b2hi, b2lo = a.sb("b2hi", [1, D], F32R), a.sb("b2lo", [1, D], F32R)
        onef = a.sb("onef", [1, P])
        one = a.sb("one", [1, P], F32R)
        src = a.sb("src", [P, NS * ST], I32)
        dst = a.sb("dst", [P, NS * ST], I32)
        dstf = a.sb("dstf", [P, NS * ST])
        node = a.sb("node", [P, AW])
        table = a.sb("table", [1, NS, 4], I32)
        xr = [a.sb(f"x{i}", [P, 2 * SUP]) for i in range(2)]
        xs = [a.sb(f"xs{i}", [P, SUP], F32R) for i in range(2)]
        hid = [a.sb(f"hid{i}", [P, DC, SUP]) for i in range(2)]
        hhi = [a.sb(f"hhi{i}", [P, DC, SUP], F32R) for i in range(2)]
        hlo = [a.sb(f"hlo{i}", [P, DC, SUP], F32R) for i in range(2)]
        msg = [a.sb(f"msg{i}", [P, ST * D]) for i in range(4)]
        ghs = [a.sb(f"ghs{i}", [P, ST, D]) for i in range(4)]
        idx = [a.sb(f"idx{i}", [P, ST], I32) for i in range(4)]
        oh = [a.sb(f"onehot{i}", [P, ST, WIN]) for i in range(2)]
        ohx = a.sb("onehot_extra", [P, ST, WIN])
        p1 = a.ps("p1", [P, DC, SUP])
        p2 = [a.ps(f"p2_{i}", [P, ST, D]) for i in range(2)]
        pg = [a.ps(f"pg{i}", [P, DC, 256]) for i in range(2)]

        consts_in = a.sem("consts_in")
        src_in = a.sem("src_in")
        x_in = [a.sem(f"x_in{i}") for i in range(2)]
        nodes_made = a.sem("nodes_made")
        weights_split = a.sem("weights_split")
        x_split = a.sem("x_split")
        l1_done = a.sem("l1_done")
        silu_done = a.sem("silu_done")
        hi_done = a.sem("hi_done")
        lo_done = a.sem("lo_done")
        l2_done = a.sem("l2_done")
        tanh_done = a.sem("tanh_done")
        rows_in = [a.sem(f"rows_in{i}") for i in range(4)]
        idx_copied = a.sem("idx_copied")
        idx_seen = a.sem("idx_seen")
        msg_done = a.sem("msg_done")
        onehot_done = a.sem("onehot_done")
        sum_done = a.sem("sum_done")
        sum_added = a.sem("sum_added")
        extra_onehot = a.sem("extra_onehot")
        extra_sum = a.sem("extra_sum")
        extra_added = a.sem("extra_added")
        xhi_done = a.sem("xhi_done")
        prep = a.sem("prep")
        block = ctx.enter_context(nc.Block())
        NCONST = 8

        @block.sync
        def _(sp):
            sp.dma_start(src[:], src_cols).then_inc(src_in, 16)
            sp.dma_start(w1f[0:NRBF, :], w1).then_inc(consts_in, 16)
            sp.dma_start(w1f[NRBF:P, :], w1).then_inc(consts_in, 16)
            sp.dma_start(w2f[:], w2.rearrange("(c p) n -> p c n", p=P)).then_inc(consts_in, 16)
            sp.dma_start(b1c[:], b1).then_inc(consts_in, 16)
            sp.dma_start(b2f[:], b2).then_inc(consts_in, 16)
            sp.dma_start(dst[:], dst_cols).then_inc(consts_in, 16)
            sp.dma_start(table[:], seg_table).then_inc(consts_in, 16)

            def load(q, u, first):
                if not first:
                    sp.wait_ge(x_split, 2 * q - 2)
                cols = bass.ds(q * (2 * SUP), 2 * SUP)
                sp.dma_start(xr[u][0:NRBF, :], rbf[:, cols]).then_inc(x_in[u], 16)
                sp.dma_start(xr[u][NRBF:P, :], rbf[:, cols]).then_inc(x_in[u], 16)

            load(0, 0, True)
            load(1, 1, True)
            with sp.Fori(1, NS // 4) as i:
                for u in range(2):
                    load(i * 2 + u, u, False)

        @block.gpsimd
        def _(pool):
            nc.gpsimd.iota(node[:], pattern=[[1, AW]], base=0, channel_multiplier=0,
                           allow_small_or_imprecise_dtypes=True).then_inc(nodes_made, 1)
            nc.gpsimd.memset(aggr[:], 0.0).then_inc(nodes_made, 1)
            pool.wait_ge(src_in, 16)

            def gather(k, u, first):
                if not first:
                    pool.wait_ge(msg_done, k - 3)
                nc.gpsimd.tensor_copy(idx[u][:], src[:, bass.ds(k * ST, ST)]).then_inc(idx_copied, 1)
                pool.wait_ge(idx_copied, k + 1)
                pool.sem_inc(idx_seen, 1)
                for t in range(ST):
                    nc.gpsimd.indirect_dma_start(
                        out=ghs[u][:, t, :], out_offset=None, in_=half_h,
                        in_offset=bass.IndirectOffsetOnAxis(ap=idx[u][:, t:t + 1], axis=0),
                    ).then_inc(rows_in[u], 16)

            for k in range(4):
                gather(k, k, True)
            with pool.Fori(1, NS // 4) as i:
                for u in range(4):
                    gather(i * 4 + u, u, False)

        @block.scalar
        def _(act):
            act.wait_ge(consts_in, 16 * (NCONST - 1))

            def silu(k, u, first):
                act.wait_ge(l1_done, k + 1)
                if not first:
                    act.wait_ge(lo_done, k - 1)
                for c in range(DC):
                    last = nc.scalar.activation(hid[u][:, c, :], p1[:, c, :], ACT.Silu, bias=b1c[:, c:c + 1])
                last.then_inc(silu_done, 1)

            def round_hi(k, u, first):
                act.wait_ge(silu_done, k + 1)
                if not first:
                    act.wait_ge(l2_done, k - 1)
                nc.scalar.activation(hhi[u][:], hid[u][:], ACT.Copy).then_inc(hi_done, 1)

            def tanh(k, u, first):
                act.wait_ge(l2_done, k + 1)
                if not first:
                    act.wait_ge(sum_added, k - 2)
                nc.scalar.activation(msg[u][:], p2[u % 2][:], ACT.Tanh, scale=0.5).then_inc(tanh_done, 1)

            def step(k, u, start):
                silu(k, u % 2, start < 2)
                round_hi(k, u % 2, start < 2)
                if start > 0:
                    tanh(k - 1, (u - 1) % 4, start < 5)

            for k in range(4):
                step(k, k, k)
            step(4, 0, 4)
            for u in range(1, 4):
                step(4 + u, u, 4 + u)
            with act.Fori(2, NS // 4) as i:
                for u in range(4):
                    step(i * 4 + u, u, 8)
            tanh(NS - 1, (NS - 1) % 4, False)

        @block.vector
        def _(dve):
            n = [0]

            def chain(ins):
                n[0] += 1
                ins.then_inc(prep, 1)
                dve.wait_ge(prep, n[0])

            dve.wait_ge(consts_in, 16 * (NCONST - 1))
            split_weight(nc.vector, chain, w1hi[:], w1lo[:], w1f[:])
            split_weight(nc.vector, chain, w2hi[:], w2lo[:], w2f[:])
            split_weight(nc.vector, chain, b2hi[:], b2lo[:], b2f[:])
            chain(nc.vector.memset(onef[:], 1.0))
            chain(nc.vector.tensor_copy(one[:], onef[:]))
            nc.vector.tensor_copy(dstf[:], dst[:]).then_inc(weights_split, 1)
            dve.wait_ge(weights_split, 1)
            dve.wait_ge(nodes_made, 2)

            def split_x(k, u, first, loaded):
                dve.wait_ge(x_in[(u // 2) % 2], loaded)
                if not first:
                    dve.wait_ge(l1_done, k - 1)
                part = xr[(u // 2) % 2][:, (u % 2) * SUP:(u % 2 + 1) * SUP]
                nc.vector.tensor_copy(xs[u % 2][:], part).then_inc(xhi_done, 1)
                dve.wait_ge(xhi_done, k + 1)
                nc.vector.tensor_tensor(xs[u % 2][NRBF:P, :], part[NRBF:P, :], xs[u % 2][NRBF:P, :].bitcast(F32),
                                        ALU.subtract).then_inc(x_split, 1)

            def lo(k, u, first):
                dve.wait_ge(hi_done, k + 1)
                if not first:
                    dve.wait_ge(l2_done, k - 1)
                nc.vector.tensor_tensor(hlo[u % 2][:], hid[u % 2][:], hhi[u % 2][:].bitcast(F32),
                                        ALU.subtract).then_inc(lo_done, 1)

            def message(k, u, filled):
                dve.wait_ge(tanh_done, k + 1)
                dve.wait_ge(rows_in[u], filled)
                nc.vector.scalar_tensor_tensor(out=msg[u][:], in0=msg[u][:], scalar=1.0,
                                               in1=ghs[u][:].rearrange("p t d -> p (t d)"),
                                               op0=ALU.add, op1=ALU.mult).then_inc(msg_done, 1)

            def compare(out, k, w0):
                return nc.vector.tensor_tensor(
                    out, node[:, bass.ds(w0, WIN)].unsqueeze(1).broadcast_to([P, ST, WIN]),
                    dstf[:, bass.ds(k * ST, ST)].unsqueeze(2).broadcast_to([P, ST, WIN]), ALU.is_equal)

            def first_node(k):
                return dve.value_load(table[0:1, bass.ds(k, 1), 0:1].rearrange("o s c -> o (s c)"),
                                      min_val=0, max_val=NPAD - 1)

            def onehot(k, u, first):
                if not first:
                    dve.wait_ge(sum_done, k - 1)
                compare(oh[u % 2][:], k, first_node(k)).then_inc(onehot_done, 1)

            def add(k, u, first):
                w0 = first_node(k)
                dve.wait_ge(sum_done, k + 1)
                if not first:
                    dve.wait_ge(sum_added, k)
                part = aggr[:, :, bass.ds(w0, WIN)]
                nc.vector.tensor_tensor(part, part, pg[u % 2][:, :, 0:WIN], ALU.add).then_inc(sum_added, 1)
                extra(k, u)

            def extra(k, u):
                count = dve.value_load(table[0:1, bass.ds(k, 1), 1:2].rearrange("o s c -> o (s c)"),
                                       min_val=0, max_val=NPAD // WIN)
                with dve.If(count > 0):
                    w0 = first_node(k)
                    before = dve.value_load(table[0:1, bass.ds(k, 1), 2:3].rearrange("o s c -> o (s c)"),
                                            min_val=0, max_val=NS * (NPAD // WIN))
                    with dve.Fori(0, count) as j:
                        dve.wait_ge(sum_added, k + 1)
                        start = nc.s_assert_within(
                            w0 + j * WIN + WIN, 0, NPAD - 1,
                            skip_runtime_bounds_check_because="it is at most the superblock's last node")
                        compare(ohx[:], k, start).then_inc(extra_onehot, 1)
                        dve.wait_ge(extra_sum, before + j + 1)
                        part = aggr[:, :, bass.ds(start, WIN)]
                        nc.vector.tensor_tensor(part, part, pg[u % 2][:, :, 0:WIN], ALU.add)\
                            .then_inc(extra_added, 1)
                        dve.wait_ge(extra_added, before + j + 1)

            def step(k, u, start, loaded, filled):
                split_x(k + 1, (u + 1) % 4, start < 1, loaded)
                lo(k, u, start < 2)
                if start >= 1:
                    message(k - 1, (u - 1) % 4, filled)
                    onehot(k - 1, (u - 1) % 4, start < 3)
                if start >= 3:
                    add(k - 3, (u - 3) % 4, start < 4)

            def loads(s):
                return 32 * (s // 4 + 1)

            def fills(s):
                return 16 * ST * (s // 4 + 1)

            split_x(0, 0, True, loads(0))
            for k in range(8):
                step(k, k % 4, k, loads(k + 1), fills(k - 1))
            with dve.Fori(2, NS // 4 - 1) as i:
                for u in range(4):
                    more = 1 if u == 3 else 0
                    less = 1 if u == 0 else 0
                    step(i * 4 + u, u, 8, i * 32 + 32 * (1 + more), i * (16 * ST) + 16 * ST * (1 - less))
            for k in range(NS - 4, NS):
                u = k % 4
                if k + 1 < NS:
                    split_x(k + 1, (u + 1) % 4, False, loads(k + 1))
                lo(k, u, False)
                message(k - 1, (u - 1) % 4, fills(k - 1))
                onehot(k - 1, (u - 1) % 4, False)
                add(k - 3, (u - 3) % 4, False)
            message(NS - 1, (NS - 1) % 4, fills(NS - 1))
            onehot(NS - 1, (NS - 1) % 4, False)
            for k in range(NS - 3, NS):
                add(k, k % 4, False)

        @block.tensor
        def _(pe):
            pe.wait_ge(weights_split, 1)
            pe.wait_ge(consts_in, 16 * (NCONST - 1))
            mm = nc.tensor.matmul

            def layer1(k, u, first):
                pe.wait_ge(x_split, k + 1)
                if not first:
                    pe.wait_ge(silu_done, k)
                for c in range(DC):
                    cols = slice(c * P, (c + 1) * P)
                    mm(p1[:, c, :], w1hi[:, cols], xs[u % 2][:], start=True, stop=False)
                    last = mm(p1[:, c, :], w1lo[:, cols], xs[u % 2][:], start=False, stop=True)
                last.then_inc(l1_done, 1)

            def layer2(k, u, first):
                pe.wait_ge(lo_done, k + 1)
                if not first:
                    pe.wait_ge(tanh_done, k - 1)
                for t in range(ST):
                    out = p2[u % 2][:, t, :]
                    mm(out, one[:], b2hi[:], start=True, stop=False)
                    mm(out, one[:], b2lo[:], start=False, stop=False)
                    for c in range(DC):
                        hi = hhi[u % 2][:, c, t * P:(t + 1) * P]
                        lo = hlo[u % 2][:, c, t * P:(t + 1) * P]
                        mm(out, hi, w2hi[:, c, :], start=False, stop=False)
                        mm(out, hi, w2lo[:, c, :], start=False, stop=False)
                        last = mm(out, lo, w2hi[:, c, :], start=False, stop=c == DC - 1)
                last.then_inc(l2_done, 1)

            def segment(k, u, one_hot):
                for c in range(DC):
                    for t in range(ST):
                        last = mm(pg[u % 2][:, c, 0:WIN], msg[u % 4][:, t * D + c * P:t * D + (c + 1) * P],
                                  one_hot[:, t, :], start=t == 0, stop=t == ST - 1)
                return last

            def window(k, u, first):
                pe.wait_ge(msg_done, k + 1)
                pe.wait_ge(onehot_done, k + 1)
                if not first:
                    pe.wait_ge(sum_added, k - 1)
                segment(k, u, oh[u % 2]).then_inc(sum_done, 1)

            def extra(k, u):
                count = pe.value_load(table[0:1, bass.ds(k, 1), 1:2].rearrange("o s c -> o (s c)"),
                                      min_val=0, max_val=NPAD // WIN)
                with pe.If(count > 0):
                    before = pe.value_load(table[0:1, bass.ds(k, 1), 2:3].rearrange("o s c -> o (s c)"),
                                           min_val=0, max_val=NS * (NPAD // WIN))
                    with pe.Fori(0, count) as j:
                        pe.wait_ge(extra_onehot, before + j + 1)
                        segment(k, u, ohx).then_inc(extra_sum, 1)
                    pe.wait_ge(extra_added, before + count)

            def step(k, u, start):
                layer1(k, u, start < 1)
                if start >= 1:
                    layer2(k - 1, (u - 1) % 4, start < 3)
                if start >= 2:
                    window(k - 2, (u - 2) % 4, start < 4)
                if start >= 3:
                    extra(k - 3, (u - 3) % 4)

            for k in range(4):
                step(k, k, k)
            with pe.Fori(1, NS // 4) as i:
                for u in range(4):
                    step(i * 4 + u, u, 4)
            layer2(NS - 1, (NS - 1) % 4, False)
            window(NS - 2, (NS - 2) % 4, False)
            extra(NS - 3, (NS - 3) % 4)
            window(NS - 1, (NS - 1) % 4, False)
            extra(NS - 2, (NS - 2) % 4)
            extra(NS - 1, (NS - 1) % 4)


def nodes(nc, aggr, route, x, half_h, x1_rows, lists, results, u1, c1, u2, c2, gate_w, gate_b):
    slot_a, slot_b, weight_a, weight_b, fill, _, _ = route
    with ExitStack() as ctx:
        a = Alloc(nc, ctx, "node")
        BF = mybir.dt.bfloat16
        zeros = a.sb("zeros", [P, 1, D])
        u1f = a.sb("u1", [P, 2 * DC, D])
        u2f = a.sb("u2", [P, DC, D])
        gw = a.sb("gate_w", [P, DC, NE])
        c1c = a.sb("c1", [P, DC])
        c2r = a.sb("c2", [P, D])
        gb = a.sb("gate_b", [P, NE])
        ident = a.sb("ident", [P, P])
        below = a.sb("below", [P, P], BF)
        ones = a.sb("ones", [P, P], BF)
        lower = a.sb("lower", [P, NE, NE])
        xg = [a.sb(f"x{i}", [P, GT, D]) for i in range(2)]
        hg = [a.sb(f"h{i}", [P, GT, D]) for i in range(2)]
        ht = a.sb("ht", [P, DC, GN])
        s2 = a.sb("s2", [P, DC, GN])
        x1 = [a.sb(f"x1_{i}", [P, GT, D]) for i in range(2)]
        f = [a.sb(f"f{i}", [P, GT, D]) for i in range(2)]
        ft = a.sb("ft", [P, DC, GN])
        stats = a.sb("stats", [P, GT, nc.vector.BN_STATS_DIM])
        mv = a.sb("mean_var", [P, GT, nc.vector.BN_AGGR_DIM])
        var = a.sb("var", [P, GT])
        std = a.sb("std", [P, GT])
        rstd = a.sb("rstd", [P, GT])
        logit = a.sb("logit", [P, GT, NE])
        prob = a.sb("prob", [P, GT, NE])
        top = a.sb("top", [P, GT])
        beats = a.sb("beats", [P, GT, NE, NE])
        ties = a.sb("ties", [P, GT, NE, NE])
        rank = a.sb("rank", [P, GT, NE])
        first = a.sb("first", [P, GT, NE])
        second = a.sb("second", [P, GT, NE])
        chosen = a.sb("chosen", [P, GT, NE], BF)
        place = a.sb("place", [P, GT, NE])
        pick = a.sb("pick", [P, GT, NE])
        slot_f = a.sb("slot_f", [P, 2, GT])
        ia = [a.sb(f"ia{i}", [P, GT], I32) for i in range(2)]
        ib = [a.sb(f"ib{i}", [P, GT], I32) for i in range(2)]
        pa = a.ps("pa", [P, 2 * DC, 512])
        pb = a.ps("pb", [P, 2 * DC, 512])
        cut = (slice(0, 4 * P), slice(4 * P, GN))
        plogit = pa[:, 3, 256:256 + GT * NE].rearrange("p (t e) -> p t e", e=NE)
        pplace = pa[:, 3, 320:320 + GT * NE]
        ptotal = pa[:, 3, 384:384 + NE]

        consts_in = a.sem("consts_in")
        masks = a.sem("masks")
        cleared = a.sem("cleared")
        mask_zero = a.sem("mask_zero")
        prep = a.sem("prep")
        x_in = [a.sem(f"x_in{i}") for i in range(2)]
        h_turned = a.sem("h_turned")
        h_copied = a.sem("h_copied")
        u1_done = a.sem("u1_done")
        s2_done = a.sem("s2_done")
        u2_done = a.sem("u2_done")
        x1_done = a.sem("x1_done")
        var_done = a.sem("var_done")
        std_done = a.sem("std_done")
        f_done = a.sem("f_done")
        f_turned = a.sem("f_turned")
        f_copied = a.sem("f_copied")
        logit_done = a.sem("logit_done")
        shift_done = a.sem("shift_done")
        exp_done = a.sem("exp_done")
        chosen_done = a.sem("chosen_done")
        place_done = a.sem("place_done")
        slots_done = a.sem("slots_done")
        slots_seen = a.sem("slots_seen")
        f_sent = [a.sem(f"f_sent{i}") for i in range(2)]
        x1_out = [a.sem(f"x1_out{i}") for i in range(2)]
        step_done = a.sem("vector_step")
        stats_seen = a.sem("stats_seen")
        block = ctx.enter_context(nc.Block())
        NCONST = 6
        LOOPS = NG // 2

        def rows(ap, g):
            return ap[bass.ds(g * GN, GN), :].rearrange("(t p) d -> p t d", p=P)

        @block.sync
        def _(sp):
            sp.dma_start(u1f[:], u1.rearrange("(c p) n -> p c n", p=P)).then_inc(consts_in, 16)
            sp.dma_start(u2f[:], u2.rearrange("(c p) n -> p c n", p=P)).then_inc(consts_in, 16)
            sp.dma_start(gw[:], gate_w.rearrange("(c p) n -> p c n", p=P)).then_inc(consts_in, 16)
            sp.dma_start(c1c[:], c1).then_inc(consts_in, 16)
            sp.dma_start(c2r[:], c2.partition_broadcast(P)).then_inc(consts_in, 16)
            sp.dma_start(gb[:], gate_b.partition_broadcast(P)).then_inc(consts_in, 16)

            def load(g, u, early):
                if not early:
                    sp.wait_ge(x1_done, g - 1)
                sp.dma_start(xg[u][:], rows(x, g)).then_inc(x_in[u], 16)
                sp.dma_start(hg[u][:], rows(half_h, g)).then_inc(x_in[u], 16)

            def clear(g):
                out = results[bass.ds(g * (CLEAR * P), CLEAR * P), :].rearrange("(t p) d -> p t d", p=P)
                sp.dma_start(out, zeros[:].broadcast_to([P, CLEAR, D])).then_inc(cleared, 16)

            def store(g, u):
                clear(g)
                sp.wait_ge(x1_done, g + 1)
                sp.dma_start(rows(x1_rows, g), x1[u][:]).then_inc(x1_out[u], 16)

            load(0, 0, True)
            load(1, 1, True)
            sp.wait_ge(masks, 5)
            with sp.Fori(0, LOOPS - 1) as i:
                for u in range(2):
                    store(i * 2 + u, u)
                    load(i * 2 + u + 2, u, False)
            store(NG - 3, 0)
            load(NG - 1, 0, False)
            store(NG - 2, 1)
            store(NG - 1, 0)
            sp.wait_ge(cleared, 16 * NG)
            sp.wait_ge(x1_out[0], 16 * ((NG + 1) // 2))
            sp.wait_ge(x1_out[1], 16 * (NG // 2))

        @block.gpsimd
        def _(pool):
            nc.gpsimd.memset(ident[:], 0.0).then_inc(mask_zero, 1)
            nc.gpsimd.memset(below[:], 1.0).then_inc(mask_zero, 1)
            nc.gpsimd.memset(lower[:], 1.0).then_inc(mask_zero, 1)
            nc.gpsimd.memset(ones[:], 1.0).then_inc(masks, 1)
            nc.gpsimd.memset(zeros[:], 0.0).then_inc(masks, 1)
            pool.wait_ge(mask_zero, 3)
            nc.gpsimd.affine_select(out=ident[:], in_=ident[:], compare_op=ALU.not_equal, fill=1.0, base=0,
                                    pattern=[[-1, P]], channel_multiplier=1).then_inc(masks, 1)
            nc.gpsimd.affine_select(out=below[:], in_=below[:], compare_op=ALU.is_gt, fill=0.0, base=0,
                                    pattern=[[1, P]], channel_multiplier=-1).then_inc(masks, 1)
            nc.gpsimd.affine_select(out=lower[:], in_=lower[:], compare_op=ALU.is_gt, fill=0.0, base=0,
                                    pattern=[[1, NE], [-1, NE]], channel_multiplier=0).then_inc(masks, 1)

            def scatter(g, u):
                pool.wait_ge(slots_done, g + 1)
                pool.sem_inc(slots_seen, 1)
                for t in range(GT):
                    for index in (ia[u], ib[u]):
                        nc.gpsimd.indirect_dma_start(
                            out=lists, out_offset=bass.IndirectOffsetOnAxis(ap=index[:, t:t + 1], axis=0),
                            in_=f[u][:, t, :], in_offset=None).then_inc(f_sent[u], 16)

            with pool.Fori(0, LOOPS) as i:
                for u in range(2):
                    scatter(i * 2 + u, u)
            scatter(NG - 1, 0)
            pool.wait_ge(f_sent[0], 16 * 2 * GT * ((NG + 1) // 2))
            pool.wait_ge(f_sent[1], 16 * 2 * GT * (NG // 2))

        @block.scalar
        def _(act):
            act.wait_ge(consts_in, 16 * NCONST)

            def group(g, early):
                act.wait_ge(h_turned, g + 1)
                for c in range(DC):
                    for half in range(2):
                        cols = cut[half]
                        last = nc.scalar.activation(ht[:, c, cols], pa[:, 2 * c + half, 0:cols.stop - cols.start],
                                                    ACT.Copy)
                last.then_inc(h_copied, 1)
                act.wait_ge(u1_done, g + 1)
                for c in range(DC):
                    for half in range(2):
                        cols = cut[half]
                        last = nc.scalar.activation(s2[:, c, cols], pb[:, 2 * c + half, 0:cols.stop - cols.start],
                                                    ACT.Silu, bias=c1c[:, c:c + 1])
                last.then_inc(s2_done, 1)
                act.wait_ge(var_done, g + 1)
                nc.scalar.activation(std[:], var[:], ACT.Sqrt).then_inc(std_done, 1)
                act.wait_ge(f_turned, g + 1)
                for c in range(DC):
                    for half in range(2):
                        cols = cut[half]
                        last = nc.scalar.activation(ft[:, c, cols], pb[:, 2 * c + half, 0:cols.stop - cols.start],
                                                    ACT.Copy)
                last.then_inc(f_copied, 1)
                act.wait_ge(shift_done, g + 1)
                nc.scalar.activation(prob[:], logit[:], ACT.Exp).then_inc(exp_done, 1)

            with act.Fori(0, NG) as g:
                group(g, False)

        @block.tensor
        def _(pe):
            mm = nc.tensor.matmul
            pe.wait_ge(consts_in, 16 * NCONST)
            pe.wait_ge(masks, 5)
            pe.wait_ge(prep, 1)

            def turn(out, tiles):
                for c in range(DC):
                    for t in range(GT):
                        last = nc.tensor.transpose(out[:, 2 * c + t // 4, (t % 4) * P:(t % 4 + 1) * P],
                                                   tiles[:, t, c * P:(c + 1) * P], ident[:])
                return last

            def group(g, u, loaded):
                pe.wait_ge(x_in[u], loaded)
                pe.wait_ge(slots_done, g)
                turn(pa, hg[u]).then_inc(h_turned, 1)
                pe.wait_ge(h_copied, g + 1)
                for m in range(DC):
                    for half in range(2):
                        cols = cut[half]
                        width = cols.stop - cols.start
                        for c in range(2 * DC):
                            if c < DC:
                                moving = ht[:, c, cols]
                            else:
                                moving = aggr[:, c - DC, bass.ds(g * GN + cols.start, width)]
                            last = mm(pb[:, 2 * m + half, 0:width], u1f[:, c, m * P:(m + 1) * P], moving,
                                      start=c == 0, stop=c == 2 * DC - 1)
                last.then_inc(u1_done, 1)
                pe.wait_ge(s2_done, g + 1)
                for t in range(GT):
                    for c in range(DC):
                        last = mm(pa[:, t // 2, (t % 2) * D:(t % 2 + 1) * D], s2[:, c, t * P:(t + 1) * P],
                                  u2f[:, c, :], start=c == 0, stop=c == DC - 1)
                last.then_inc(u2_done, 1)
                pe.wait_ge(f_done, g + 1)
                turn(pb, f[u]).then_inc(f_turned, 1)
                pe.wait_ge(f_copied, g + 1)
                for t in range(GT):
                    for c in range(DC):
                        last = mm(plogit[:, t, :], ft[:, c, t * P:(t + 1) * P], gw[:, c, :],
                                  start=c == 0, stop=c == DC - 1)
                last.then_inc(logit_done, 1)
                pe.wait_ge(chosen_done, g + 1)
                sel = chosen[:].rearrange("p t e -> p (t e)")
                mm(pplace, below[:], sel, start=True, stop=False, skip_group_check=True)
                for d in range(1, GT):
                    mm(pplace[:, d * NE:], ones[:], sel[:, 0:(GT - d) * NE], start=False, stop=d == GT - 1,
                       skip_group_check=True)
                for t in range(GT):
                    last = mm(ptotal, ones[:], chosen[:, t, :], start=t == 0, stop=t == GT - 1,
                              skip_group_check=True)
                last.then_inc(place_done, 1)

            with pe.Fori(0, LOOPS) as i:
                for u in range(2):
                    group(i * 2 + u, u, i * 32 + 32)
            group(NG - 1, 0, 32 * (LOOPS + 1))

        @block.vector
        def _(dve):
            dve.wait_ge(consts_in, 16 * NCONST)
            nc.vector.tensor_scalar(u1f[:, 0:DC, :], u1f[:, 0:DC, :], 2.0, None, ALU.mult).then_inc(prep, 1)
            for e in range(NE):
                last = nc.vector.memset(fill[:, e:e + 1], float(e * LIST))
            last.then_inc(prep, 1)
            dve.wait_ge(prep, 2)
            dve.wait_ge(masks, 5)

            def group(g, u, loaded, sent, stored):
                n = [0]
                LINKS = 24

                def link(ins):
                    n[0] += 1
                    ins.then_inc(step_done, 1)
                    dve.wait_ge(step_done, g * LINKS + n[0])

                wide = [P, GT, NE, NE]
                dve.wait_ge(x_in[u], loaded)
                if stored is not None:
                    dve.wait_ge(x1_out[u], stored)
                    dve.wait_ge(f_sent[u], sent)
                link(nc.vector.scalar_tensor_tensor(out=x1[u][:], in0=hg[u][:], scalar=2.0, in1=xg[u][:],
                                                    op0=ALU.mult, op1=ALU.add))
                link(nc.vector.tensor_tensor(x1[u][:], x1[u][:], c2r[:].unsqueeze(1).broadcast_to([P, GT, D]),
                                             ALU.add))
                dve.wait_ge(u2_done, g + 1)
                flat = x1[u][:].rearrange("p t d -> p (t d)")
                update = pa[:].rearrange("p b n -> p (b n)")[:, 0:GT * D]
                nc.vector.tensor_tensor(flat, flat, update, ALU.add).then_inc(x1_done, 1)
                dve.wait_ge(x1_done, g + 1)
                for t in range(GT):
                    last = nc.vector.bn_stats(stats[:, t, :], x1[u][:, t, :])
                link(last)
                dve.sem_inc(stats_seen, 1)
                for t in range(GT):
                    last = nc.vector.bn_aggr(mv[:, t, :], stats[:, t, :])
                link(last)
                nc.vector.tensor_scalar(var[:], mv[:, :, 1], EPS, None, ALU.add).then_inc(var_done, 1)
                dve.wait_ge(std_done, g + 1)
                inverse_root(nc.vector, link, rstd[:], std[:], var[:])
                for t in range(GT):
                    last = nc.vector.tensor_scalar(f[u][:, t, :], x1[u][:, t, :], mv[:, t, 0:1],
                                                   rstd[:, t:t + 1], ALU.subtract, ALU.mult)
                last.then_inc(f_done, 1)
                dve.wait_ge(logit_done, g + 1)
                link(nc.vector.tensor_tensor(logit[:], plogit, gb[:].unsqueeze(1).broadcast_to([P, GT, NE]),
                                             ALU.add))
                link(nc.vector.tensor_reduce(top[:], logit[:], AX.X, ALU.max))
                nc.vector.tensor_tensor(logit[:], logit[:], top[:].unsqueeze(2).broadcast_to([P, GT, NE]),
                                        ALU.subtract).then_inc(shift_done, 1)
                dve.wait_ge(exp_done, g + 1)
                link(nc.vector.tensor_reduce(top[:], prob[:], AX.X, ALU.add))
                link(nc.vector.reciprocal(top[:], top[:]))
                link(nc.vector.tensor_tensor(prob[:], prob[:], top[:].unsqueeze(2).broadcast_to([P, GT, NE]),
                                             ALU.mult))
                other = prob[:].unsqueeze(2).broadcast_to(wide)
                own = prob[:].unsqueeze(3).broadcast_to(wide)
                nc.vector.tensor_tensor(beats[:], other, own, ALU.is_gt)
                link(nc.vector.tensor_tensor(ties[:], other, own, ALU.is_equal))
                link(nc.vector.tensor_tensor(ties[:], ties[:], lower[:].unsqueeze(1).broadcast_to(wide), ALU.mult))
                link(nc.vector.tensor_tensor(beats[:], beats[:], ties[:], ALU.add))
                link(nc.vector.tensor_reduce(rank[:], beats[:], AX.X, ALU.add))
                nc.vector.tensor_scalar(chosen[:], rank[:], 2.0, None, ALU.is_lt).then_inc(chosen_done, 1)
                nc.vector.tensor_scalar(first[:], rank[:], 0.0, None, ALU.is_equal)
                link(nc.vector.tensor_scalar(second[:], rank[:], 1.0, None, ALU.is_equal))
                tiles = bass.ds(g * GT, GT)
                link(nc.vector.tensor_tensor(pick[:], first[:], prob[:], ALU.mult))
                nc.vector.tensor_reduce(weight_a[:, tiles], pick[:], AX.X, ALU.add)
                link(nc.vector.tensor_tensor(rank[:], second[:], prob[:], ALU.mult))
                nc.vector.tensor_reduce(weight_b[:, tiles], rank[:], AX.X, ALU.add)
                dve.wait_ge(place_done, g + 1)
                link(nc.vector.tensor_tensor(place[:], pplace.rearrange("p (t e) -> p t e", e=NE),
                                             fill[:].unsqueeze(1).broadcast_to([P, GT, NE]), ALU.add))
                nc.vector.tensor_tensor(fill[:], fill[:], ptotal, ALU.add)
                nc.vector.tensor_tensor(first[:], first[:], place[:], ALU.mult)
                link(nc.vector.tensor_tensor(second[:], second[:], place[:], ALU.mult))
                nc.vector.tensor_reduce(slot_f[:, 0, :], first[:], AX.X, ALU.add)
                link(nc.vector.tensor_reduce(slot_f[:, 1, :], second[:], AX.X, ALU.add))
                nc.vector.tensor_copy(slot_a[:, tiles], slot_f[:, 0, :])
                nc.vector.tensor_copy(slot_b[:, tiles], slot_f[:, 1, :])
                nc.vector.tensor_copy(ia[u][:], slot_f[:, 0, :])
                nc.vector.tensor_copy(ib[u][:], slot_f[:, 1, :]).then_inc(slots_done, 1)
                dve.wait_ge(slots_done, g + 1)
                assert n[0] == LINKS, n[0]

            for u in range(2):
                group(u, u, 32, None, None)
            with dve.Fori(1, LOOPS) as i:
                for u in range(2):
                    group(i * 2 + u, u, i * 32 + 32, i * (16 * 2 * GT), i * 16)
            group(NG - 1, 0, 32 * (LOOPS + 1), 16 * 2 * GT * LOOPS, 16 * LOOPS)


def experts(nc, route, lists, results, w1, b1, w2, b2):
    slot_a, slot_b, _, _, fill, index_a, index_b = route
    with ExitStack() as ctx:
        a = Alloc(nc, ctx, "exp")
        count = a.sb("count", [P, NE])
        count_i = a.sb("count_i", [P, NE], I32)
        blocks_i = a.sb("blocks_i", [P, NE], I32)
        blocks_f = a.sb("blocks_f", [P, NE])
        upto = a.sb("upto", [P, NE])
        nought = a.sb("nought", [P, NE])
        shift = a.sb("shift", [P, NE])
        moved = [a.sb(f"moved{i}", [P, NT]) for i in range(2)]
        table = a.sb("table", [P, NE, 4], I32)
        zeros = a.sb("zeros", [P, XT, D])
        ident = a.sb("ident", [P, P])
        w1f = a.sb("w1f", [P, DC, H])
        w2f = a.sb("w2f", [P, HC, D])
        w1hi = [a.sb(f"w1hi{i}", [P, DC, H], F32R) for i in range(2)]
        w1lo = [a.sb(f"w1lo{i}", [P, DC, H], F32R) for i in range(2)]
        w2hi = [a.sb(f"w2hi{i}", [P, HC, D], F32R) for i in range(2)]
        w2lo = [a.sb(f"w2lo{i}", [P, HC, D], F32R) for i in range(2)]
        b1c = a.sb("b1c", [P, NE, HC])
        b2r = a.sb("b2r", [P, NE, D])
        rows = a.sb("rows", [P, XT, D])
        xhi, xlo = a.sb("xhi", [P, DC, XB], F32R), a.sb("xlo", [P, DC, XB], F32R)
        g = a.sb("g", [P, HC, XB])
        ghi, glo = a.sb("ghi", [P, HC, XB], F32R), a.sb("glo", [P, HC, XB], F32R)
        y = a.sb("y", [P, XT, D])
        pt = a.ps("pt", [P, DC, XB])
        p1 = a.ps("p1", [P, HC, XB])
        p2 = a.ps("p2", [P, XT, D])

        consts_in = a.sem("consts_in")
        zero_done = a.sem("zero_done")
        ident_done = a.sem("ident_done")
        table_done = a.sem("table_done")
        tails_out = a.sem("tails_out")
        w_in = a.sem("w_in")
        w_split = a.sem("w_split")
        rows_in = a.sem("rows_in")
        turned = a.sem("turned")
        xhi_done = a.sem("xhi_done")
        xlo_done = a.sem("xlo_done")
        l1_done = a.sem("l1_done")
        gelu_done = a.sem("gelu_done")
        ghi_done = a.sem("ghi_done")
        glo_done = a.sem("glo_done")
        l2_done = a.sem("l2_done")
        y_done = a.sem("y_done")
        y_seen = a.sem("y_seen")
        y_out = a.sem("y_out")
        prep = a.sem("prep")
        split_step = a.sem("split_step")
        block = ctx.enter_context(nc.Block())

        def entry(eng, e, column, most):
            return eng.value_load(table[0:1, bass.ds(e, 1), column:column + 1].rearrange("o s c -> o (s c)"),
                                  min_val=0, max_val=most)

        def each_block(eng, e, body):
            blocks = entry(eng, e, 0, MOST)
            with eng.If(blocks > 0):
                before = entry(eng, e, 1, ALL)
                with eng.Fori(0, blocks) as q:
                    m = nc.s_assert_within(before + q, 0, ALL - 1, skip_runtime_bounds_check_because=
                                           "ALL blocks hold two rows per node however they are routed")
                    body(m, q)

        @block.sync
        def _(sp):
            sp.dma_start(b1c[:], b1).then_inc(consts_in, 16)
            sp.dma_start(b2r[:], b2.partition_broadcast(P)).then_inc(consts_in, 16)
            sp.wait_ge(zero_done, 1)
            sp.wait_ge(table_done, 1)
            for e in range(NE):
                row = entry(sp, e, 2, NPAD)
                out = lists[bass.ds(row + e * LIST, XB), :].rearrange("(t p) d -> p t d", p=P)
                sp.dma_start(out, zeros[:]).then_inc(tails_out, 16)

            def weights(e):
                sp.dma_start(w1f[:], w1[bass.ds(e * D, D), :].rearrange("(c p) n -> p c n", p=P)).then_inc(w_in, 16)
                sp.dma_start(w2f[:], w2[bass.ds(e * H, H), :].rearrange("(c p) n -> p c n", p=P)).then_inc(w_in, 16)

            def load(m, row):
                sp.wait_ge(turned, m)
                sp.dma_start(rows[:], lists[bass.ds(row, XB), :].rearrange("(t p) d -> p t d", p=P))\
                    .then_inc(rows_in, 16)

            weights(0)
            sp.wait_ge(tails_out, 16 * NE)
            with sp.Fori(0, NE) as e:
                sp.wait_ge(w_split, e + 1)
                more = nc.s_assert_within(
                    e + 1 - (e + 1) // NE, 0, NE - 1,
                    skip_runtime_bounds_check_because="e < NE; the last load is of expert NE - 1 again")
                weights(more)
                each_block(sp, e, lambda m, q: load(m, e * LIST + q * XB))
            load(entry(sp, NE - 1, 1, ALL) + entry(sp, NE - 1, 0, MOST), 0)
            sp.wait_ge(w_in, 32 * (NE + 1))

        @block.gpsimd
        def _(pool):
            nc.gpsimd.memset(zeros[:], 0.0).then_inc(zero_done, 1)
            nc.gpsimd.memset(ident[:], 0.0).then_inc(ident_done, 1)
            pool.wait_ge(ident_done, 1)
            nc.gpsimd.affine_select(out=ident[:], in_=ident[:], compare_op=ALU.not_equal, fill=1.0, base=0,
                                    pattern=[[-1, P]], channel_multiplier=1).then_inc(ident_done, 1)
            pool.wait_ge(table_done, 1)

            def store(m, row):
                pool.wait_ge(y_done, m + 1)
                pool.sem_inc(y_seen, 1)
                pool.dma_start(results[bass.ds(row, XB), :].rearrange("(t p) d -> p t d", p=P), y[:])\
                    .then_inc(y_out, 16)

            with pool.Fori(0, NE) as e:
                each_block(pool, e, lambda m, q: store(m, m * XB))
            total = entry(pool, NE - 1, 1, ALL) + entry(pool, NE - 1, 0, MOST)
            pool.wait_ge(y_out, total * 16)

        @block.scalar
        def _(act):
            act.wait_ge(consts_in, 32)
            act.wait_ge(table_done, 1)

            def round_x(m):
                act.wait_ge(turned, m + 1)
                act.wait_ge(l1_done, m * HC)
                nc.scalar.activation(xhi[:], pt[:], ACT.Copy).then_inc(xhi_done, 1)

            def body(m, e):
                for c in range(HC):
                    act.wait_ge(l1_done, m * HC + c + 1)
                    act.wait_ge(glo_done, m * HC)
                    nc.scalar.activation(g[:, c, :], p1[:, c, :], ACT.Gelu,
                                         bias=b1c[:, bass.ds(e, 1), c:c + 1].rearrange("p o c -> p (o c)"))\
                        .then_inc(gelu_done, 1)
                    act.wait_ge(gelu_done, m * HC + c + 1)
                    act.wait_ge(l2_done, m)
                    nc.scalar.activation(ghi[:, c, :], g[:, c, :], ACT.Copy).then_inc(ghi_done, 1)
                round_x(m + 1)

            round_x(0)
            with act.Fori(0, NE) as e:
                each_block(act, e, lambda m, q: body(m, e))

        @block.vector
        def _(dve):
            n = [0]

            def chain(ins):
                n[0] += 1
                ins.then_inc(prep, 1)
                dve.wait_ge(prep, n[0])

            for e in range(NE):
                last = nc.vector.tensor_scalar(count[:, e:e + 1], fill[:, e:e + 1], float(e * LIST), None,
                                               ALU.subtract)
            chain(last)
            chain(nc.vector.tensor_copy(count_i[:], count[:]))
            chain(nc.vector.tensor_scalar(blocks_f[:], count[:], float(XB - 1), None, ALU.add))
            chain(nc.vector.tensor_copy(blocks_i[:], blocks_f[:]))
            chain(nc.vector.tensor_scalar(blocks_i[:], blocks_i[:], XB.bit_length() - 1, None,
                                          ALU.logical_shift_right))
            chain(nc.vector.tensor_copy(blocks_f[:], blocks_i[:]))
            chain(nc.vector.memset(nought[:], 0.0))
            chain(nc.vector.tensor_tensor_scan(upto[:], blocks_f[:], nought[:], 0.0, ALU.add, ALU.add))
            chain(nc.vector.tensor_tensor(upto[:], upto[:], blocks_f[:], ALU.subtract))
            nc.vector.tensor_copy(table[:, :, 0], blocks_i[:])
            nc.vector.tensor_copy(table[:, :, 2], count_i[:])
            nc.vector.tensor_copy(table[:, :, 1], upto[:]).then_inc(table_done, 1)
            dve.wait_ge(table_done, 1)
            dve.wait_ge(consts_in, 32)

            def split(e, u, loaded, step):
                dve.wait_ge(w_in, loaded)
                nc.vector.tensor_copy(w1hi[u][:], w1f[:])
                nc.vector.tensor_copy(w2hi[u][:], w2f[:]).then_inc(split_step, 1)
                dve.wait_ge(split_step, step)
                nc.vector.tensor_tensor(w1lo[u][:], w1f[:], w1hi[u][:].bitcast(F32), ALU.subtract)
                nc.vector.tensor_tensor(w2lo[u][:], w2f[:], w2hi[u][:].bitcast(F32), ALU.subtract)\
                    .then_inc(w_split, 1)

            def x_low(m):
                dve.wait_ge(xhi_done, m + 1)
                dve.wait_ge(l1_done, m * HC)
                nc.vector.tensor_tensor(xlo[:], pt[:], xhi[:].bitcast(F32), ALU.subtract).then_inc(xlo_done, 1)

            def body(m, e):
                for c in range(HC):
                    dve.wait_ge(ghi_done, m * HC + c + 1)
                    dve.wait_ge(l2_done, m)
                    nc.vector.tensor_tensor(glo[:, c, :], g[:, c, :], ghi[:, c, :].bitcast(F32), ALU.subtract)\
                        .then_inc(glo_done, 1)
                x_low(m + 1)
                dve.wait_ge(l2_done, m + 1)
                dve.wait_ge(y_out, m * 16)
                nc.vector.tensor_tensor(y[:], p2[:], b2r[:, bass.ds(e, 1), :].broadcast_to([P, XT, D]),
                                        ALU.add).then_inc(y_done, 1)

            chain(nc.vector.tensor_scalar(shift[:], upto[:], float(XB), None, ALU.mult))
            for e in range(NE - 1, 0, -1):
                chain(nc.vector.tensor_tensor(shift[:, e:e + 1], shift[:, e:e + 1], shift[:, e - 1:e],
                                              ALU.subtract))
            chain(nc.vector.tensor_scalar(shift[:, 1:NE], shift[:, 1:NE], float(LIST), None, ALU.subtract))
            for slot, index in ((slot_a, index_a), (slot_b, index_b)):
                chain(nc.vector.tensor_copy(moved[0][:], slot[:]))
                for e in range(1, NE):
                    chain(nc.vector.tensor_scalar(moved[1][:], slot[:], float(e * LIST), shift[:, e:e + 1],
                                                  ALU.is_ge, ALU.mult))
                    chain(nc.vector.tensor_tensor(moved[0][:], moved[0][:], moved[1][:], ALU.add))
                chain(nc.vector.tensor_copy(index[:], moved[0][:]))
            split(0, 0, 32, 1)
            x_low(0)
            with dve.Fori(0, NE // 2) as i:
                for u in range(2):
                    e = i * 2 + u
                    dve.wait_ge(l2_done, entry(dve, e, 1, ALL))
                    split(e + 1, (u + 1) % 2, e * 32 + 64, e + 2)
                    each_block(dve, e, lambda m, q: body(m, e))

        @block.tensor
        def _(pe):
            mm = nc.tensor.matmul
            pe.wait_ge(ident_done, 2)
            pe.wait_ge(table_done, 1)

            def turn(m):
                pe.wait_ge(rows_in, m * 16 + 16)
                pe.wait_ge(xlo_done, m)
                for c in range(DC):
                    for t in range(XT):
                        last = nc.tensor.transpose(pt[:, c, t * P:(t + 1) * P], rows[:, t, c * P:(c + 1) * P],
                                                   ident[:])
                last.then_inc(turned, 1)

            def body(m, u):
                pe.wait_ge(xlo_done, m + 1)
                pe.wait_ge(gelu_done, m * HC)
                for j in range(HC):
                    for c in range(DC):
                        hi, lo = (w[u][:, c, j * P:(j + 1) * P] for w in (w1hi, w1lo))
                        mm(p1[:, j, :], hi, xhi[:, c, :], start=c == 0, stop=False)
                        mm(p1[:, j, :], hi, xlo[:, c, :], start=False, stop=False)
                        last = mm(p1[:, j, :], lo, xhi[:, c, :], start=False, stop=c == DC - 1)
                    last.then_inc(l1_done, 1)
                turn(m + 1)
                pe.wait_ge(glo_done, m * HC + HC)
                pe.wait_ge(y_done, m)
                for t in range(XT):
                    for j in range(HC):
                        hi, lo = (x[:, j, t * P:(t + 1) * P] for x in (ghi, glo))
                        mm(p2[:, t, :], hi, w2hi[u][:, j, :], start=j == 0, stop=False)
                        mm(p2[:, t, :], hi, w2lo[u][:, j, :], start=False, stop=False)
                        last = mm(p2[:, t, :], lo, w2hi[u][:, j, :], start=False, stop=j == HC - 1)
                last.then_inc(l2_done, 1)

            turn(0)
            with pe.Fori(0, NE // 2) as i:
                for u in range(2):
                    e = i * 2 + u
                    pe.wait_ge(w_split, e + 1)
                    each_block(pe, e, lambda m, q: body(m, u))


def combine(nc, route, x1_rows, results, out):
    _, _, weight_a, weight_b, _, index_a, index_b = route
    with ExitStack() as ctx:
        a = Alloc(nc, ctx, "comb")
        x1 = [a.sb(f"x1_{i}", [P, GT, D]) for i in range(2)]
        ya = [a.sb(f"ya{i}", [P, GT, D]) for i in range(2)]
        yb = [a.sb(f"yb{i}", [P, GT, D]) for i in range(2)]
        x1_in = [a.sem(f"x1_in{i}") for i in range(2)]
        y_in = [a.sem(f"y_in{i}") for i in range(2)]
        half_done = a.sem("half_done")
        sum_done = a.sem("sum_done")
        sent = [a.sem(f"sent{i}") for i in range(2)]
        block = ctx.enter_context(nc.Block())
        x_v = x1_rows.rearrange("(g t p) d -> g p t d", p=P, t=GT)
        o_v = out.rearrange("(g t p) d -> g p t d", p=P, t=GT)

        @block.sync
        def _(sp):
            for g in range(NG):
                if g >= 2:
                    sp.wait_ge(sent[g % 2], 16 * (g // 2))
                sp.dma_start(x1[g % 2][:], x_v[g]).then_inc(x1_in[g % 2], 16)

        @block.gpsimd
        def _(pool):
            for g in range(NG):
                if g >= 2:
                    pool.wait_ge(sum_done, g - 1)
                for t in range(GT):
                    for slot, y in ((index_a, ya), (index_b, yb)):
                        nc.gpsimd.indirect_dma_start(
                            out=y[g % 2][:, t, :], out_offset=None, in_=results,
                            in_offset=bass.IndirectOffsetOnAxis(ap=slot[:, g * GT + t:g * GT + t + 1], axis=0),
                        ).then_inc(y_in[g % 2], 16)

        @block.vector
        def _(dve):
            for g in range(NG):
                dve.wait_ge(x1_in[g % 2], 16 * (g // 2 + 1))
                dve.wait_ge(y_in[g % 2], 16 * 2 * GT * (g // 2 + 1))
                for step, (weight, y) in enumerate(((weight_a, ya), (weight_b, yb))):
                    for t in range(GT):
                        tile = g * GT + t
                        last = nc.vector.scalar_tensor_tensor(
                            out=x1[g % 2][:, t, :], in0=y[g % 2][:, t, :], scalar=weight[:, tile:tile + 1],
                            in1=x1[g % 2][:, t, :], op0=ALU.mult, op1=ALU.add)
                    if step == 0:
                        last.then_inc(half_done, 1)
                        dve.wait_ge(half_done, g + 1)
                last.then_inc(sum_done, 1)

        @block.scalar
        def _(act):
            for g in range(NG):
                act.wait_ge(sum_done, g + 1)
                act.dma_start(o_v[g], x1[g % 2][:]).then_inc(sent[g % 2], 16)
            act.wait_ge(sent[0], 16 * ((NG + 1) // 2))
            act.wait_ge(sent[1], 16 * (NG // 2))


def build(nc, x, src_cols, dst_cols, dst_rows, rbf, w1, b1, w2, b2, u1, c1, u2, c2,
          gate_w, gate_b, ew1, eb1, ew2, eb2, out):
    half_h = nc.dram_tensor("half_h", (NPAD, D), F32, kind="Internal").ap()
    seg_scratch = nc.dram_tensor("seg_scratch", (NS, 2), I32, kind="Internal").ap()
    seg_table = nc.dram_tensor("seg_table", (1, NS, 4), I32, kind="Internal").ap()
    x1_rows = nc.dram_tensor("x1_rows", (NPAD, D), F32, kind="Internal").ap()
    lists = nc.dram_tensor("lists", (NE * LIST, D), F32, kind="Internal").ap()
    results = nc.dram_tensor("results", (RES, D), F32, kind="Internal").ap()
    with ExitStack() as ctx:
        a = Alloc(nc, ctx, "all")
        route = (a.sb("slot_a", [P, NT]), a.sb("slot_b", [P, NT]),
                 a.sb("weight_a", [P, NT]), a.sb("weight_b", [P, NT]), a.sb("fill", [P, NE]),
                 a.sb("index_a", [P, NT], I32), a.sb("index_b", [P, NT], I32))
        with ExitStack() as inner:
            aggr = inner.enter_context(nc.sbuf_tensor("aggr", [P, DC, AW], F32))
            normalise(nc, x, half_h, dst_rows, seg_scratch, seg_table)
            edges(nc, aggr, rbf, src_cols, dst_cols, half_h, seg_table, w1, b1, w2, b2)
            nodes(nc, aggr, route, x, half_h, x1_rows, lists, results, u1, c1, u2, c2, gate_w, gate_b)
        experts(nc, route, lists, results, ew1, eb1, ew2, eb2)
        combine(nc, route, x1_rows, results, out)


def kernel(**inputs):
    import concourse.bacc as bacc
    from concourse.bass_utils import run_bass_kernel_spmd

    v = {name: np.asarray(a) for name, a in inputs.items()}

    def padded(a, rows, value=0):
        return np.concatenate([a, np.full((rows - a.shape[0], *a.shape[1:]), value, a.dtype)])

    src = padded(v["src"], EPAD)
    dst = padded(v["dst"], EPAD, NPAD - 1)
    arrays = {
        "x": padded(v["x"], NPAD),
        "src_cols": src.reshape(NS * ST, P).T,
        "dst_cols": dst.reshape(NS * ST, P).T,
        "dst_rows": dst.reshape(2, HALF_S, SUP).transpose(1, 0, 2),
        "rbf": padded(v["edge_attr_64"], EPAD).T,
        "w1": v["L0_gnn_W1"],
        "b1": v["L0_gnn_b1"].reshape(DC, P).T,
        "w2": v["L0_gnn_W2"],
        "b2": v["L0_gnn_b2"].reshape(1, D),
        "u1": v["L0_gnn_U1"],
        "c1": v["L0_gnn_c1"].reshape(DC, P).T,
        "u2": v["L0_gnn_U2"],
        "c2": v["L0_gnn_c2"],
        "gate_w": v["L0_ffn_gate_w"],
        "gate_b": v["L0_ffn_gate_b"],
        "ew1": v["L0_ffn_W1"].reshape(NE * D, H),
        "eb1": v["L0_ffn_b1"].reshape(NE, HC, P).transpose(2, 0, 1),
        "ew2": v["L0_ffn_W2"].reshape(NE * H, D),
        "eb2": v["L0_ffn_b2"],
    }
    nc = bacc.Bacc("TRN2", target_bir_lowering=False, num_devices=1)
    feeds, args = {}, []
    for name, a in arrays.items():
        feeds[f"in_{name}"] = np.ascontiguousarray(a)
        args.append(nc.dram_tensor(f"in_{name}", a.shape, mybir.dt.from_np(a.dtype), kind="ExternalInput").ap())
    out = nc.dram_tensor("out", (NPAD, D), F32, kind="ExternalOutput").ap()
    build(nc, *args, out)
    result = run_bass_kernel_spmd(nc, [feeds], core_ids=[0])
    return result.results[0]["out"][:N_NODES]
```

```python
import concourse.bass as bass
import numpy as np
from concourse import mybir
from contextlib import ExitStack

F32 = mybir.dt.float32
F32R = mybir.dt.float32r
F16 = mybir.dt.float16
I32 = mybir.dt.int32
ALU = mybir.AluOpType
ACT = mybir.ActivationFunctionType
AX = mybir.AxisListType

P = 128
N_NODES = 6250
N_EDGES = 100000
D = 256
DC = D // P
NRBF = 64
NT = -(-N_NODES // P)
NPAD = NT * P
SUP = 512
ST = SUP // P
NS = -(-N_EDGES // SUP)
EPAD = NS * SUP
HALF_S = NS // 2
WIN = 64
PACK = 1 << 13
AW = NPAD + WIN
GT = 7
NG = NT // GT
GN = GT * P
GH = GN // 2
NE = 8
H = 512
HC = H // P
XB = 512
XT = XB // P
LIST = NPAD + XB
MOST = -(-NPAD // XB)
ALL = 2 * NPAD // XB + NE
CLEAR = -(-ALL * XB // (NG * P))
RES = CLEAR * NG * P
EPS = 1e-5
H_SCALE = 512.0
MSG_SCALE = 2 * H_SCALE


class Alloc:

    def __init__(self, nc, ctx, stage):
        self.nc, self.ctx, self.stage = nc, ctx, stage

    def sb(self, name, shape, dt=F32):
        return self.ctx.enter_context(self.nc.sbuf_tensor(f"{self.stage}_{name}", shape, dt))

    def ps(self, name, shape):
        return self.ctx.enter_context(self.nc.psum_tensor(f"{self.stage}_{name}", shape, F32))

    def sem(self, name):
        return self.ctx.enter_context(self.nc.semaphore(f"{self.stage}_{name}"))


def inverse_root(dve, chain, r, root, v):
    chain(dve.reciprocal(r, root))
    chain(dve.tensor_tensor(root, r, r, ALU.mult))
    chain(dve.tensor_tensor(root, root, v, ALU.mult))
    chain(dve.tensor_scalar(root, root, -0.5, 1.5, ALU.mult, ALU.add))
    chain(dve.tensor_tensor(r, r, root, ALU.mult))


def normalise(nc, x, scaled_h, dst_rows, seg_scratch, seg_table):
    with ExitStack() as ctx:
        a = Alloc(nc, ctx, "norm")
        xin = [a.sb(f"x{i}", [P, GT, D]) for i in range(2)]
        hout = [a.sb(f"h{i}", [P, GT, D]) for i in range(2)]
        stats = a.sb("stats", [P, GT, nc.vector.BN_STATS_DIM])
        mv = a.sb("mean_var", [P, GT, nc.vector.BN_AGGR_DIM])
        rstd = a.sb("rstd", [P, GT])
        var = a.sb("var", [P, GT])
        std = a.sb("std", [P, GT])
        rows = a.sb("dst_rows", [HALF_S, 2, SUP], I32)
        rows_f = a.sb("dst_rows_f", [HALF_S, 2, SUP])
        span = a.sb("span", [HALF_S, 2, 2])
        span_i = a.sb("span_i", [HALF_S, 2, 2], I32)
        flat = a.sb("flat", [1, NS, 2], I32)
        flat_f = a.sb("flat_f", [1, NS])
        zeros = a.sb("zeros", [1, NS])
        upto = a.sb("upto", [1, NS])
        table = a.sb("table", [1, NS, 4], I32)
        x_in = [a.sem(f"x_in{i}") for i in range(2)]
        h_out = [a.sem(f"h_out{i}") for i in range(2)]
        h_ready = a.sem("h_ready")
        rows_in = a.sem("rows_in")
        span_ready = a.sem("span_ready")
        span_out = a.sem("span_out")
        flat_in = a.sem("flat_in")
        table_ready = a.sem("table_ready")
        table_out = a.sem("table_out")
        step = a.sem("vector_step")
        var_ready = a.sem("var_ready")
        std_ready = a.sem("std_ready")
        x_v = x.rearrange("(g t p) d -> g p t d", p=P, t=GT)
        h_v = scaled_h.rearrange("(g t p) d -> g p t d", p=P, t=GT)
        block = ctx.enter_context(nc.Block())

        @block.sync
        def _(sp):
            sp.dma_start(rows[:], dst_rows).then_inc(rows_in, 16)
            for g in range(NG):
                if g >= 2:
                    sp.wait_ge(h_ready, g - 1)
                sp.dma_start(xin[g % 2][:], x_v[g]).then_inc(x_in[g % 2], 16)

        @block.scalar
        def _(act):
            act.wait_ge(span_ready, 1)
            act.dma_start(seg_scratch.rearrange("(a p) c -> p a c", a=2), span_i[:]).then_inc(span_out, 16)
            act.wait_ge(span_out, 16)
            act.dma_start(flat[:], seg_scratch.rearrange("(o s) c -> o s c", o=1)).then_inc(flat_in, 16)
            for g in range(NG):
                act.wait_ge(var_ready, g + 1)
                nc.scalar.activation(std[:], var[:], ACT.Sqrt).then_inc(std_ready, 1)
                act.wait_ge(h_ready, g + 1)
                act.dma_start(h_v[g], hout[g % 2][:]).then_inc(h_out[g % 2], 16)
                if g == 1:
                    act.wait_ge(table_ready, 1)
                    act.dma_start(seg_table, table[:]).then_inc(table_out, 16)
            act.wait_ge(table_out, 16)
            act.wait_ge(h_out[0], 16 * ((NG + 1) // 2))
            act.wait_ge(h_out[1], 16 * (NG // 2))

        @block.vector
        def _(dve):
            n = [0]

            def link(ins):
                n[0] += 1
                ins.then_inc(step, 1)
                dve.wait_ge(step, n[0])

            def spans():
                dve.wait_ge(rows_in, 16)
                link(nc.vector.tensor_copy(rows_f[:], rows[:]))
                nc.vector.tensor_reduce(span[:, :, 0:1], rows_f[:], AX.X, ALU.min)
                link(nc.vector.tensor_reduce(span[:, :, 1:2], rows_f[:], AX.X, ALU.max))
                link(nc.vector.tensor_tensor(span[:, :, 1:2], span[:, :, 1:2], span[:, :, 0:1], ALU.subtract))
                link(nc.vector.tensor_copy(span_i[:], span[:]))
                nc.vector.tensor_scalar(span_i[:, :, 1:2], span_i[:, :, 1:2], WIN.bit_length() - 1, None,
                                        ALU.logical_shift_right).then_inc(span_ready, 1)

            def window_table():
                link(nc.vector.memset(zeros[:], 0.0))
                link(nc.vector.memset(table[:], 0))
                dve.wait_ge(flat_in, 16)
                link(nc.vector.tensor_copy(flat_f[:], flat[:, :, 1]))
                link(nc.vector.tensor_tensor_scan(upto[:], flat_f[:], zeros[:], 0.0, ALU.add, ALU.add))
                link(nc.vector.tensor_tensor(upto[:], upto[:], flat_f[:], ALU.subtract))
                link(nc.vector.tensor_scalar(flat_f[:], flat_f[:], float(PACK), None, ALU.mult))
                link(nc.vector.tensor_tensor(flat_f[:], flat_f[:], flat[:, :, 0], ALU.add))
                nc.vector.tensor_copy(table[:, :, 0], flat_f[:])
                nc.vector.tensor_copy(table[:, :, 1], flat[:, :, 0])
                nc.vector.tensor_copy(table[:, :, 2], upto[:]).then_inc(table_ready, 1)

            spans()
            for g in range(NG):
                dve.wait_ge(x_in[g % 2], 16 * (g // 2 + 1))
                if g >= 2:
                    dve.wait_ge(h_out[g % 2], 16 * (g // 2))
                for t in range(GT):
                    last = nc.vector.bn_stats(stats[:, t, :], xin[g % 2][:, t, :])
                link(last)
                for t in range(GT):
                    last = nc.vector.bn_aggr(mv[:, t, :], stats[:, t, :])
                link(last)
                nc.vector.tensor_scalar(var[:], mv[:, :, 1], EPS, H_SCALE ** -2, ALU.add, ALU.mult).then_inc(var_ready, 1)
                dve.wait_ge(std_ready, g + 1)
                inverse_root(nc.vector, link, rstd[:], std[:], var[:])
                for t in range(GT):
                    last = nc.vector.tensor_scalar(hout[g % 2][:, t, :], xin[g % 2][:, t, :], mv[:, t, 0:1],
                                                   rstd[:, t:t + 1], ALU.subtract, ALU.mult)
                last.then_inc(h_ready, 1)
                if g == 0:
                    window_table()


def split_weight(dve, chain, hi, lo, w):
    chain(dve.tensor_copy(hi, w))
    chain(dve.tensor_tensor(lo, w, hi.bitcast(F32), ALU.subtract))


def entry(eng, table, row, column):
    most = (PACK * (NPAD // WIN + 1), NPAD - 1, NS * (NPAD // WIN))[column]
    return eng.value_load(table[0:1, bass.ds(row, 1), column:column + 1].rearrange("o s c -> o (s c)"),
                          min_val=0, max_val=most)


def edges(nc, aggr, rbf, src_cols, dst_cols, scaled_h, seg_table, w1, b1, w2, b2):
    with ExitStack() as ctx:
        a = Alloc(nc, ctx, "edge")
        w1f = a.sb("w1f", [P, D])
        w1hi, w1lo = a.sb("w1hi", [P, D], F32R), a.sb("w1lo", [P, D], F32R)
        w2f = a.sb("w2f", [P, DC, D])
        w2hi, w2lo = a.sb("w2hi", [P, DC, D], F32R), a.sb("w2lo", [P, DC, D], F32R)
        b1c = a.sb("b1c", [P, DC])
        b2f = a.sb("b2f", [64, D])
        b2hi, b2parts = a.sb("b2hi", [64, D], F32R), a.sb("b2parts", [64, D], F32R)
        onef = a.sb("onef", [64, P])
        one = a.sb("one", [64, P], F32R)
        src = a.sb("src", [P, NS * ST], I32)
        dst = a.sb("dst", [P, NS * ST], I32)
        dstf = a.sb("dstf", [P, NS * ST])
        starts = a.sb("starts", [P, NS, 4], I32)
        node = a.sb("node", [P, AW])
        table = a.sb("table", [1, NS, 4], I32)
        xr = [a.sb(f"x{i}", [P, 2 * SUP]) for i in range(2)]
        xs = [a.sb(f"xs{i}", [P, SUP], F32R) for i in range(2)]
        hid = [a.sb(f"hid{i}", [P, DC, SUP]) for i in range(2)]
        hhi = [a.sb(f"hhi{i}", [P, DC, SUP], F32R) for i in range(2)]
        hlo = [a.sb(f"hlo{i}", [P, DC, SUP], F32R) for i in range(2)]
        msg = [a.sb(f"msg{i}", [P, ST * D]) for i in range(2)]
        mhi = [a.sb(f"mhi{i}", [P, ST * D], F16) for i in range(4)]
        mlo = [a.sb(f"mlo{i}", [P, ST * D], F16) for i in range(4)]
        ghs = [a.sb(f"ghs{i}", [P, ST, D]) for i in range(4)]
        idx = [a.sb(f"idx{i}", [P, ST], I32) for i in range(4)]
        oh = [a.sb(f"onehot{i}", [P, ST, WIN], F16) for i in range(2)]
        ohx = a.sb("onehot_extra", [P, ST, WIN], F16)
        p1 = a.ps("p1", [P, DC, SUP])
        p2 = [a.ps(f"p2_{i}", [P, ST, D]) for i in range(2)]
        pg = [a.ps(f"pg{i}", [P, DC, 256]) for i in range(2)]

        consts_in = a.sem("consts_in")
        src_in = a.sem("src_in")
        x_in = [a.sem(f"x_in{i}") for i in range(2)]
        nodes_made = a.sem("nodes_made")
        weights_split = a.sem("weights_split")
        x_split = a.sem("x_split")
        l1_done = a.sem("l1_done")
        silu_done = a.sem("silu_done")
        hi_done = a.sem("hi_done")
        lo_done = a.sem("lo_done")
        l2_done = a.sem("l2_done")
        tanh_done = a.sem("tanh_done")
        rows_in = [a.sem(f"rows_in{i}") for i in range(4)]
        idx_copied = a.sem("idx_copied")
        idx_seen = a.sem("idx_seen")
        msg_done = a.sem("msg_done")
        mhi_done = a.sem("mhi_done")
        mlo_done = a.sem("mlo_done")
        onehot_done = a.sem("onehot_done")
        sum_done = a.sem("sum_done")
        sum_added = a.sem("sum_added")
        extra_onehot = a.sem("extra_onehot")
        extra_sum = a.sem("extra_sum")
        extra_added = a.sem("extra_added")
        xhi_done = a.sem("xhi_done")
        prep = a.sem("prep")
        block = ctx.enter_context(nc.Block())
        NCONST = 9

        @block.sync
        def _(sp):
            sp.dma_start(src[:], src_cols).then_inc(src_in, 16)
            sp.dma_start(w1f[0:NRBF, :], w1).then_inc(consts_in, 16)
            sp.dma_start(w1f[NRBF:P, :], w1).then_inc(consts_in, 16)
            sp.dma_start(w2f[:], w2.rearrange("(c p) n -> p c n", p=P)).then_inc(consts_in, 16)
            sp.dma_start(b1c[:], b1).then_inc(consts_in, 16)
            sp.dma_start(b2f[0:1, :], b2).then_inc(consts_in, 16)
            sp.dma_start(b2f[32:33, :], b2).then_inc(consts_in, 16)
            sp.dma_start(dst[:], dst_cols).then_inc(consts_in, 16)
            sp.dma_start(table[:], seg_table).then_inc(consts_in, 16)
            sp.dma_start(starts[:], seg_table[0].partition_broadcast(P)).then_inc(consts_in, 16)

            def load(q, u, first):
                if not first:
                    sp.wait_ge(x_split, 2 * q - 2)
                cols = bass.ds(q * (2 * SUP), 2 * SUP)
                sp.dma_start(xr[u][0:NRBF, :], rbf[:, cols]).then_inc(x_in[u], 16)
                sp.dma_start(xr[u][NRBF:P, :], rbf[:, cols]).then_inc(x_in[u], 16)

            load(0, 0, True)
            load(1, 1, True)
            with sp.Fori(1, NS // 4) as i:
                for u in range(2):
                    load(i * 2 + u, u, False)

        @block.gpsimd
        def _(pool):
            nc.gpsimd.iota(node[:], pattern=[[1, AW]], base=0, channel_multiplier=0,
                           allow_small_or_imprecise_dtypes=True).then_inc(nodes_made, 1)
            nc.gpsimd.memset(aggr[:], 0.0).then_inc(nodes_made, 1)
            nc.gpsimd.memset(b2parts[:].bitcast(F32), 0.0).then_inc(nodes_made, 1)
            pool.wait_ge(src_in, 16)

            def gather(k, u, first):
                if not first:
                    pool.wait_ge(msg_done, k - 3)
                nc.gpsimd.tensor_copy(idx[u][:], src[:, bass.ds(k * ST, ST)]).then_inc(idx_copied, 1)
                pool.wait_ge(idx_copied, k + 1)
                pool.sem_inc(idx_seen, 1)
                for t in range(ST):
                    nc.gpsimd.indirect_dma_start(
                        out=ghs[u][:, t, :], out_offset=None, in_=scaled_h,
                        in_offset=bass.IndirectOffsetOnAxis(ap=idx[u][:, t:t + 1], axis=0),
                    ).then_inc(rows_in[u], 16)

            for k in range(4):
                gather(k, k, True)
            with pool.Fori(1, NS // 4) as i:
                for u in range(4):
                    gather(i * 4 + u, u, False)

        @block.scalar
        def _(act):
            act.wait_ge(consts_in, 16 * NCONST)

            def silu(k, u, first):
                act.wait_ge(l1_done, k + 1)
                if not first:
                    act.wait_ge(lo_done, k - 1)
                for c in range(DC):
                    last = nc.scalar.activation(hid[u][:, c, :], p1[:, c, :], ACT.Silu, bias=b1c[:, c:c + 1])
                last.then_inc(silu_done, 1)

            def round_hi(k, u, first):
                act.wait_ge(silu_done, k + 1)
                if not first:
                    act.wait_ge(l2_done, k - 1)
                nc.scalar.activation(hhi[u][:], hid[u][:], ACT.Copy).then_inc(hi_done, 1)

            def tanh(k, u, first):
                act.wait_ge(l2_done, k + 1)
                if not first:
                    act.wait_ge(mlo_done, k - 1)
                nc.scalar.activation(msg[u][:], p2[u][:], ACT.Tanh, scale=0.5).then_inc(tanh_done, 1)

            def round_msg(k, u, first):
                act.wait_ge(msg_done, k + 1)
                if not first:
                    act.wait_ge(sum_added, k - 2)
                nc.scalar.activation(mhi[u][:], msg[u % 2][:], ACT.Copy).then_inc(mhi_done, 1)

            def round_x(k, u, first, loaded):
                act.wait_ge(x_in[(u // 2) % 2], loaded)
                if not first:
                    act.wait_ge(l1_done, k - 1)
                part = xr[(u // 2) % 2][:, (u % 2) * SUP:(u % 2 + 1) * SUP]
                nc.scalar.activation(xs[u % 2][:], part, ACT.Copy).then_inc(xhi_done, 1)

            def step(k, u, start, loaded):
                if loaded is not None:
                    round_x(k + 1, (u + 1) % 4, start < 1, loaded)
                silu(k, u % 2, start < 2)
                round_hi(k, u % 2, start < 2)
                if start >= 2:
                    round_msg(k - 2, (u - 2) % 4, start < 6)
                if start >= 1:
                    tanh(k - 1, (u - 1) % 2, start < 3)

            round_x(0, 0, True, 32)
            for k in range(8):
                step(k, k % 4, k, 32 * ((k + 1) // 4 + 1))
            with act.Fori(2, NS // 4 - 1) as i:
                for u in range(4):
                    step(i * 4 + u, u, 8, i * 32 + (64 if u == 3 else 32))
            for k in range(NS - 4, NS):
                step(k, k % 4, 8, 32 * ((k + 1) // 4 + 1) if k + 1 < NS else None)
            round_msg(NS - 2, (NS - 2) % 4, False)
            tanh(NS - 1, (NS - 1) % 2, False)
            round_msg(NS - 1, (NS - 1) % 4, False)

        @block.vector
        def _(dve):
            n = [0]

            def chain(ins):
                n[0] += 1
                ins.then_inc(prep, 1)
                dve.wait_ge(prep, n[0])

            dve.wait_ge(consts_in, 16 * NCONST)
            split_weight(nc.vector, chain, w1hi[:], w1lo[:], w1f[:])
            split_weight(nc.vector, chain, w2hi[:], w2lo[:], w2f[:])
            dve.wait_ge(nodes_made, 3)
            for row in (0, 32):
                chain(nc.vector.tensor_copy(b2hi[row:row + 1, :], b2f[row:row + 1, :]))
            chain(nc.vector.tensor_copy(b2parts[0:1, :], b2f[0:1, :]))
            chain(nc.vector.tensor_tensor(b2parts[32:33, :], b2f[32:33, :], b2hi[32:33, :].bitcast(F32),
                                          ALU.subtract))
            chain(nc.vector.memset(onef[:], 1.0))
            chain(nc.vector.tensor_copy(one[:], onef[:]))
            nc.vector.tensor_tensor(dstf[:].rearrange("p (s t) -> p s t", t=ST),
                                    dst[:].rearrange("p (s t) -> p s t", t=ST),
                                    starts[:, :, 1:2].broadcast_to([P, NS, ST]), ALU.subtract)\
                .then_inc(weights_split, 1)
            dve.wait_ge(weights_split, 1)
            
            def split_x(k, u):
                dve.wait_ge(xhi_done, k + 1)
                part = xr[(u // 2) % 2][:, (u % 2) * SUP:(u % 2 + 1) * SUP]
                nc.vector.tensor_tensor(xs[u % 2][NRBF:P, :], part[NRBF:P, :], xs[u % 2][NRBF:P, :].bitcast(F32),
                                        ALU.subtract).then_inc(x_split, 1)

            def lo(k, u, first):
                dve.wait_ge(hi_done, k + 1)
                if not first:
                    dve.wait_ge(l2_done, k - 1)
                nc.vector.tensor_tensor(hlo[u % 2][:], hid[u % 2][:], hhi[u % 2][:].bitcast(F32),
                                        ALU.subtract).then_inc(lo_done, 1)

            def message(k, u, filled):
                dve.wait_ge(tanh_done, k + 1)
                dve.wait_ge(rows_in[u], filled)
                nc.vector.scalar_tensor_tensor(out=msg[u % 2][:], in0=msg[u % 2][:], scalar=1.0,
                                               in1=ghs[u][:].rearrange("p t d -> p (t d)"),
                                               op0=ALU.add, op1=ALU.mult).then_inc(msg_done, 1)

            def low_msg(k, u, first):
                dve.wait_ge(mhi_done, k + 1)
                if not first:
                    dve.wait_ge(sum_added, k - 3)
                nc.vector.tensor_tensor(mlo[u][:], msg[u % 2][:], mhi[u][:], ALU.subtract).then_inc(mlo_done, 1)

            def compare(out, k, offset):
                return nc.vector.tensor_tensor(
                    out, node[:, bass.ds(offset, WIN)].unsqueeze(1).broadcast_to([P, ST, WIN]),
                    dstf[:, bass.ds(k * ST, ST)].unsqueeze(2).broadcast_to([P, ST, WIN]), ALU.is_equal)

            def onehot(k, u, first):
                if not first:
                    dve.wait_ge(sum_done, k - 1)
                compare(oh[u % 2][:], k, 0).then_inc(onehot_done, 1)

            def add(k, u, first, word):
                w0 = nc.s_assert_within(word - word // PACK * PACK, 0, NPAD - 1,
                                        skip_runtime_bounds_check_because="it is a node")
                dve.wait_ge(sum_done, k + 1)
                if not first:
                    dve.wait_ge(sum_added, k)
                part = aggr[:, :, bass.ds(w0, WIN)]
                nc.vector.tensor_tensor(part, part, pg[u % 2][:, :, 0:WIN], ALU.add).then_inc(sum_added, 1)
                extra(k, u, word)

            def extra(k, u, word):
                with dve.If(word >= PACK):
                    w0 = entry(dve, table, k, 1)
                    before = entry(dve, table, k, 2)
                    with dve.Fori(0, word // PACK) as j:
                        dve.wait_ge(sum_added, k + 1)
                        offset = nc.s_assert_within(
                            j * WIN + WIN, 0, NPAD - 1,
                            skip_runtime_bounds_check_because="it is at most the span of the nodes")
                        start = nc.s_assert_within(
                            w0 + j * WIN + WIN, 0, NPAD - 1,
                            skip_runtime_bounds_check_because="it is at most the superblock's last node")
                        compare(ohx[:], k, offset).then_inc(extra_onehot, 1)
                        dve.wait_ge(extra_sum, before + j + 1)
                        part = aggr[:, :, bass.ds(start, WIN)]
                        nc.vector.tensor_tensor(part, part, pg[u % 2][:, :, 0:WIN], ALU.add)\
                            .then_inc(extra_added, 1)
                        dve.wait_ge(extra_added, before + j + 1)

            def step(k, u, start, filled, ahead=True):
                if ahead:
                    split_x(k + 1, (u + 1) % 4)
                if start >= 2:
                    onehot(k - 2, (u - 2) % 4, start < 4)
                lo(k, u, start < 2)
                if start >= 2:
                    low_msg(k - 2, (u - 2) % 4, start < 6)
                if start >= 4:
                    word = entry(dve, table, k - 4, 0)
                if start >= 1:
                    message(k - 1, (u - 1) % 4, filled)
                if start >= 4:
                    add(k - 4, u, start < 5, word)

            def fills(s):
                return 16 * ST * (s // 4 + 1)

            split_x(0, 0)
            for k in range(8):
                step(k, k % 4, k, fills(k - 1))
            with dve.Fori(2, NS // 4 - 1) as i:
                for u in range(4):
                    step(i * 4 + u, u, 8, i * (16 * ST) + (0 if u == 0 else 16 * ST))
            for k in range(NS - 4, NS):
                step(k, k % 4, 8, fills(k - 1), k + 1 < NS)
            low_msg(NS - 2, (NS - 2) % 4, False)
            onehot(NS - 2, (NS - 2) % 4, False)
            message(NS - 1, (NS - 1) % 4, fills(NS - 1))
            add(NS - 4, (NS - 4) % 4, False, entry(dve, table, NS - 4, 0))
            add(NS - 3, (NS - 3) % 4, False, entry(dve, table, NS - 3, 0))
            low_msg(NS - 1, (NS - 1) % 4, False)
            onehot(NS - 1, (NS - 1) % 4, False)
            add(NS - 2, (NS - 2) % 4, False, entry(dve, table, NS - 2, 0))
            add(NS - 1, (NS - 1) % 4, False, entry(dve, table, NS - 1, 0))

        @block.tensor
        def _(pe):
            pe.wait_ge(weights_split, 1)
            pe.wait_ge(consts_in, 16 * NCONST)
            mm = nc.tensor.matmul

            def layer1(k, u, first):
                pe.wait_ge(x_split, k + 1)
                if not first:
                    pe.wait_ge(silu_done, k)
                for c in range(DC):
                    cols = slice(c * P, (c + 1) * P)
                    mm(p1[:, c, :], w1hi[:, cols], xs[u % 2][:], start=True, stop=False)
                    last = mm(p1[:, c, :], w1lo[:, cols], xs[u % 2][:], start=False, stop=True)
                last.then_inc(l1_done, 1)

            def layer2(k, u, first):
                pe.wait_ge(lo_done, k + 1)
                if not first:
                    pe.wait_ge(tanh_done, k - 1)
                for t in range(ST):
                    out = p2[u % 2][:, t, :]
                    mm(out, one[:], b2parts[:], start=True, stop=False)
                    for c in range(DC):
                        hi = hhi[u % 2][:, c, t * P:(t + 1) * P]
                        lo = hlo[u % 2][:, c, t * P:(t + 1) * P]
                        mm(out, hi, w2hi[:, c, :], start=False, stop=False)
                        mm(out, hi, w2lo[:, c, :], start=False, stop=False)
                        last = mm(out, lo, w2hi[:, c, :], start=False, stop=c == DC - 1)
                last.then_inc(l2_done, 1)

            def segment(k, u, one_hot):
                for c in range(DC):
                    for t in range(ST):
                        part = slice(t * D + c * P, t * D + (c + 1) * P)
                        mm(pg[u % 2][:, c, 0:WIN], mhi[u % 4][:, part], one_hot[:, t, :], start=t == 0, stop=False)
                        last = mm(pg[u % 2][:, c, 0:WIN], mlo[u % 4][:, part], one_hot[:, t, :],
                                  start=False, stop=t == ST - 1)
                return last

            def window(k, u, first):
                pe.wait_ge(mlo_done, k + 1)
                pe.wait_ge(onehot_done, k + 1)
                if not first:
                    pe.wait_ge(sum_added, k - 1)
                segment(k, u, oh[u % 2]).then_inc(sum_done, 1)

            def extra(k, u, word):
                with pe.If(word >= PACK):
                    before = entry(pe, table, k, 2)
                    with pe.Fori(0, word // PACK) as j:
                        pe.wait_ge(extra_onehot, before + j + 1)
                        segment(k, u, ohx).then_inc(extra_sum, 1)
                    pe.wait_ge(extra_added, before + word // PACK)

            def step(k, u, start):
                layer1(k, u, start < 1)
                if start >= 1:
                    layer2(k - 1, (u - 1) % 4, start < 3)
                if start >= 4:
                    word = entry(pe, table, k - 4, 0)
                if start >= 3:
                    window(k - 3, (u - 3) % 4, start < 5)
                if start >= 4:
                    extra(k - 4, u, word)

            for k in range(8):
                step(k, k % 4, k)
            with pe.Fori(2, NS // 4) as i:
                for u in range(4):
                    step(i * 4 + u, u, 8)
            layer2(NS - 1, (NS - 1) % 4, False)
            for k in range(NS - 3, NS):
                window(k, k % 4, False)
                extra(k - 1, (k - 1) % 4, entry(pe, table, k - 1, 0))
            extra(NS - 1, (NS - 1) % 4, entry(pe, table, NS - 1, 0))


def nodes(nc, aggr, route, x, scaled_h, x1_rows, lists, results, u1, c1, u2, c2, gate_w, gate_b):
    slot_a, slot_b, weight_a, weight_b, fill, _, _ = route
    with ExitStack() as ctx:
        a = Alloc(nc, ctx, "node")
        BF = mybir.dt.bfloat16
        zeros = a.sb("zeros", [P, 1, D])
        u1f = a.sb("u1", [P, 2 * DC, D])
        u2f = a.sb("u2", [P, DC, D])
        gw = a.sb("gate_w", [P, DC, NE])
        c1c = a.sb("c1", [P, DC])
        c2r = a.sb("c2", [P, D])
        gb = a.sb("gate_b", [P, NE])
        ident = a.sb("ident", [P, P])
        below = a.sb("below", [P, P], BF)
        ones = a.sb("ones", [P, P], BF)
        lower = a.sb("lower", [P, NE, NE])
        xg = [a.sb(f"x{i}", [P, GT, D]) for i in range(2)]
        hg = [a.sb(f"h{i}", [P, GT, D]) for i in range(2)]
        ht = [a.sb(f"ht{i}", [P, DC, GN]) for i in range(2)]
        s2 = a.sb("s2", [P, DC, GN])
        x1 = [a.sb(f"x1_{i}", [P, GT, D]) for i in range(2)]
        f = [a.sb(f"f{i}", [P, GT, D]) for i in range(2)]
        ft = a.sb("ft", [P, DC, GN])
        stats = a.sb("stats", [P, GT, nc.vector.BN_STATS_DIM])
        mv = a.sb("mean_var", [P, GT, nc.vector.BN_AGGR_DIM])
        var = a.sb("var", [P, GT])
        guess = a.sb("guess", [P, GT], I32)
        half = a.sb("half", [P, GT])
        rstd = a.sb("rstd", [P, GT])
        logit = a.sb("logit", [P, GT, NE])
        prob = a.sb("prob", [P, GT, NE])
        top = a.sb("top", [P, GT])
        beats = a.sb("beats", [P, GT, NE, NE])
        ties = a.sb("ties", [P, GT, NE, NE])
        rank = a.sb("rank", [P, GT, NE])
        first = a.sb("first", [P, GT, NE])
        second = a.sb("second", [P, GT, NE])
        chosen = a.sb("chosen", [P, GT, NE], BF)
        place = a.sb("place", [P, GT, NE])
        pick = a.sb("pick", [P, GT, NE])
        slot_f = a.sb("slot_f", [P, 2, GT])
        ia = [a.sb(f"ia{i}", [P, GT], I32) for i in range(2)]
        ib = [a.sb(f"ib{i}", [P, GT], I32) for i in range(2)]
        pt = a.ps("pt", [P, 2, 512])
        pz = a.ps("pz", [P, 2, 512])
        pu = a.ps("pu", [P, 4, 512])
        plogit = pu[:, 3, 256:256 + GT * NE].rearrange("p (t e) -> p t e", e=NE)
        pplace = pu[:, 3, 320:320 + GT * NE]
        ptotal = pu[:, 3, 384:384 + NE]
        cut = (slice(0, 4 * P), slice(4 * P, GN))

        consts_in = a.sem("consts_in")
        masks = a.sem("masks")
        cleared = a.sem("cleared")
        mask_zero = a.sem("mask_zero")
        prep = a.sem("prep")
        x_in = [a.sem(f"x_in{i}") for i in range(2)]
        turned = a.sem("turned")
        copied = a.sem("copied")
        z_done = a.sem("z_done")
        silu_done = a.sem("silu_done")
        u2_done = a.sem("u2_done")
        x1_done = a.sem("x1_done")
        f_done = a.sem("f_done")
        logit_done = a.sem("logit_done")
        shift_done = a.sem("shift_done")
        exp_done = a.sem("exp_done")
        chosen_done = a.sem("chosen_done")
        place_done = a.sem("place_done")
        slots_done = a.sem("slots_done")
        slots_seen = a.sem("slots_seen")
        f_sent = [a.sem(f"f_sent{i}") for i in range(2)]
        x1_out = [a.sem(f"x1_out{i}") for i in range(2)]
        stats_done = a.sem("stats_done")
        stats_seen = a.sem("stats_seen")
        base_links = a.sem("base_links")
        shift_links = a.sem("shift_links")
        norm_links = a.sem("norm_links")
        router_links = a.sem("router_links")
        route_links = a.sem("route_links")
        block = ctx.enter_context(nc.Block())
        NCONST = 6
        LOOPS = NG // 2

        def rows(ap, g):
            return ap[bass.ds(g * GN, GN), :].rearrange("(t p) d -> p t d", p=P)

        @block.sync
        def _(sp):
            sp.dma_start(u1f[:], u1.rearrange("(c p) n -> p c n", p=P)).then_inc(consts_in, 16)
            sp.dma_start(u2f[:], u2.rearrange("(c p) n -> p c n", p=P)).then_inc(consts_in, 16)
            sp.dma_start(gw[:], gate_w.rearrange("(c p) n -> p c n", p=P)).then_inc(consts_in, 16)
            sp.dma_start(c1c[:], c1).then_inc(consts_in, 16)
            sp.dma_start(c2r[:], c2.partition_broadcast(P)).then_inc(consts_in, 16)
            sp.dma_start(gb[:], gate_b.partition_broadcast(P)).then_inc(consts_in, 16)

            def load(g, u, early):
                if not early:
                    sp.wait_ge(x1_done, g - 1)
                sp.dma_start(xg[u][:], rows(x, g)).then_inc(x_in[u], 16)
                sp.dma_start(hg[u][:], rows(scaled_h, g)).then_inc(x_in[u], 16)

            def clear(g):
                out = results[bass.ds(g * (CLEAR * P), CLEAR * P), :].rearrange("(t p) d -> p t d", p=P)
                sp.dma_start(out, zeros[:].broadcast_to([P, CLEAR, D])).then_inc(cleared, 16)

            def store(g, u):
                clear(g)
                sp.wait_ge(x1_done, g + 1)
                sp.dma_start(rows(x1_rows, g), x1[u][:]).then_inc(x1_out[u], 16)

            load(0, 0, True)
            load(1, 1, True)
            sp.wait_ge(masks, 5)
            with sp.Fori(0, LOOPS - 1) as i:
                for u in range(2):
                    store(i * 2 + u, u)
                    load(i * 2 + u + 2, u, False)
            store(NG - 3, 0)
            load(NG - 1, 0, False)
            store(NG - 2, 1)
            store(NG - 1, 0)
            sp.wait_ge(cleared, 16 * NG)
            sp.wait_ge(x1_out[0], 16 * ((NG + 1) // 2))
            sp.wait_ge(x1_out[1], 16 * (NG // 2))

        @block.gpsimd
        def _(pool):
            nc.gpsimd.memset(ident[:], 0.0).then_inc(mask_zero, 1)
            nc.gpsimd.memset(below[:], 1.0).then_inc(mask_zero, 1)
            nc.gpsimd.memset(lower[:], 1.0).then_inc(mask_zero, 1)
            nc.gpsimd.memset(ones[:], 1.0).then_inc(masks, 1)
            nc.gpsimd.memset(zeros[:], 0.0).then_inc(masks, 1)
            pool.wait_ge(mask_zero, 3)
            nc.gpsimd.affine_select(out=ident[:], in_=ident[:], compare_op=ALU.not_equal, fill=1.0, base=0,
                                    pattern=[[-1, P]], channel_multiplier=1).then_inc(masks, 1)
            nc.gpsimd.affine_select(out=below[:], in_=below[:], compare_op=ALU.is_gt, fill=0.0, base=0,
                                    pattern=[[1, P]], channel_multiplier=-1).then_inc(masks, 1)
            nc.gpsimd.affine_select(out=lower[:], in_=lower[:], compare_op=ALU.is_gt, fill=0.0, base=0,
                                    pattern=[[1, NE], [-1, NE]], channel_multiplier=0).then_inc(masks, 1)

            def scatter(g, u):
                pool.wait_ge(slots_done, g + 1)
                pool.sem_inc(slots_seen, 1)
                for t in range(GT):
                    for index in (ia[u], ib[u]):
                        nc.gpsimd.indirect_dma_start(
                            out=lists, out_offset=bass.IndirectOffsetOnAxis(ap=index[:, t:t + 1], axis=0),
                            in_=f[u][:, t, :], in_offset=None).then_inc(f_sent[u], 16)

            with pool.Fori(0, LOOPS) as i:
                for u in range(2):
                    scatter(i * 2 + u, u)
            scatter(NG - 1, 0)
            pool.wait_ge(f_sent[0], 16 * 2 * GT * ((NG + 1) // 2))
            pool.wait_ge(f_sent[1], 16 * 2 * GT * (NG // 2))

        def turns(k):
            if isinstance(k, int) and k == 0:
                return (2, 3), None
            if isinstance(k, int) and k >= NG - 1:
                return None, (4 * (NG - 1) + 2 * (k - NG + 1), 4 * (NG - 1) + 2 * (k - NG + 1) + 1)
            return (k * 4, k * 4 + 3), (k * 4 + 1, k * 4 + 2)

        @block.scalar
        def _(act):
            act.wait_ge(consts_in, 16 * NCONST)

            def copy(n, out):
                act.wait_ge(turned, n + 1)
                for half_cols, cols in enumerate(cut):
                    last = nc.scalar.activation(out[:, cols], pt[:, half_cols, 0:cols.stop - cols.start], ACT.Copy)
                last.then_inc(copied, 1)

            def silu(k, m):
                act.wait_ge(z_done, k * DC + m + 1)
                for half_cols, cols in enumerate(cut):
                    last = nc.scalar.activation(s2[:, m, cols], pz[:, half_cols, 0:cols.stop - cols.start],
                                                ACT.Silu, bias=c1c[:, m:m + 1])
                last.then_inc(silu_done, 1)

            def step(k, u):
                at_h, at_f = turns(k)
                fixed = isinstance(k, int)
                if not fixed or k < NG:
                    silu(k, 0)
                    if at_h:
                        copy(at_h[0], ht[1 - u][:, 0, :])
                    silu(k, 1)
                if at_f:
                    copy(at_f[0], ft[:, 0, :])
                    copy(at_f[1], ft[:, 1, :])
                if at_h:
                    copy(at_h[1], ht[1 - u][:, 1, :])
                if at_f:
                    act.wait_ge(shift_done, k)
                    nc.scalar.activation(prob[:], logit[:], ACT.Exp).then_inc(exp_done, 1)

            for c in range(DC):
                copy(c, ht[0][:, c, :])
            for k in range(2):
                step(k, k)
            with act.Fori(1, LOOPS) as i:
                for u in range(2):
                    step(i * 2 + u, u)
            for k in range(NG - 1, NG + 1):
                step(k, k % 2)

        @block.tensor
        def _(pe):
            mm = nc.tensor.matmul
            pe.wait_ge(consts_in, 16 * NCONST)
            pe.wait_ge(masks, 5)
            pe.wait_ge(prep, 1)

            def turn(n, tiles, c):
                if not isinstance(n, int) or n > 0:
                    pe.wait_ge(copied, n)
                for t in range(GT):
                    last = nc.tensor.transpose(pt[:, t // 4, (t % 4) * P:(t % 4 + 1) * P],
                                               tiles[:, t, c * P:(c + 1) * P], ident[:])
                last.then_inc(turned, 1)

            def layer1(k, u, m):
                if not isinstance(k, int) or k > 0 or m > 0:
                    pe.wait_ge(silu_done, k * DC + m)
                for half_cols, cols in enumerate(cut):
                    width = cols.stop - cols.start
                    for c in range(2 * DC):
                        if c < DC:
                            moving = ht[u][:, c, cols]
                        else:
                            moving = aggr[:, c - DC, bass.ds(k * GN + cols.start, width)]
                        last = mm(pz[:, half_cols, 0:width], u1f[:, c, m * P:(m + 1) * P], moving,
                                  start=c == 0, stop=c == 2 * DC - 1)
                last.then_inc(z_done, 1)

            def layer2(tiles):
                for t in tiles:
                    for c in range(DC):
                        last = mm(pu[:, t // 2, (t % 2) * D:(t % 2 + 1) * D], s2[:, c, t * P:(t + 1) * P],
                                  u2f[:, c, :], start=c == 0, stop=c == DC - 1)
                return last

            def logits(g):
                for t in range(GT):
                    for c in range(DC):
                        last = mm(plogit[:, t, :], ft[:, c, t * P:(t + 1) * P], gw[:, c, :],
                                  start=c == 0, stop=c == DC - 1)
                last.then_inc(logit_done, 1)

            def places(g):
                pe.wait_ge(chosen_done, g + 1)
                if not isinstance(g, int) or g < NG - 1:
                    pe.wait_ge(x1_done, g + 2)
                sel = chosen[:].rearrange("p t e -> p (t e)")
                mm(pplace, below[:], sel, start=True, stop=False, skip_group_check=True)
                for d in range(1, GT):
                    mm(pplace[:, d * NE:], ones[:], sel[:, 0:(GT - d) * NE], start=False, stop=d == GT - 1,
                       skip_group_check=True)
                for t in range(GT):
                    last = mm(ptotal, ones[:], chosen[:, t, :], start=t == 0, stop=t == GT - 1,
                              skip_group_check=True)
                last.then_inc(place_done, 1)

            def step(k, u, next_loaded):
                fixed = isinstance(k, int)
                updates = not fixed or k < NG
                at_h, at_f = turns(k)
                if updates:
                    pe.wait_ge(copied, 2 if fixed and k == 0 else k * 4)
                    layer1(k, u, 0)
                if at_h:
                    pe.wait_ge(x_in[1 - u], next_loaded)
                    turn(at_h[0], hg[1 - u], 0)
                if not fixed or k >= 2:
                    places(k - 2)
                if updates:
                    layer1(k, u, 1)
                if at_f:
                    pe.wait_ge(f_done, k)
                    turn(at_f[0], f[1 - u], 0)
                if updates:
                    pe.wait_ge(silu_done, k * DC + 2)
                    if not fixed or k > 0:
                        pe.wait_ge(x1_done, k)
                    layer2(range(0, 3))
                if at_f:
                    turn(at_f[1], f[1 - u], 1)
                if not fixed or k >= 2:
                    pe.wait_ge(slots_done, k - 1)
                if updates:
                    layer2(range(3, GT)).then_inc(u2_done, 1)
                if at_h:
                    turn(at_h[1], hg[1 - u], 1)
                if at_f:
                    pe.wait_ge(copied, at_f[1] + 1)
                    logits(k - 1)

            pe.wait_ge(x_in[0], 32)
            for c in range(DC):
                turn(c, hg[0], c)
            step(0, 0, 32)
            step(1, 1, 64)
            with pe.Fori(1, LOOPS) as i:
                for u in range(2):
                    step(i * 2 + u, u, i * 32 + (32 if u == 0 else 64))
            for k in range(NG - 1, NG + 1):
                step(k, k % 2, None)
            places(NG - 1)

        @block.vector
        def _(dve):
            dve.wait_ge(consts_in, 16 * NCONST)
            nc.vector.tensor_scalar(u1f[:, 0:DC, :], u1f[:, 0:DC, :], 1 / H_SCALE, None, ALU.mult)
            nc.vector.tensor_scalar(u1f[:, DC:, :], u1f[:, DC:, :], 1 / MSG_SCALE, None, ALU.mult).then_inc(prep, 1)
            for e in range(NE):
                last = nc.vector.memset(fill[:, e:e + 1], float(e * LIST))
            last.then_inc(prep, 1)
            dve.wait_ge(prep, 2)
            dve.wait_ge(masks, 5)

            def linker(sem, g, per_group):
                n = [0]

                def link(ins):
                    n[0] += 1
                    assert n[0] <= per_group
                    ins.then_inc(sem, 1)
                    dve.wait_ge(sem, g * per_group + n[0])
                return link

            def base(g, u, loaded):
                link = linker(base_links, g, 2)
                dve.wait_ge(x_in[u], loaded)
                if not isinstance(g, int) or g >= 2:
                    dve.wait_ge(x1_out[u], (g // 2) * 16 if isinstance(g, int) else (loaded - 32) // 2)
                    dve.wait_ge(f_sent[u], (g // 2) * (32 * GT) if isinstance(g, int) else (loaded - 32) * GT)
                link(nc.vector.scalar_tensor_tensor(out=x1[u][:], in0=hg[u][:], scalar=1 / H_SCALE, in1=xg[u][:],
                                                    op0=ALU.mult, op1=ALU.add))
                link(nc.vector.tensor_tensor(x1[u][:], x1[u][:], c2r[:].unsqueeze(1).broadcast_to([P, GT, D]),
                                             ALU.add))

            def update(g, u):
                dve.wait_ge(u2_done, g + 1)
                flat = x1[u][:].rearrange("p t d -> p (t d)")
                nc.vector.tensor_tensor(flat, flat, pu[:].rearrange("p b n -> p (b n)")[:, 0:GT * D], ALU.add)\
                    .then_inc(x1_done, 1)
                dve.wait_ge(x1_done, g + 1)

            def norm(g, u):
                link = linker(norm_links, g, 16)
                for t in range(GT):
                    last = nc.vector.bn_stats(stats[:, t, :], x1[u][:, t, :])
                last.then_inc(stats_done, 1)
                dve.wait_ge(stats_done, g + 1)
                dve.sem_inc(stats_seen, 1)
                for t in range(GT):
                    last = nc.vector.bn_aggr(mv[:, t, :], stats[:, t, :])
                link(last)
                link(nc.vector.tensor_scalar(var[:], mv[:, :, 1], EPS, None, ALU.add))
                link(nc.vector.tensor_scalar(guess[:], var[:].bitcast(I32), 1, None, ALU.logical_shift_right))
                link(nc.vector.tensor_scalar(rstd[:].bitcast(I32), guess[:], -1.0, float(0x5F375A00),
                                             ALU.mult, ALU.add))
                for _ in range(3):
                    link(nc.vector.tensor_tensor(half[:], rstd[:], rstd[:], ALU.mult))
                    link(nc.vector.tensor_tensor(half[:], half[:], var[:], ALU.mult))
                    link(nc.vector.tensor_scalar(half[:], half[:], -0.5, 1.5, ALU.mult, ALU.add))
                    link(nc.vector.tensor_tensor(rstd[:], rstd[:], half[:], ALU.mult))
                for t in range(GT):
                    last = nc.vector.tensor_scalar(f[u][:, t, :], x1[u][:, t, :], mv[:, t, 0:1],
                                                   rstd[:, t:t + 1], ALU.subtract, ALU.mult)
                last.then_inc(f_done, 1)

            def shift(g):
                link = linker(shift_links, g, 2)
                dve.wait_ge(logit_done, g + 1)
                link(nc.vector.tensor_tensor(logit[:], plogit, gb[:].unsqueeze(1).broadcast_to([P, GT, NE]),
                                             ALU.add))
                link(nc.vector.tensor_reduce(top[:], logit[:], AX.X, ALU.max))
                nc.vector.tensor_tensor(logit[:], logit[:], top[:].unsqueeze(2).broadcast_to([P, GT, NE]),
                                        ALU.subtract).then_inc(shift_done, 1)

            def router(g):
                link = linker(router_links, g, 10)
                wide = [P, GT, NE, NE]
                dve.wait_ge(exp_done, g + 1)
                link(nc.vector.tensor_reduce(top[:], prob[:], AX.X, ALU.add))
                link(nc.vector.reciprocal(top[:], top[:]))
                link(nc.vector.tensor_tensor(prob[:], prob[:], top[:].unsqueeze(2).broadcast_to([P, GT, NE]),
                                             ALU.mult))
                other = prob[:].unsqueeze(2).broadcast_to(wide)
                own = prob[:].unsqueeze(3).broadcast_to(wide)
                nc.vector.tensor_tensor(beats[:], other, own, ALU.is_gt)
                link(nc.vector.tensor_tensor(ties[:], other, own, ALU.is_equal))
                link(nc.vector.tensor_tensor(ties[:], ties[:], lower[:].unsqueeze(1).broadcast_to(wide), ALU.mult))
                link(nc.vector.tensor_tensor(beats[:], beats[:], ties[:], ALU.add))
                link(nc.vector.tensor_reduce(rank[:], beats[:], AX.X, ALU.add))
                nc.vector.tensor_scalar(chosen[:], rank[:], 2.0, None, ALU.is_lt).then_inc(chosen_done, 1)
                nc.vector.tensor_scalar(first[:], rank[:], 0.0, None, ALU.is_equal)
                link(nc.vector.tensor_scalar(second[:], rank[:], 1.0, None, ALU.is_equal))
                tiles = bass.ds(g * GT, GT)
                link(nc.vector.tensor_tensor(pick[:], first[:], prob[:], ALU.mult))
                nc.vector.tensor_reduce(weight_a[:, tiles], pick[:], AX.X, ALU.add)
                link(nc.vector.tensor_tensor(rank[:], second[:], prob[:], ALU.mult))
                nc.vector.tensor_reduce(weight_b[:, tiles], rank[:], AX.X, ALU.add)

            def route(g, u):
                link = linker(route_links, g, 3)
                dve.wait_ge(place_done, g + 1)
                link(nc.vector.tensor_tensor(place[:], pplace.rearrange("p (t e) -> p t e", e=NE),
                                             fill[:].unsqueeze(1).broadcast_to([P, GT, NE]), ALU.add))
                nc.vector.tensor_tensor(fill[:], fill[:], ptotal, ALU.add)
                nc.vector.tensor_tensor(first[:], first[:], place[:], ALU.mult)
                link(nc.vector.tensor_tensor(second[:], second[:], place[:], ALU.mult))
                nc.vector.tensor_reduce(slot_f[:, 0, :], first[:], AX.X, ALU.add)
                link(nc.vector.tensor_reduce(slot_f[:, 1, :], second[:], AX.X, ALU.add))
                tiles = bass.ds(g * GT, GT)
                nc.vector.tensor_copy(slot_a[:, tiles], slot_f[:, 0, :])
                nc.vector.tensor_copy(slot_b[:, tiles], slot_f[:, 1, :])
                nc.vector.tensor_copy(ia[u][:], slot_f[:, 0, :])
                nc.vector.tensor_copy(ib[u][:], slot_f[:, 1, :]).then_inc(slots_done, 1)
                dve.wait_ge(slots_done, g + 1)

            def step(k, u, next_loaded):
                fixed = isinstance(k, int)
                if not fixed or k >= 1:
                    shift(k - 1)
                if not fixed or k < NG:
                    update(k, u)
                if not fixed or k >= 1:
                    router(k - 1)
                if not fixed or k < NG:
                    norm(k, u)
                if not fixed or k >= 1:
                    route(k - 1, 1 - u)
                if not fixed or k < NG - 1:
                    base(k + 1, 1 - u, next_loaded)

            base(0, 0, 32)
            step(0, 0, 32)
            step(1, 1, 64)
            with dve.Fori(1, LOOPS) as i:
                for u in range(2):
                    step(i * 2 + u, u, i * 32 + (32 if u == 0 else 64))
            for k in range(NG - 1, NG + 1):
                step(k, k % 2, None)


def experts(nc, route, lists, results, w1, b1, w2, b2):
    slot_a, slot_b, _, _, fill, index_a, index_b = route
    with ExitStack() as ctx:
        a = Alloc(nc, ctx, "exp")
        count = a.sb("count", [P, NE])
        count_i = a.sb("count_i", [P, NE], I32)
        blocks_i = a.sb("blocks_i", [P, NE], I32)
        blocks_f = a.sb("blocks_f", [P, NE])
        upto = a.sb("upto", [P, NE])
        nought = a.sb("nought", [P, NE])
        shift = a.sb("shift", [P, NE])
        moved = [a.sb(f"moved{i}", [P, NT]) for i in range(2)]
        table = a.sb("table", [P, NE, 4], I32)
        zeros = a.sb("zeros", [P, XT, D])
        ident = a.sb("ident", [P, P])
        w1f = a.sb("w1f", [P, DC, H])
        w2f = a.sb("w2f", [P, HC, D])
        w1hi = [a.sb(f"w1hi{i}", [P, DC, H], F32R) for i in range(2)]
        w1lo = [a.sb(f"w1lo{i}", [P, DC, H], F32R) for i in range(2)]
        w2hi = [a.sb(f"w2hi{i}", [P, HC, D], F32R) for i in range(2)]
        w2lo = [a.sb(f"w2lo{i}", [P, HC, D], F32R) for i in range(2)]
        b1c = a.sb("b1c", [P, NE, HC])
        b2r = a.sb("b2r", [P, NE, D])
        rows = a.sb("rows", [P, XT, D])
        xhi, xlo = a.sb("xhi", [P, DC, XB], F32R), a.sb("xlo", [P, DC, XB], F32R)
        g = a.sb("g", [P, HC, XB])
        ghi, glo = a.sb("ghi", [P, HC, XB], F32R), a.sb("glo", [P, HC, XB], F32R)
        y = a.sb("y", [P, XT, D])
        pt = a.ps("pt", [P, DC, XB])
        p1 = a.ps("p1", [P, HC, XB])
        p2 = a.ps("p2", [P, XT, D])

        consts_in = a.sem("consts_in")
        zero_done = a.sem("zero_done")
        ident_done = a.sem("ident_done")
        table_done = a.sem("table_done")
        tails_out = a.sem("tails_out")
        w_in = a.sem("w_in")
        w_split = a.sem("w_split")
        rows_in = a.sem("rows_in")
        turned = a.sem("turned")
        xhi_done = a.sem("xhi_done")
        xlo_done = a.sem("xlo_done")
        l1_done = a.sem("l1_done")
        gelu_done = a.sem("gelu_done")
        ghi_done = a.sem("ghi_done")
        glo_done = a.sem("glo_done")
        l2_done = a.sem("l2_done")
        y_done = a.sem("y_done")
        y_seen = a.sem("y_seen")
        y_out = a.sem("y_out")
        prep = a.sem("prep")
        split_step = a.sem("split_step")
        block = ctx.enter_context(nc.Block())

        def entry(eng, e, column, most):
            return eng.value_load(table[0:1, bass.ds(e, 1), column:column + 1].rearrange("o s c -> o (s c)"),
                                  min_val=0, max_val=most)

        def each_block(eng, e, body):
            blocks = entry(eng, e, 0, MOST)
            with eng.If(blocks > 0):
                before = entry(eng, e, 1, ALL)
                with eng.Fori(0, blocks) as q:
                    m = nc.s_assert_within(before + q, 0, ALL - 1, skip_runtime_bounds_check_because=
                                           "ALL blocks hold two rows per node however they are routed")
                    body(m, q)

        @block.sync
        def _(sp):
            sp.dma_start(b1c[:], b1).then_inc(consts_in, 16)
            sp.dma_start(b2r[:], b2.partition_broadcast(P)).then_inc(consts_in, 16)
            sp.wait_ge(zero_done, 1)
            sp.wait_ge(table_done, 1)
            for e in range(NE):
                row = entry(sp, e, 2, NPAD)
                out = lists[bass.ds(row + e * LIST, XB), :].rearrange("(t p) d -> p t d", p=P)
                sp.dma_start(out, zeros[:]).then_inc(tails_out, 16)

            def weights(e):
                sp.dma_start(w1f[:], w1[bass.ds(e * D, D), :].rearrange("(c p) n -> p c n", p=P)).then_inc(w_in, 16)
                sp.dma_start(w2f[:], w2[bass.ds(e * H, H), :].rearrange("(c p) n -> p c n", p=P)).then_inc(w_in, 16)

            def load(m, row):
                sp.wait_ge(turned, m)
                sp.dma_start(rows[:], lists[bass.ds(row, XB), :].rearrange("(t p) d -> p t d", p=P))\
                    .then_inc(rows_in, 16)

            weights(0)
            sp.wait_ge(tails_out, 16 * NE)
            with sp.Fori(0, NE) as e:
                sp.wait_ge(w_split, e + 1)
                more = nc.s_assert_within(
                    e + 1 - (e + 1) // NE, 0, NE - 1,
                    skip_runtime_bounds_check_because="e < NE; the last load is of expert NE - 1 again")
                weights(more)
                each_block(sp, e, lambda m, q: load(m, e * LIST + q * XB))
            load(entry(sp, NE - 1, 1, ALL) + entry(sp, NE - 1, 0, MOST), 0)
            sp.wait_ge(w_in, 32 * (NE + 1))

        @block.gpsimd
        def _(pool):
            nc.gpsimd.memset(zeros[:], 0.0).then_inc(zero_done, 1)
            nc.gpsimd.memset(ident[:], 0.0).then_inc(ident_done, 1)
            pool.wait_ge(ident_done, 1)
            nc.gpsimd.affine_select(out=ident[:], in_=ident[:], compare_op=ALU.not_equal, fill=1.0, base=0,
                                    pattern=[[-1, P]], channel_multiplier=1).then_inc(ident_done, 1)
            pool.wait_ge(table_done, 1)

            def store(m, row):
                pool.wait_ge(y_done, m + 1)
                pool.sem_inc(y_seen, 1)
                pool.dma_start(results[bass.ds(row, XB), :].rearrange("(t p) d -> p t d", p=P), y[:])\
                    .then_inc(y_out, 16)

            with pool.Fori(0, NE) as e:
                each_block(pool, e, lambda m, q: store(m, m * XB))
            total = entry(pool, NE - 1, 1, ALL) + entry(pool, NE - 1, 0, MOST)
            pool.wait_ge(y_out, total * 16)

        @block.scalar
        def _(act):
            act.wait_ge(consts_in, 32)
            act.wait_ge(table_done, 1)

            def round_x(m):
                act.wait_ge(turned, m + 1)
                act.wait_ge(l1_done, m * HC)
                nc.scalar.activation(xhi[:], pt[:], ACT.Copy).then_inc(xhi_done, 1)

            def body(m, e):
                for c in range(HC):
                    act.wait_ge(l1_done, m * HC + c + 1)
                    act.wait_ge(glo_done, m * HC)
                    nc.scalar.activation(g[:, c, :], p1[:, c, :], ACT.Gelu,
                                         bias=b1c[:, bass.ds(e, 1), c:c + 1].rearrange("p o c -> p (o c)"))\
                        .then_inc(gelu_done, 1)
                    act.wait_ge(gelu_done, m * HC + c + 1)
                    act.wait_ge(l2_done, m)
                    nc.scalar.activation(ghi[:, c, :], g[:, c, :], ACT.Copy).then_inc(ghi_done, 1)
                round_x(m + 1)

            round_x(0)
            with act.Fori(0, NE) as e:
                each_block(act, e, lambda m, q: body(m, e))

        @block.vector
        def _(dve):
            n = [0]

            def chain(ins):
                n[0] += 1
                ins.then_inc(prep, 1)
                dve.wait_ge(prep, n[0])

            for e in range(NE):
                last = nc.vector.tensor_scalar(count[:, e:e + 1], fill[:, e:e + 1], float(e * LIST), None,
                                               ALU.subtract)
            chain(last)
            chain(nc.vector.tensor_copy(count_i[:], count[:]))
            chain(nc.vector.tensor_scalar(blocks_f[:], count[:], float(XB - 1), None, ALU.add))
            chain(nc.vector.tensor_copy(blocks_i[:], blocks_f[:]))
            chain(nc.vector.tensor_scalar(blocks_i[:], blocks_i[:], XB.bit_length() - 1, None,
                                          ALU.logical_shift_right))
            chain(nc.vector.tensor_copy(blocks_f[:], blocks_i[:]))
            chain(nc.vector.memset(nought[:], 0.0))
            chain(nc.vector.tensor_tensor_scan(upto[:], blocks_f[:], nought[:], 0.0, ALU.add, ALU.add))
            chain(nc.vector.tensor_tensor(upto[:], upto[:], blocks_f[:], ALU.subtract))
            nc.vector.tensor_copy(table[:, :, 0], blocks_i[:])
            nc.vector.tensor_copy(table[:, :, 2], count_i[:])
            nc.vector.tensor_copy(table[:, :, 1], upto[:]).then_inc(table_done, 1)
            dve.wait_ge(table_done, 1)
            dve.wait_ge(consts_in, 32)

            def split(e, u, loaded, step):
                dve.wait_ge(w_in, loaded)
                nc.vector.tensor_copy(w1hi[u][:], w1f[:])
                nc.vector.tensor_copy(w2hi[u][:], w2f[:]).then_inc(split_step, 1)
                dve.wait_ge(split_step, step)
                nc.vector.tensor_tensor(w1lo[u][:], w1f[:], w1hi[u][:].bitcast(F32), ALU.subtract)
                nc.vector.tensor_tensor(w2lo[u][:], w2f[:], w2hi[u][:].bitcast(F32), ALU.subtract)\
                    .then_inc(w_split, 1)

            def x_low(m):
                dve.wait_ge(xhi_done, m + 1)
                dve.wait_ge(l1_done, m * HC)
                nc.vector.tensor_tensor(xlo[:], pt[:], xhi[:].bitcast(F32), ALU.subtract).then_inc(xlo_done, 1)

            def body(m, e):
                for c in range(HC):
                    dve.wait_ge(ghi_done, m * HC + c + 1)
                    dve.wait_ge(l2_done, m)
                    nc.vector.tensor_tensor(glo[:, c, :], g[:, c, :], ghi[:, c, :].bitcast(F32), ALU.subtract)\
                        .then_inc(glo_done, 1)
                x_low(m + 1)
                dve.wait_ge(l2_done, m + 1)
                dve.wait_ge(y_out, m * 16)
                nc.vector.tensor_tensor(y[:], p2[:], b2r[:, bass.ds(e, 1), :].broadcast_to([P, XT, D]),
                                        ALU.add).then_inc(y_done, 1)

            chain(nc.vector.tensor_scalar(shift[:], upto[:], float(XB), None, ALU.mult))
            for e in range(NE - 1, 0, -1):
                chain(nc.vector.tensor_tensor(shift[:, e:e + 1], shift[:, e:e + 1], shift[:, e - 1:e],
                                              ALU.subtract))
            chain(nc.vector.tensor_scalar(shift[:, 1:NE], shift[:, 1:NE], float(LIST), None, ALU.subtract))
            for slot, index in ((slot_a, index_a), (slot_b, index_b)):
                chain(nc.vector.tensor_copy(moved[0][:], slot[:]))
                for e in range(1, NE):
                    chain(nc.vector.tensor_scalar(moved[1][:], slot[:], float(e * LIST), shift[:, e:e + 1],
                                                  ALU.is_ge, ALU.mult))
                    chain(nc.vector.tensor_tensor(moved[0][:], moved[0][:], moved[1][:], ALU.add))
                chain(nc.vector.tensor_copy(index[:], moved[0][:]))
            split(0, 0, 32, 1)
            x_low(0)
            with dve.Fori(0, NE // 2) as i:
                for u in range(2):
                    e = i * 2 + u
                    dve.wait_ge(l2_done, entry(dve, e, 1, ALL))
                    split(e + 1, (u + 1) % 2, e * 32 + 64, e + 2)
                    each_block(dve, e, lambda m, q: body(m, e))

        @block.tensor
        def _(pe):
            mm = nc.tensor.matmul
            pe.wait_ge(ident_done, 2)
            pe.wait_ge(table_done, 1)

            def turn(m):
                pe.wait_ge(rows_in, m * 16 + 16)
                pe.wait_ge(xlo_done, m)
                for c in range(DC):
                    for t in range(XT):
                        last = nc.tensor.transpose(pt[:, c, t * P:(t + 1) * P], rows[:, t, c * P:(c + 1) * P],
                                                   ident[:])
                last.then_inc(turned, 1)

            def body(m, u):
                pe.wait_ge(xlo_done, m + 1)
                pe.wait_ge(gelu_done, m * HC)
                for j in range(HC):
                    for c in range(DC):
                        hi, lo = (w[u][:, c, j * P:(j + 1) * P] for w in (w1hi, w1lo))
                        mm(p1[:, j, :], hi, xhi[:, c, :], start=c == 0, stop=False)
                        mm(p1[:, j, :], hi, xlo[:, c, :], start=False, stop=False)
                        last = mm(p1[:, j, :], lo, xhi[:, c, :], start=False, stop=c == DC - 1)
                    last.then_inc(l1_done, 1)
                turn(m + 1)
                pe.wait_ge(glo_done, m * HC + HC)
                pe.wait_ge(y_done, m)
                for t in range(XT):
                    for j in range(HC):
                        hi, lo = (x[:, j, t * P:(t + 1) * P] for x in (ghi, glo))
                        mm(p2[:, t, :], hi, w2hi[u][:, j, :], start=j == 0, stop=False)
                        mm(p2[:, t, :], hi, w2lo[u][:, j, :], start=False, stop=False)
                        last = mm(p2[:, t, :], lo, w2hi[u][:, j, :], start=False, stop=j == HC - 1)
                last.then_inc(l2_done, 1)

            turn(0)
            with pe.Fori(0, NE // 2) as i:
                for u in range(2):
                    e = i * 2 + u
                    pe.wait_ge(w_split, e + 1)
                    each_block(pe, e, lambda m, q: body(m, u))


def combine(nc, route, x1_rows, results, out):
    _, _, weight_a, weight_b, _, index_a, index_b = route
    with ExitStack() as ctx:
        a = Alloc(nc, ctx, "comb")
        x1 = [a.sb(f"x1_{i}", [P, GT, D]) for i in range(2)]
        ya = [a.sb(f"ya{i}", [P, GT, D]) for i in range(2)]
        yb = [a.sb(f"yb{i}", [P, GT, D]) for i in range(2)]
        x1_in = [a.sem(f"x1_in{i}") for i in range(2)]
        y_in = [a.sem(f"y_in{i}") for i in range(2)]
        half_done = a.sem("half_done")
        sum_done = a.sem("sum_done")
        sent = [a.sem(f"sent{i}") for i in range(2)]
        block = ctx.enter_context(nc.Block())
        x_v = x1_rows.rearrange("(g t p) d -> g p t d", p=P, t=GT)
        o_v = out.rearrange("(g t p) d -> g p t d", p=P, t=GT)

        @block.sync
        def _(sp):
            for g in range(NG):
                if g >= 2:
                    sp.wait_ge(sent[g % 2], 16 * (g // 2))
                sp.dma_start(x1[g % 2][:], x_v[g]).then_inc(x1_in[g % 2], 16)

        @block.gpsimd
        def _(pool):
            for g in range(NG):
                if g >= 2:
                    pool.wait_ge(sum_done, g - 1)
                for t in range(GT):
                    for slot, y in ((index_a, ya), (index_b, yb)):
                        nc.gpsimd.indirect_dma_start(
                            out=y[g % 2][:, t, :], out_offset=None, in_=results,
                            in_offset=bass.IndirectOffsetOnAxis(ap=slot[:, g * GT + t:g * GT + t + 1], axis=0),
                        ).then_inc(y_in[g % 2], 16)

        @block.vector
        def _(dve):
            for g in range(NG):
                dve.wait_ge(x1_in[g % 2], 16 * (g // 2 + 1))
                dve.wait_ge(y_in[g % 2], 16 * 2 * GT * (g // 2 + 1))
                for step, (weight, y) in enumerate(((weight_a, ya), (weight_b, yb))):
                    for t in range(GT):
                        tile = g * GT + t
                        last = nc.vector.scalar_tensor_tensor(
                            out=x1[g % 2][:, t, :], in0=y[g % 2][:, t, :], scalar=weight[:, tile:tile + 1],
                            in1=x1[g % 2][:, t, :], op0=ALU.mult, op1=ALU.add)
                    if step == 0:
                        last.then_inc(half_done, 1)
                        dve.wait_ge(half_done, g + 1)
                last.then_inc(sum_done, 1)

        @block.scalar
        def _(act):
            for g in range(NG):
                act.wait_ge(sum_done, g + 1)
                act.dma_start(o_v[g], x1[g % 2][:]).then_inc(sent[g % 2], 16)
            act.wait_ge(sent[0], 16 * ((NG + 1) // 2))
            act.wait_ge(sent[1], 16 * (NG // 2))


def build(nc, x, src_cols, dst_cols, dst_rows, rbf, w1, b1, w2, b2, u1, c1, u2, c2,
          gate_w, gate_b, ew1, eb1, ew2, eb2, out):
    scaled_h = nc.dram_tensor("scaled_h", (NPAD, D), F32, kind="Internal").ap()
    seg_scratch = nc.dram_tensor("seg_scratch", (NS, 2), I32, kind="Internal").ap()
    seg_table = nc.dram_tensor("seg_table", (1, NS, 4), I32, kind="Internal").ap()
    x1_rows = nc.dram_tensor("x1_rows", (NPAD, D), F32, kind="Internal").ap()
    lists = nc.dram_tensor("lists", (NE * LIST, D), F32, kind="Internal").ap()
    results = nc.dram_tensor("results", (RES, D), F32, kind="Internal").ap()
    with ExitStack() as ctx:
        a = Alloc(nc, ctx, "all")
        route = (a.sb("slot_a", [P, NT]), a.sb("slot_b", [P, NT]),
                 a.sb("weight_a", [P, NT]), a.sb("weight_b", [P, NT]), a.sb("fill", [P, NE]),
                 a.sb("index_a", [P, NT], I32), a.sb("index_b", [P, NT], I32))
        with ExitStack() as inner:
            aggr = inner.enter_context(nc.sbuf_tensor("aggr", [P, DC, AW], F32))
            normalise(nc, x, scaled_h, dst_rows, seg_scratch, seg_table)
            edges(nc, aggr, rbf, src_cols, dst_cols, scaled_h, seg_table, w1, b1, w2, b2)
            nodes(nc, aggr, route, x, scaled_h, x1_rows, lists, results, u1, c1, u2, c2, gate_w, gate_b)
        experts(nc, route, lists, results, ew1, eb1, ew2, eb2)
        combine(nc, route, x1_rows, results, out)


def kernel(**inputs):
    import concourse.bacc as bacc
    from concourse.bass_utils import run_bass_kernel_spmd

    v = {name: np.asarray(a) for name, a in inputs.items()}

    def padded(a, rows, value=0):
        return np.concatenate([a, np.full((rows - a.shape[0], *a.shape[1:]), value, a.dtype)])

    src = padded(v["src"], EPAD)
    dst = padded(v["dst"], EPAD, NPAD - 1)
    arrays = {
        "x": padded(v["x"], NPAD),
        "src_cols": src.reshape(NS * ST, P).T,
        "dst_cols": dst.reshape(NS * ST, P).T,
        "dst_rows": dst.reshape(2, HALF_S, SUP).transpose(1, 0, 2),
        "rbf": padded(v["edge_attr_64"], EPAD).T,
        "w1": v["L0_gnn_W1"],
        "b1": v["L0_gnn_b1"].reshape(DC, P).T,
        "w2": v["L0_gnn_W2"],
        "b2": v["L0_gnn_b2"].reshape(1, D),
        "u1": v["L0_gnn_U1"],
        "c1": v["L0_gnn_c1"].reshape(DC, P).T,
        "u2": v["L0_gnn_U2"],
        "c2": v["L0_gnn_c2"],
        "gate_w": v["L0_ffn_gate_w"],
        "gate_b": v["L0_ffn_gate_b"],
        "ew1": v["L0_ffn_W1"].reshape(NE * D, H),
        "eb1": v["L0_ffn_b1"].reshape(NE, HC, P).transpose(2, 0, 1),
        "ew2": v["L0_ffn_W2"].reshape(NE * H, D),
        "eb2": v["L0_ffn_b2"],
    }
    nc = bacc.Bacc("TRN2", target_bir_lowering=False, num_devices=1)
    feeds, args = {}, []
    for name, a in arrays.items():
        feeds[f"in_{name}"] = np.ascontiguousarray(a)
        args.append(nc.dram_tensor(f"in_{name}", a.shape, mybir.dt.from_np(a.dtype), kind="ExternalInput").ap())
    out = nc.dram_tensor("out", (NPAD, D), F32, kind="ExternalOutput").ap()
    build(nc, *args, out)
    result = run_bass_kernel_spmd(nc, [feeds], core_ids=[0])
    return result.results[0]["out"][:N_NODES]
```

```python
import concourse.bass as bass
import numpy as np
from concourse import mybir
from contextlib import ExitStack

F32 = mybir.dt.float32
F32R = mybir.dt.float32r
F16 = mybir.dt.float16
I32 = mybir.dt.int32
ALU = mybir.AluOpType
ACT = mybir.ActivationFunctionType
AX = mybir.AxisListType

P = 128
N_NODES = 6250
N_EDGES = 100000
D = 256
DC = D // P
NRBF = 64
NT = -(-N_NODES // P)
NPAD = NT * P
SUP = 512
ST = SUP // P
NS = -(-N_EDGES // SUP)
EPAD = NS * SUP
HALF_S = NS // 2
WIN = 64
PACK = 1 << 13
AW = NPAD + WIN
GT = 7
NG = NT // GT
GN = GT * P
GH = GN // 2
NE = 8
H = 512
HC = H // P
XB = 512
XT = XB // P
LIST = NPAD + XB
MOST = -(-NPAD // XB)
ALL = 2 * NPAD // XB + NE
LISTED = 1 << MOST.bit_length()
WHY = "ALL blocks hold two rows per node however they are routed"
DR = D + 4
RANK = XB + NPAD
EPS = 1e-5
H_SCALE = 512.0
MSG_SCALE = 2 * H_SCALE


class Alloc:

    def __init__(self, nc, ctx, stage):
        self.nc, self.ctx, self.stage = nc, ctx, stage

    def sb(self, name, shape, dt=F32):
        return self.ctx.enter_context(self.nc.sbuf_tensor(f"{self.stage}_{name}", shape, dt))

    def ps(self, name, shape):
        return self.ctx.enter_context(self.nc.psum_tensor(f"{self.stage}_{name}", shape, F32))

    def sem(self, name):
        return self.ctx.enter_context(self.nc.semaphore(f"{self.stage}_{name}"))


def inverse_root(dve, chain, r, root, v):
    chain(dve.reciprocal(r, root))
    chain(dve.tensor_tensor(root, r, r, ALU.mult))
    chain(dve.tensor_tensor(root, root, v, ALU.mult))
    chain(dve.tensor_scalar(root, root, -0.5, 1.5, ALU.mult, ALU.add))
    chain(dve.tensor_tensor(r, r, root, ALU.mult))


def normalise(nc, node, aggr, x, scaled_h, dst_rows, seg_scratch, seg_table):
    with ExitStack() as ctx:
        a = Alloc(nc, ctx, "norm")
        xin = [a.sb(f"x{i}", [P, GT, D]) for i in range(NG)]
        hout = [a.sb(f"h{i}", [P, GT, D]) for i in range(3)]
        stats = a.sb("stats", [P, GT, nc.vector.BN_STATS_DIM])
        mv = [a.sb(f"mean_var{i}", [P, GT, nc.vector.BN_AGGR_DIM]) for i in range(3)]
        rstd = [a.sb(f"rstd{i}", [P, GT]) for i in range(3)]
        var = [a.sb(f"var{i}", [P, GT]) for i in range(3)]
        std = [a.sb(f"std{i}", [P, GT]) for i in range(3)]
        shift = [a.sb(f"shift{i}", [P, GT]) for i in range(3)]
        rows = a.sb("dst_rows", [HALF_S, 2, SUP], I32)
        rows_f = a.sb("dst_rows_f", [HALF_S, 2, SUP])
        span = a.sb("span", [HALF_S, 2, 2])
        span_i = a.sb("span_i", [HALF_S, 2, 2], I32)
        flat = a.sb("flat", [1, NS, 2], I32)
        flat_f = a.sb("flat_f", [1, NS])
        zeros = a.sb("zeros", [1, NS])
        upto = a.sb("upto", [1, NS])
        table = a.sb("table", [1, NS, 4], I32)
        x_in = [a.sem(f"x_in{i}") for i in range(NG)]
        h_out = [a.sem(f"h_out{i}") for i in range(3)]
        h_ready = a.sem("h_ready")
        rows_in = a.sem("rows_in")
        span_ready = a.sem("span_ready")
        span_out = a.sem("span_out")
        flat_in = a.sem("flat_in")
        table_ready = a.sem("table_ready")
        table_out = a.sem("table_out")
        step = a.sem("vector_step")
        var_ready = a.sem("var_ready")
        std_ready = a.sem("std_ready")
        scales_ready = a.sem("scales_ready")
        start_made = a.sem("start_made")
        x_v = x.rearrange("(g t p) d -> g p t d", p=P, t=GT)
        h_v = scaled_h.rearrange("(g t p) d -> g p t d", p=P, t=GT)
        block = ctx.enter_context(nc.Block())

        @block.gpsimd
        def _(pool):
            nc.gpsimd.iota(node[:], pattern=[[1, AW]], base=0, channel_multiplier=0,
                           allow_small_or_imprecise_dtypes=True).then_inc(start_made, 1)
            nc.gpsimd.memset(aggr[:], 0.0).then_inc(start_made, 1)
            pool.wait_ge(start_made, 2)
            pool.wait_ge(span_ready, 1)
            pool.dma_start(seg_scratch.rearrange("(a p) c -> p a c", a=2), span_i[:]).then_inc(span_out, 16)
            pool.wait_ge(span_out, 16)
            pool.dma_start(flat[:], seg_scratch.rearrange("(o s) c -> o s c", o=1)).then_inc(flat_in, 16)
            pool.wait_ge(table_ready, 1)
            pool.dma_start(seg_table, table[:]).then_inc(table_out, 16)
            pool.wait_ge(table_out, 16)

        @block.sync
        def _(sp):
            sp.dma_start(rows[:], dst_rows).then_inc(rows_in, 16)
            for g in range(NG):
                sp.dma_start(xin[g][:], x_v[g]).then_inc(x_in[g], 16)

        @block.scalar
        def _(act):

            def root(g):
                act.wait_ge(var_ready, g + 1)
                nc.scalar.activation(std[g % 3][:], var[g % 3][:], ACT.Sqrt).then_inc(std_ready, 1)

            root(0)
            root(1)
            for g in range(NG):
                act.wait_ge(scales_ready, g + 1)
                if g >= 3:
                    act.wait_ge(h_out[g % 3], 16 * (g // 3))
                for t in range(GT):
                    last = nc.scalar.activation(hout[g % 3][:, t, :], xin[g][:, t, :], ACT.Identity,
                                                bias=shift[g % 3][:, t:t + 1], scale=rstd[g % 3][:, t:t + 1])
                last.then_inc(h_ready, 1)
                if g + 2 < NG:
                    root(g + 2)
                act.wait_ge(h_ready, g + 1)
                act.dma_start(h_v[g], hout[g % 3][:]).then_inc(h_out[g % 3], 16)
            for i in range(3):
                act.wait_ge(h_out[i], 16 * ((NG + 2 - i) // 3))

        @block.vector
        def _(dve):
            n = [0]

            def link(ins):
                n[0] += 1
                ins.then_inc(step, 1)
                dve.wait_ge(step, n[0])

            def spans():
                dve.wait_ge(rows_in, 16)
                link(nc.vector.tensor_copy(rows_f[:], rows[:]))
                nc.vector.tensor_reduce(span[:, :, 0:1], rows_f[:], AX.X, ALU.min)
                link(nc.vector.tensor_reduce(span[:, :, 1:2], rows_f[:], AX.X, ALU.max))
                link(nc.vector.tensor_tensor(span[:, :, 1:2], span[:, :, 1:2], span[:, :, 0:1], ALU.subtract))
                link(nc.vector.tensor_copy(span_i[:], span[:]))
                nc.vector.tensor_scalar(span_i[:, :, 1:2], span_i[:, :, 1:2], WIN.bit_length() - 1, None,
                                        ALU.logical_shift_right).then_inc(span_ready, 1)

            def window_table():
                link(nc.vector.memset(zeros[:], 0.0))
                link(nc.vector.memset(table[:], 0))
                dve.wait_ge(flat_in, 16)
                link(nc.vector.tensor_copy(flat_f[:], flat[:, :, 1]))
                link(nc.vector.tensor_tensor_scan(upto[:], flat_f[:], zeros[:], 0.0, ALU.add, ALU.add))
                link(nc.vector.tensor_tensor(upto[:], upto[:], flat_f[:], ALU.subtract))
                link(nc.vector.tensor_scalar(flat_f[:], flat_f[:], float(PACK), None, ALU.mult))
                link(nc.vector.tensor_tensor(flat_f[:], flat_f[:], flat[:, :, 0], ALU.add))
                nc.vector.tensor_copy(table[:, :, 0], flat_f[:])
                nc.vector.tensor_copy(table[:, :, 1], flat[:, :, 0])
                nc.vector.tensor_copy(table[:, :, 2], upto[:]).then_inc(table_ready, 1)

            def statistics(g):
                dve.wait_ge(x_in[g], 16)
                for t in range(GT):
                    last = nc.vector.bn_stats(stats[:, t, :], xin[g][:, t, :])
                link(last)
                for t in range(GT):
                    last = nc.vector.bn_aggr(mv[g % 3][:, t, :], stats[:, t, :])
                link(last)
                nc.vector.tensor_scalar(var[g % 3][:], mv[g % 3][:, :, 1], EPS, H_SCALE ** -2, ALU.add, ALU.mult)\
                    .then_inc(var_ready, 1)

            def scales(g):
                dve.wait_ge(std_ready, g + 1)
                if g >= 3:
                    dve.wait_ge(h_ready, g - 2)
                inverse_root(nc.vector, link, rstd[g % 3][:], std[g % 3][:], var[g % 3][:])
                nc.vector.scalar_tensor_tensor(out=shift[g % 3][:], in0=mv[g % 3][:, :, 0], scalar=-1.0,
                                               in1=rstd[g % 3][:], op0=ALU.mult, op1=ALU.mult)\
                    .then_inc(scales_ready, 1)

            spans()
            statistics(0)
            statistics(1)
            for g in range(NG):
                scales(g)
                if g + 2 < NG:
                    statistics(g + 2)
                if g == NG - 2:
                    window_table()


def split_weight(dve, chain, hi, lo, w):
    chain(dve.tensor_copy(hi, w))
    chain(dve.tensor_tensor(lo, w, hi.bitcast(F32), ALU.subtract))


def entry(eng, table, row, column):
    most = (PACK * (NPAD // WIN + 1), NPAD - 1, NS * (NPAD // WIN))[column]
    return eng.value_load(table[0:1, bass.ds(row, 1), column:column + 1].rearrange("o s c -> o (s c)"),
                          min_val=0, max_val=most)


def edges(nc, node, aggr, rbf, src_cols, dst_cols, scaled_h, seg_table, w1, b1, w2, b2):
    with ExitStack() as ctx:
        a = Alloc(nc, ctx, "edge")
        w1f = a.sb("w1f", [P, D])
        w1hi, w1lo = a.sb("w1hi", [P, D], F32R), a.sb("w1lo", [P, D], F32R)
        w2f = a.sb("w2f", [P, DC, D])
        w2hi, w2lo = a.sb("w2hi", [P, DC, D], F32R), a.sb("w2lo", [P, DC, D], F32R)
        b1c = a.sb("b1c", [P, DC])
        b2f = a.sb("b2f", [64, D])
        b2hi, b2parts = a.sb("b2hi", [64, D], F32R), a.sb("b2parts", [64, D], F32R)
        onef = a.sb("onef", [64, P])
        one = a.sb("one", [64, P], F32R)
        src = a.sb("src", [P, NS * ST], I32)
        dst = a.sb("dst", [P, NS * ST], I32)
        dstf = a.sb("dstf", [P, NS * ST])
        starts = a.sb("starts", [P, NS, 4], I32)
        table = a.sb("table", [1, NS, 4], I32)
        xr = [a.sb(f"x{i}", [P, 2 * SUP]) for i in range(2)]
        xs = [a.sb(f"xs{i}", [P, SUP], F32R) for i in range(2)]
        hid = [a.sb(f"hid{i}", [P, DC, SUP]) for i in range(2)]
        hhi = [a.sb(f"hhi{i}", [P, DC, SUP], F32R) for i in range(2)]
        hlo = [a.sb(f"hlo{i}", [P, DC, SUP], F32R) for i in range(2)]
        msg = [a.sb(f"msg{i}", [P, ST * D]) for i in range(2)]
        mhi = [a.sb(f"mhi{i}", [P, ST * D], F16) for i in range(4)]
        mlo = [a.sb(f"mlo{i}", [P, ST * D], F16) for i in range(4)]
        ghs = [a.sb(f"ghs{i}", [P, ST, D]) for i in range(4)]
        idx = [a.sb(f"idx{i}", [P, ST], I32) for i in range(4)]
        oh = [a.sb(f"onehot{i}", [P, ST, WIN], F16) for i in range(2)]
        ohx = a.sb("onehot_extra", [P, ST, WIN], F16)
        p1 = a.ps("p1", [P, DC, SUP])
        p2 = [a.ps(f"p2_{i}", [P, ST, D]) for i in range(2)]
        pg = [a.ps(f"pg{i}", [P, DC, 256]) for i in range(2)]

        consts_in = a.sem("consts_in")
        src_in = a.sem("src_in")
        x_in = [a.sem(f"x_in{i}") for i in range(2)]
        parts_zero = a.sem("parts_zero")
        weights_split = a.sem("weights_split")
        x_split = a.sem("x_split")
        l1_done = a.sem("l1_done")
        silu_done = a.sem("silu_done")
        hi_done = a.sem("hi_done")
        lo_done = a.sem("lo_done")
        l2_done = a.sem("l2_done")
        tanh_done = a.sem("tanh_done")
        rows_in = [a.sem(f"rows_in{i}") for i in range(4)]
        idx_copied = a.sem("idx_copied")
        idx_seen = a.sem("idx_seen")
        msg_done = a.sem("msg_done")
        mhi_done = a.sem("mhi_done")
        mlo_done = a.sem("mlo_done")
        onehot_done = a.sem("onehot_done")
        sum_done = a.sem("sum_done")
        sum_added = a.sem("sum_added")
        extra_onehot = a.sem("extra_onehot")
        extra_sum = a.sem("extra_sum")
        extra_added = a.sem("extra_added")
        xhi_done = a.sem("xhi_done")
        prep = a.sem("prep")
        block = ctx.enter_context(nc.Block())
        NCONST = 9

        @block.sync
        def _(sp):
            sp.dma_start(src[:], src_cols).then_inc(src_in, 16)
            sp.dma_start(w1f[0:NRBF, :], w1).then_inc(consts_in, 16)
            sp.dma_start(w1f[NRBF:P, :], w1).then_inc(consts_in, 16)
            sp.dma_start(w2f[:], w2.rearrange("(c p) n -> p c n", p=P)).then_inc(consts_in, 16)
            sp.dma_start(b1c[:], b1).then_inc(consts_in, 16)
            sp.dma_start(b2f[0:1, :], b2).then_inc(consts_in, 16)
            sp.dma_start(b2f[32:33, :], b2).then_inc(consts_in, 16)
            sp.dma_start(dst[:], dst_cols).then_inc(consts_in, 16)
            sp.dma_start(table[:], seg_table).then_inc(consts_in, 16)
            sp.dma_start(starts[:], seg_table[0].partition_broadcast(P)).then_inc(consts_in, 16)

            def load(q, u, first):
                if not first:
                    sp.wait_ge(x_split, 2 * q - 2)
                cols = bass.ds(q * (2 * SUP), 2 * SUP)
                sp.dma_start(xr[u][0:NRBF, :], rbf[:, cols]).then_inc(x_in[u], 16)
                sp.dma_start(xr[u][NRBF:P, :], rbf[:, cols]).then_inc(x_in[u], 16)

            load(0, 0, True)
            load(1, 1, True)
            with sp.Fori(1, NS // 4) as i:
                for u in range(2):
                    load(i * 2 + u, u, False)

        @block.gpsimd
        def _(pool):
            nc.gpsimd.memset(b2parts[:].bitcast(F32), 0.0).then_inc(parts_zero, 1)
            pool.wait_ge(src_in, 16)

            def gather(k, u, first):
                if not first:
                    pool.wait_ge(msg_done, k - 3)
                nc.gpsimd.tensor_copy(idx[u][:], src[:, bass.ds(k * ST, ST)]).then_inc(idx_copied, 1)
                pool.wait_ge(idx_copied, k + 1)
                pool.sem_inc(idx_seen, 1)
                for t in range(ST):
                    nc.gpsimd.indirect_dma_start(
                        out=ghs[u][:, t, :], out_offset=None, in_=scaled_h,
                        in_offset=bass.IndirectOffsetOnAxis(ap=idx[u][:, t:t + 1], axis=0),
                    ).then_inc(rows_in[u], 16)

            for k in range(4):
                gather(k, k, True)
            with pool.Fori(1, NS // 4) as i:
                for u in range(4):
                    gather(i * 4 + u, u, False)

        @block.scalar
        def _(act):
            act.wait_ge(consts_in, 16 * NCONST)

            def silu(k, u, first):
                act.wait_ge(l1_done, k + 1)
                if not first:
                    act.wait_ge(lo_done, k - 1)
                for c in range(DC):
                    last = nc.scalar.activation(hid[u][:, c, :], p1[:, c, :], ACT.Silu, bias=b1c[:, c:c + 1])
                last.then_inc(silu_done, 1)

            def round_hi(k, u, first):
                act.wait_ge(silu_done, k + 1)
                if not first:
                    act.wait_ge(l2_done, k - 1)
                nc.scalar.activation(hhi[u][:], hid[u][:], ACT.Copy).then_inc(hi_done, 1)

            def tanh(k, u, first):
                act.wait_ge(l2_done, k + 1)
                if not first:
                    act.wait_ge(mlo_done, k - 1)
                nc.scalar.activation(msg[u][:], p2[u][:], ACT.Tanh, scale=0.5).then_inc(tanh_done, 1)

            def round_msg(k, u, first):
                act.wait_ge(msg_done, k + 1)
                if not first:
                    act.wait_ge(sum_added, k - 2)
                nc.scalar.activation(mhi[u][:], msg[u % 2][:], ACT.Copy).then_inc(mhi_done, 1)

            def round_x(k, u, first, loaded):
                act.wait_ge(x_in[(u // 2) % 2], loaded)
                if not first:
                    act.wait_ge(l1_done, k - 1)
                part = xr[(u // 2) % 2][:, (u % 2) * SUP:(u % 2 + 1) * SUP]
                nc.scalar.activation(xs[u % 2][:], part, ACT.Copy).then_inc(xhi_done, 1)

            def step(k, u, start, loaded):
                if loaded is not None:
                    round_x(k + 1, (u + 1) % 4, start < 1, loaded)
                silu(k, u % 2, start < 2)
                round_hi(k, u % 2, start < 2)
                if start >= 2:
                    round_msg(k - 2, (u - 2) % 4, start < 6)
                if start >= 1:
                    tanh(k - 1, (u - 1) % 2, start < 3)

            round_x(0, 0, True, 32)
            for k in range(8):
                step(k, k % 4, k, 32 * ((k + 1) // 4 + 1))
            with act.Fori(2, NS // 4 - 1) as i:
                for u in range(4):
                    step(i * 4 + u, u, 8, i * 32 + (64 if u == 3 else 32))
            for k in range(NS - 4, NS):
                step(k, k % 4, 8, 32 * ((k + 1) // 4 + 1) if k + 1 < NS else None)
            round_msg(NS - 2, (NS - 2) % 4, False)
            tanh(NS - 1, (NS - 1) % 2, False)
            round_msg(NS - 1, (NS - 1) % 4, False)

        @block.vector
        def _(dve):
            n = [0]

            def chain(ins):
                n[0] += 1
                ins.then_inc(prep, 1)
                dve.wait_ge(prep, n[0])

            dve.wait_ge(consts_in, 16 * NCONST)
            split_weight(nc.vector, chain, w1hi[:], w1lo[:], w1f[:])
            split_weight(nc.vector, chain, w2hi[:], w2lo[:], w2f[:])
            dve.wait_ge(parts_zero, 1)
            for row in (0, 32):
                chain(nc.vector.tensor_copy(b2hi[row:row + 1, :], b2f[row:row + 1, :]))
            chain(nc.vector.tensor_copy(b2parts[0:1, :], b2f[0:1, :]))
            chain(nc.vector.tensor_tensor(b2parts[32:33, :], b2f[32:33, :], b2hi[32:33, :].bitcast(F32),
                                          ALU.subtract))
            chain(nc.vector.memset(onef[:], 1.0))
            chain(nc.vector.tensor_copy(one[:], onef[:]))
            nc.vector.tensor_tensor(dstf[:].rearrange("p (s t) -> p s t", t=ST),
                                    dst[:].rearrange("p (s t) -> p s t", t=ST),
                                    starts[:, :, 1:2].broadcast_to([P, NS, ST]), ALU.subtract)\
                .then_inc(weights_split, 1)
            dve.wait_ge(weights_split, 1)

            def split_x(k, u):
                dve.wait_ge(xhi_done, k + 1)
                part = xr[(u // 2) % 2][:, (u % 2) * SUP:(u % 2 + 1) * SUP]
                nc.vector.tensor_tensor(xs[u % 2][NRBF:P, :], part[NRBF:P, :], xs[u % 2][NRBF:P, :].bitcast(F32),
                                        ALU.subtract).then_inc(x_split, 1)

            def lo(k, u, first):
                dve.wait_ge(hi_done, k + 1)
                if not first:
                    dve.wait_ge(l2_done, k - 1)
                nc.vector.tensor_tensor(hlo[u % 2][:], hid[u % 2][:], hhi[u % 2][:].bitcast(F32),
                                        ALU.subtract).then_inc(lo_done, 1)

            def message(k, u, filled):
                dve.wait_ge(tanh_done, k + 1)
                dve.wait_ge(rows_in[u], filled)
                nc.vector.scalar_tensor_tensor(out=msg[u % 2][:], in0=msg[u % 2][:], scalar=1.0,
                                               in1=ghs[u][:].rearrange("p t d -> p (t d)"),
                                               op0=ALU.add, op1=ALU.mult).then_inc(msg_done, 1)

            def low_msg(k, u, first):
                dve.wait_ge(mhi_done, k + 1)
                if not first:
                    dve.wait_ge(sum_added, k - 3)
                nc.vector.tensor_tensor(mlo[u][:], msg[u % 2][:], mhi[u][:], ALU.subtract).then_inc(mlo_done, 1)

            def compare(out, k, offset):
                return nc.vector.tensor_tensor(
                    out, node[:, bass.ds(offset, WIN)].unsqueeze(1).broadcast_to([P, ST, WIN]),
                    dstf[:, bass.ds(k * ST, ST)].unsqueeze(2).broadcast_to([P, ST, WIN]), ALU.is_equal)

            def onehot(k, u, first):
                if not first:
                    dve.wait_ge(sum_done, k - 1)
                compare(oh[u % 2][:], k, 0).then_inc(onehot_done, 1)

            def add(k, u, first, word):
                w0 = nc.s_assert_within(word - word // PACK * PACK, 0, NPAD - 1,
                                        skip_runtime_bounds_check_because="it is a node")
                dve.wait_ge(sum_done, k + 1)
                if not first:
                    dve.wait_ge(sum_added, k)
                part = aggr[:, :, bass.ds(w0, WIN)]
                nc.vector.tensor_tensor(part, part, pg[u % 2][:, :, 0:WIN], ALU.add).then_inc(sum_added, 1)
                extra(k, u, word)

            def extra(k, u, word):
                with dve.If(word >= PACK):
                    w0 = entry(dve, table, k, 1)
                    before = entry(dve, table, k, 2)
                    with dve.Fori(0, word // PACK) as j:
                        dve.wait_ge(sum_added, k + 1)
                        offset = nc.s_assert_within(
                            j * WIN + WIN, 0, NPAD - 1,
                            skip_runtime_bounds_check_because="it is at most the span of the nodes")
                        start = nc.s_assert_within(
                            w0 + j * WIN + WIN, 0, NPAD - 1,
                            skip_runtime_bounds_check_because="it is at most the superblock's last node")
                        compare(ohx[:], k, offset).then_inc(extra_onehot, 1)
                        dve.wait_ge(extra_sum, before + j + 1)
                        part = aggr[:, :, bass.ds(start, WIN)]
                        nc.vector.tensor_tensor(part, part, pg[u % 2][:, :, 0:WIN], ALU.add)\
                            .then_inc(extra_added, 1)
                        dve.wait_ge(extra_added, before + j + 1)

            def step(k, u, start, filled, ahead=True):
                if ahead:
                    split_x(k + 1, (u + 1) % 4)
                if start >= 2:
                    onehot(k - 2, (u - 2) % 4, start < 4)
                lo(k, u, start < 2)
                if start >= 2:
                    low_msg(k - 2, (u - 2) % 4, start < 6)
                if start >= 4:
                    word = entry(dve, table, k - 4, 0)
                if start >= 1:
                    message(k - 1, (u - 1) % 4, filled)
                if start >= 4:
                    add(k - 4, u, start < 5, word)

            def fills(s):
                return 16 * ST * (s // 4 + 1)

            split_x(0, 0)
            for k in range(8):
                step(k, k % 4, k, fills(k - 1))
            with dve.Fori(2, NS // 4 - 1) as i:
                for u in range(4):
                    step(i * 4 + u, u, 8, i * (16 * ST) + (0 if u == 0 else 16 * ST))
            for k in range(NS - 4, NS):
                step(k, k % 4, 8, fills(k - 1), k + 1 < NS)
            low_msg(NS - 2, (NS - 2) % 4, False)
            onehot(NS - 2, (NS - 2) % 4, False)
            message(NS - 1, (NS - 1) % 4, fills(NS - 1))
            add(NS - 4, (NS - 4) % 4, False, entry(dve, table, NS - 4, 0))
            add(NS - 3, (NS - 3) % 4, False, entry(dve, table, NS - 3, 0))
            low_msg(NS - 1, (NS - 1) % 4, False)
            onehot(NS - 1, (NS - 1) % 4, False)
            add(NS - 2, (NS - 2) % 4, False, entry(dve, table, NS - 2, 0))
            add(NS - 1, (NS - 1) % 4, False, entry(dve, table, NS - 1, 0))

        @block.tensor
        def _(pe):
            pe.wait_ge(weights_split, 1)
            pe.wait_ge(consts_in, 16 * NCONST)
            mm = nc.tensor.matmul

            def layer1(k, u, first):
                pe.wait_ge(x_split, k + 1)
                if not first:
                    pe.wait_ge(silu_done, k)
                for c in range(DC):
                    cols = slice(c * P, (c + 1) * P)
                    mm(p1[:, c, :], w1hi[:, cols], xs[u % 2][:], start=True, stop=False)
                    last = mm(p1[:, c, :], w1lo[:, cols], xs[u % 2][:], start=False, stop=True)
                last.then_inc(l1_done, 1)

            def layer2(k, u, first):
                pe.wait_ge(lo_done, k + 1)
                if not first:
                    pe.wait_ge(tanh_done, k - 1)
                for t in range(ST):
                    out = p2[u % 2][:, t, :]
                    mm(out, one[:], b2parts[:], start=True, stop=False)
                    for c in range(DC):
                        hi = hhi[u % 2][:, c, t * P:(t + 1) * P]
                        lo = hlo[u % 2][:, c, t * P:(t + 1) * P]
                        mm(out, hi, w2hi[:, c, :], start=False, stop=False)
                        mm(out, hi, w2lo[:, c, :], start=False, stop=False)
                        last = mm(out, lo, w2hi[:, c, :], start=False, stop=c == DC - 1)
                last.then_inc(l2_done, 1)

            def segment(k, u, one_hot):
                for c in range(DC):
                    for t in range(ST):
                        part = slice(t * D + c * P, t * D + (c + 1) * P)
                        mm(pg[u % 2][:, c, 0:WIN], mhi[u % 4][:, part], one_hot[:, t, :], start=t == 0, stop=False)
                        last = mm(pg[u % 2][:, c, 0:WIN], mlo[u % 4][:, part], one_hot[:, t, :],
                                  start=False, stop=t == ST - 1)
                return last

            def window(k, u, first):
                pe.wait_ge(mlo_done, k + 1)
                pe.wait_ge(onehot_done, k + 1)
                if not first:
                    pe.wait_ge(sum_added, k - 1)
                segment(k, u, oh[u % 2]).then_inc(sum_done, 1)

            def extra(k, u, word):
                with pe.If(word >= PACK):
                    before = entry(pe, table, k, 2)
                    with pe.Fori(0, word // PACK) as j:
                        pe.wait_ge(extra_onehot, before + j + 1)
                        segment(k, u, ohx).then_inc(extra_sum, 1)
                    pe.wait_ge(extra_added, before + word // PACK)

            def step(k, u, start):
                layer1(k, u, start < 1)
                if start >= 1:
                    layer2(k - 1, (u - 1) % 4, start < 3)
                if start >= 4:
                    word = entry(pe, table, k - 4, 0)
                if start >= 3:
                    window(k - 3, (u - 3) % 4, start < 5)
                if start >= 4:
                    extra(k - 4, u, word)

            for k in range(8):
                step(k, k % 4, k)
            with pe.Fori(2, NS // 4) as i:
                for u in range(4):
                    step(i * 4 + u, u, 8)
            layer2(NS - 1, (NS - 1) % 4, False)
            for k in range(NS - 3, NS):
                window(k, k % 4, False)
                extra(k - 1, (k - 1) % 4, entry(pe, table, k - 1, 0))
            extra(NS - 1, (NS - 1) % 4, entry(pe, table, NS - 1, 0))


def x1_place(aggr, g):
    return aggr[:, :, bass.ds(g * GN, GN)]


def x1_view(rows):
    return rows[:].rearrange("p t d -> p (t d)").rearrange("p (c n) -> p c n", c=DC)


def nodes(nc, aggr, fill, x, scaled_h, lists, u1, c1, u2, c2, gate_w, gate_b):
    with ExitStack() as ctx:
        a = Alloc(nc, ctx, "node")
        BF = mybir.dt.bfloat16
        u1f = a.sb("u1", [P, 2 * DC, D])
        u2f = a.sb("u2", [P, DC, D])
        gw = a.sb("gate_w", [P, DC, NE])
        c1c = a.sb("c1", [P, DC])
        c2r = a.sb("c2", [P, D])
        gb = a.sb("gate_b", [P, NE])
        ident = a.sb("ident", [P, P])
        below = a.sb("below", [P, P], BF)
        ones = a.sb("ones", [P, P], BF)
        lower = a.sb("lower", [P, NE, NE])
        xg = [a.sb(f"x{i}", [P, GT, D]) for i in range(2)]
        hg = [a.sb(f"h{i}", [P, GT, D]) for i in range(2)]
        ht = [a.sb(f"ht{i}", [P, DC, GN]) for i in range(2)]
        s2 = a.sb("s2", [P, DC, GN])
        x1 = [a.sb(f"x1_{i}", [P, GT, D]) for i in range(2)]
        f = [a.sb(f"f{i}", [P, GT, DR]) for i in range(2)]
        number = a.sb("number", [P, NE])
        home = a.sb("home", [P, NT])
        ft = a.sb("ft", [P, DC, GN])
        stats = a.sb("stats", [P, GT, nc.vector.BN_STATS_DIM])
        mv = a.sb("mean_var", [P, GT, nc.vector.BN_AGGR_DIM])
        var = a.sb("var", [P, GT])
        guess = a.sb("guess", [P, GT], I32)
        half = a.sb("half", [P, GT])
        rstd = a.sb("rstd", [P, GT])
        logit = a.sb("logit", [P, GT, NE])
        prob = a.sb("prob", [P, GT, NE])
        top = a.sb("top", [P, GT])
        beats = a.sb("beats", [P, GT, NE, NE])
        ties = a.sb("ties", [P, GT, NE, NE])
        rank = a.sb("rank", [P, GT, NE])
        first = a.sb("first", [P, GT, NE])
        second = a.sb("second", [P, GT, NE])
        chosen = a.sb("chosen", [P, GT, NE], BF)
        place = a.sb("place", [P, GT, NE])
        pick = a.sb("pick", [P, GT, NE])
        named = a.sb("named", [P, GT, NE])
        slot_f = a.sb("slot_f", [P, 2, GT])
        ia = [a.sb(f"ia{i}", [P, GT], I32) for i in range(2)]
        ib = [a.sb(f"ib{i}", [P, GT], I32) for i in range(2)]
        pt = a.ps("pt", [P, 2, 512])
        pz = a.ps("pz", [P, 2, 512])
        pu = a.ps("pu", [P, 4, 512])
        plogit = pu[:, 3, 256:256 + GT * NE].rearrange("p (t e) -> p t e", e=NE)
        pplace = pu[:, 3, 320:320 + GT * NE]
        ptotal = pu[:, 3, 384:384 + NE]
        cut = (slice(0, 4 * P), slice(4 * P, GN))

        consts_in = a.sem("consts_in")
        masks = a.sem("masks")
        mask_zero = a.sem("mask_zero")
        prep = a.sem("prep")
        x_in = [a.sem(f"x_in{i}") for i in range(2)]
        turned = a.sem("turned")
        copied = a.sem("copied")
        z_done = a.sem("z_done")
        silu_done = a.sem("silu_done")
        u2_done = a.sem("u2_done")
        x1_done = a.sem("x1_done")
        f_done = a.sem("f_done")
        logit_done = a.sem("logit_done")
        shift_done = a.sem("shift_done")
        exp_done = a.sem("exp_done")
        chosen_done = a.sem("chosen_done")
        place_done = a.sem("place_done")
        slots_done = a.sem("slots_done")
        slots_seen = a.sem("slots_seen")
        f_sent = [a.sem(f"f_sent{i}") for i in range(2)]
        x1_kept = a.sem("x1_kept")
        stats_done = a.sem("stats_done")
        stats_seen = a.sem("stats_seen")
        base_links = a.sem("base_links")
        shift_links = a.sem("shift_links")
        norm_links = a.sem("norm_links")
        router_links = a.sem("router_links")
        route_links = a.sem("route_links")
        block = ctx.enter_context(nc.Block())
        NCONST = 6
        LOOPS = NG // 2

        def rows(ap, g):
            return ap[bass.ds(g * GN, GN), :].rearrange("(t p) d -> p t d", p=P)

        @block.sync
        def _(sp):
            sp.dma_start(u1f[:], u1.rearrange("(c p) n -> p c n", p=P)).then_inc(consts_in, 16)
            sp.dma_start(u2f[:], u2.rearrange("(c p) n -> p c n", p=P)).then_inc(consts_in, 16)
            sp.dma_start(gw[:], gate_w.rearrange("(c p) n -> p c n", p=P)).then_inc(consts_in, 16)
            sp.dma_start(c1c[:], c1).then_inc(consts_in, 16)
            sp.dma_start(c2r[:], c2.partition_broadcast(P)).then_inc(consts_in, 16)
            sp.dma_start(gb[:], gate_b.partition_broadcast(P)).then_inc(consts_in, 16)

            def load(g, u, early):
                if not early:
                    sp.wait_ge(base_links, g * 2 - 3)
                    sp.wait_ge(turned, 2 if isinstance(g, int) and g == 2 else g * 4 - 8)
                sp.dma_start(xg[u][:], rows(x, g)).then_inc(x_in[u], 16)
                sp.dma_start(hg[u][:], rows(scaled_h, g)).then_inc(x_in[u], 16)

            load(0, 0, True)
            load(1, 1, True)
            load(2, 0, False)
            load(3, 1, False)
            with sp.Fori(2, LOOPS) as i:
                for u in range(2):
                    load(i * 2 + u, u, False)
            load(NG - 1, 0, False)

        @block.gpsimd
        def _(pool):
            nc.gpsimd.memset(ident[:], 0.0).then_inc(mask_zero, 1)
            nc.gpsimd.memset(below[:], 1.0).then_inc(mask_zero, 1)
            nc.gpsimd.memset(lower[:], 1.0).then_inc(mask_zero, 1)
            nc.gpsimd.memset(ones[:], 1.0).then_inc(masks, 1)
            nc.gpsimd.iota(home[:], pattern=[[P, NT]], base=XB, channel_multiplier=1,
                           allow_small_or_imprecise_dtypes=True).then_inc(masks, 1)
            pool.wait_ge(mask_zero, 3)
            nc.gpsimd.affine_select(out=ident[:], in_=ident[:], compare_op=ALU.not_equal, fill=1.0, base=0,
                                    pattern=[[-1, P]], channel_multiplier=1).then_inc(masks, 1)
            nc.gpsimd.affine_select(out=below[:], in_=below[:], compare_op=ALU.is_gt, fill=0.0, base=0,
                                    pattern=[[1, P]], channel_multiplier=-1).then_inc(masks, 1)
            nc.gpsimd.affine_select(out=lower[:], in_=lower[:], compare_op=ALU.is_gt, fill=0.0, base=0,
                                    pattern=[[1, NE], [-1, NE]], channel_multiplier=0).then_inc(masks, 1)

            def scatter(g, u):
                pool.wait_ge(slots_done, g + 1)
                pool.sem_inc(slots_seen, 1)
                for t in range(GT):
                    for index in (ia[u], ib[u]):
                        nc.gpsimd.indirect_dma_start(
                            out=lists, out_offset=bass.IndirectOffsetOnAxis(ap=index[:, t:t + 1], axis=0),
                            in_=f[u][:, t, :], in_offset=None).then_inc(f_sent[u], 16)

            with pool.Fori(0, LOOPS) as i:
                for u in range(2):
                    scatter(i * 2 + u, u)
            scatter(NG - 1, 0)
            pool.wait_ge(f_sent[0], 16 * 2 * GT * ((NG + 1) // 2))
            pool.wait_ge(f_sent[1], 16 * 2 * GT * (NG // 2))

        def turns(k):
            if isinstance(k, int) and k == 0:
                return (2, 3), None
            if isinstance(k, int) and k >= NG - 1:
                return None, (4 * (NG - 1) + 2 * (k - NG + 1), 4 * (NG - 1) + 2 * (k - NG + 1) + 1)
            return (k * 4, k * 4 + 3), (k * 4 + 1, k * 4 + 2)

        @block.scalar
        def _(act):
            act.wait_ge(consts_in, 16 * NCONST)

            def copy(n, out):
                act.wait_ge(turned, n + 1)
                for half_cols, cols in enumerate(cut):
                    last = nc.scalar.activation(out[:, cols], pt[:, half_cols, 0:cols.stop - cols.start], ACT.Copy)
                last.then_inc(copied, 1)

            def silu(k, m):
                act.wait_ge(z_done, k * DC + m + 1)
                for half_cols, cols in enumerate(cut):
                    last = nc.scalar.activation(s2[:, m, cols], pz[:, half_cols, 0:cols.stop - cols.start],
                                                ACT.Silu, bias=c1c[:, m:m + 1])
                last.then_inc(silu_done, 1)

            def keep(g, u):
                act.wait_ge(x1_done, g + 1)
                nc.scalar.activation(x1_place(aggr, g), x1_view(x1[u]), ACT.Copy).then_inc(x1_kept, 1)

            def step(k, u):
                at_h, at_f = turns(k)
                fixed = isinstance(k, int)
                if not fixed or k < NG:
                    silu(k, 0)
                    if at_h:
                        copy(at_h[0], ht[1 - u][:, 0, :])
                if not fixed or k >= 1:
                    keep(k - 1, 1 - u)
                if not fixed or k < NG:
                    silu(k, 1)
                if at_f:
                    copy(at_f[0], ft[:, 0, :])
                    copy(at_f[1], ft[:, 1, :])
                if at_h:
                    copy(at_h[1], ht[1 - u][:, 1, :])
                if at_f:
                    act.wait_ge(shift_done, k)
                    nc.scalar.activation(prob[:], logit[:], ACT.Exp).then_inc(exp_done, 1)

            for c in range(DC):
                copy(c, ht[0][:, c, :])
            for k in range(2):
                step(k, k)
            with act.Fori(1, LOOPS) as i:
                for u in range(2):
                    step(i * 2 + u, u)
            for k in range(NG - 1, NG + 1):
                step(k, k % 2)

        @block.tensor
        def _(pe):
            mm = nc.tensor.matmul
            pe.wait_ge(consts_in, 16 * NCONST)
            pe.wait_ge(masks, 5)
            pe.wait_ge(prep, 1)

            def turn(n, tiles, c):
                if not isinstance(n, int) or n > 0:
                    pe.wait_ge(copied, n)
                for t in range(GT):
                    last = nc.tensor.transpose(pt[:, t // 4, (t % 4) * P:(t % 4 + 1) * P],
                                               tiles[:, t, c * P:(c + 1) * P], ident[:])
                last.then_inc(turned, 1)

            def layer1(k, u, m):
                if not isinstance(k, int) or k > 0 or m > 0:
                    pe.wait_ge(silu_done, k * DC + m)
                for half_cols, cols in enumerate(cut):
                    width = cols.stop - cols.start
                    for c in range(2 * DC):
                        if c < DC:
                            moving = ht[u][:, c, cols]
                        else:
                            moving = aggr[:, c - DC, bass.ds(k * GN + cols.start, width)]
                        last = mm(pz[:, half_cols, 0:width], u1f[:, c, m * P:(m + 1) * P], moving,
                                  start=c == 0, stop=c == 2 * DC - 1)
                last.then_inc(z_done, 1)

            def layer2(tiles):
                for t in tiles:
                    for c in range(DC):
                        last = mm(pu[:, t // 2, (t % 2) * D:(t % 2 + 1) * D], s2[:, c, t * P:(t + 1) * P],
                                  u2f[:, c, :], start=c == 0, stop=c == DC - 1)
                return last

            def logits(g):
                for t in range(GT):
                    for c in range(DC):
                        last = mm(plogit[:, t, :], ft[:, c, t * P:(t + 1) * P], gw[:, c, :],
                                  start=c == 0, stop=c == DC - 1)
                last.then_inc(logit_done, 1)

            def places(g):
                pe.wait_ge(chosen_done, g + 1)
                if not isinstance(g, int) or g < NG - 1:
                    pe.wait_ge(x1_done, g + 2)
                sel = chosen[:].rearrange("p t e -> p (t e)")
                mm(pplace, below[:], sel, start=True, stop=False, skip_group_check=True)
                for d in range(1, GT):
                    mm(pplace[:, d * NE:], ones[:], sel[:, 0:(GT - d) * NE], start=False, stop=d == GT - 1,
                       skip_group_check=True)
                for t in range(GT):
                    last = mm(ptotal, ones[:], chosen[:, t, :], start=t == 0, stop=t == GT - 1,
                              skip_group_check=True)
                last.then_inc(place_done, 1)

            def step(k, u, next_loaded):
                fixed = isinstance(k, int)
                updates = not fixed or k < NG
                at_h, at_f = turns(k)
                if updates:
                    pe.wait_ge(copied, 2 if fixed and k == 0 else k * 4)
                    layer1(k, u, 0)
                if at_h:
                    pe.wait_ge(x_in[1 - u], next_loaded)
                    turn(at_h[0], hg[1 - u], 0)
                if not fixed or k >= 2:
                    places(k - 2)
                if updates:
                    layer1(k, u, 1)
                if at_f:
                    pe.wait_ge(f_done, k)
                    turn(at_f[0], f[1 - u], 0)
                if updates:
                    pe.wait_ge(silu_done, k * DC + 2)
                    if not fixed or k > 0:
                        pe.wait_ge(x1_done, k)
                    layer2(range(0, 3))
                if at_f:
                    turn(at_f[1], f[1 - u], 1)
                if not fixed or k >= 2:
                    pe.wait_ge(slots_done, k - 1)
                if updates:
                    layer2(range(3, GT)).then_inc(u2_done, 1)
                if at_h:
                    turn(at_h[1], hg[1 - u], 1)
                if at_f:
                    pe.wait_ge(copied, at_f[1] + 1)
                    logits(k - 1)

            pe.wait_ge(x_in[0], 32)
            for c in range(DC):
                turn(c, hg[0], c)
            step(0, 0, 32)
            step(1, 1, 64)
            with pe.Fori(1, LOOPS) as i:
                for u in range(2):
                    step(i * 2 + u, u, i * 32 + (32 if u == 0 else 64))
            for k in range(NG - 1, NG + 1):
                step(k, k % 2, None)
            places(NG - 1)

        @block.vector
        def _(dve):
            dve.wait_ge(consts_in, 16 * NCONST)
            nc.vector.tensor_scalar(u1f[:, 0:DC, :], u1f[:, 0:DC, :], 1 / H_SCALE, None, ALU.mult)
            nc.vector.tensor_scalar(u1f[:, DC:, :], u1f[:, DC:, :], 1 / MSG_SCALE, None, ALU.mult).then_inc(prep, 1)
            for e in range(NE):
                last = nc.vector.memset(fill[:, e:e + 1], float(e * LIST))
                last = nc.vector.memset(number[:, e:e + 1], float(e))
            last.then_inc(prep, 1)
            dve.wait_ge(prep, 2)
            dve.wait_ge(masks, 5)

            def linker(sem, g, per_group):
                n = [0]

                def link(ins):
                    n[0] += 1
                    assert n[0] <= per_group
                    ins.then_inc(sem, 1)
                    dve.wait_ge(sem, g * per_group + n[0])
                return link

            def base(g, u, loaded):
                link = linker(base_links, g, 2)
                dve.wait_ge(x_in[u], loaded)
                if not isinstance(g, int) or g >= 2:
                    dve.wait_ge(x1_kept, g - 1)
                link(nc.vector.scalar_tensor_tensor(out=x1[u][:], in0=hg[u][:], scalar=1 / H_SCALE, in1=xg[u][:],
                                                    op0=ALU.mult, op1=ALU.add))
                link(nc.vector.tensor_tensor(x1[u][:], x1[u][:], c2r[:].unsqueeze(1).broadcast_to([P, GT, D]),
                                             ALU.add))

            def update(g, u):
                dve.wait_ge(u2_done, g + 1)
                flat = x1[u][:].rearrange("p t d -> p (t d)")
                nc.vector.tensor_tensor(flat, flat, pu[:].rearrange("p b n -> p (b n)")[:, 0:GT * D], ALU.add)\
                    .then_inc(x1_done, 1)
                dve.wait_ge(x1_done, g + 1)

            def norm(g, u, before):
                link = linker(norm_links, g, 16)
                for t in range(GT):
                    last = nc.vector.bn_stats(stats[:, t, :], x1[u][:, t, :])
                last.then_inc(stats_done, 1)
                dve.wait_ge(stats_done, g + 1)
                dve.sem_inc(stats_seen, 1)
                for t in range(GT):
                    last = nc.vector.bn_aggr(mv[:, t, :], stats[:, t, :])
                link(last)
                link(nc.vector.tensor_scalar(var[:], mv[:, :, 1], EPS, None, ALU.add))
                link(nc.vector.tensor_scalar(guess[:], var[:].bitcast(I32), 1, None, ALU.logical_shift_right))
                link(nc.vector.tensor_scalar(rstd[:].bitcast(I32), guess[:], -1.0, float(0x5F375A00),
                                             ALU.mult, ALU.add))
                for _ in range(3):
                    link(nc.vector.tensor_tensor(half[:], rstd[:], rstd[:], ALU.mult))
                    link(nc.vector.tensor_tensor(half[:], half[:], var[:], ALU.mult))
                    link(nc.vector.tensor_scalar(half[:], half[:], -0.5, 1.5, ALU.mult, ALU.add))
                    link(nc.vector.tensor_tensor(rstd[:], rstd[:], half[:], ALU.mult))
                if not isinstance(g, int) or g >= 2:
                    dve.wait_ge(f_sent[u], before * (32 * GT))
                for t in range(GT):
                    last = nc.vector.tensor_scalar(f[u][:, t, 0:D], x1[u][:, t, :], mv[:, t, 0:1],
                                                   rstd[:, t:t + 1], ALU.subtract, ALU.mult)
                last.then_inc(f_done, 1)

            def shift(g):
                link = linker(shift_links, g, 2)
                dve.wait_ge(logit_done, g + 1)
                link(nc.vector.tensor_tensor(logit[:], plogit, gb[:].unsqueeze(1).broadcast_to([P, GT, NE]),
                                             ALU.add))
                link(nc.vector.tensor_reduce(top[:], logit[:], AX.X, ALU.max))
                nc.vector.tensor_tensor(logit[:], logit[:], top[:].unsqueeze(2).broadcast_to([P, GT, NE]),
                                        ALU.subtract).then_inc(shift_done, 1)

            def router(g, u):
                link = linker(router_links, g, 9)
                wide = [P, GT, NE, NE]
                dve.wait_ge(exp_done, g + 1)
                link(nc.vector.tensor_reduce(top[:], prob[:], AX.X, ALU.add))
                link(nc.vector.reciprocal(top[:], top[:]))
                link(nc.vector.tensor_tensor(prob[:], prob[:], top[:].unsqueeze(2).broadcast_to([P, GT, NE]),
                                             ALU.mult))
                other = prob[:].unsqueeze(2).broadcast_to(wide)
                own = prob[:].unsqueeze(3).broadcast_to(wide)
                nc.vector.tensor_tensor(beats[:], other, own, ALU.is_gt)
                link(nc.vector.tensor_tensor(ties[:], other, own, ALU.is_equal))
                link(nc.vector.tensor_tensor(ties[:], ties[:], lower[:].unsqueeze(1).broadcast_to(wide), ALU.mult))
                link(nc.vector.tensor_tensor(beats[:], beats[:], ties[:], ALU.add))
                link(nc.vector.tensor_reduce(rank[:], beats[:], AX.X, ALU.add))
                nc.vector.tensor_scalar(chosen[:], rank[:], 2.0, None, ALU.is_lt).then_inc(chosen_done, 1)
                nc.vector.tensor_scalar(first[:], rank[:], 0.0, None, ALU.is_equal)
                link(nc.vector.tensor_scalar(second[:], rank[:], 1.0, None, ALU.is_equal))
                nc.vector.tensor_tensor(named[:], first[:], number[:].unsqueeze(1).broadcast_to([P, GT, NE]),
                                        ALU.mult)
                nc.vector.tensor_tensor(pick[:], first[:], prob[:], ALU.mult)
                link(nc.vector.tensor_tensor(rank[:], second[:], prob[:], ALU.mult))
                nc.vector.tensor_reduce(f[u][:, :, D], named[:], AX.X, ALU.add)
                nc.vector.tensor_reduce(f[u][:, :, D + 1], pick[:], AX.X, ALU.add)
                nc.vector.tensor_reduce(f[u][:, :, D + 2], rank[:], AX.X, ALU.add)
                nc.vector.tensor_copy(f[u][:, :, D + 3], home[:, bass.ds(g * GT, GT)])

            def route(g, u):
                link = linker(route_links, g, 3)
                dve.wait_ge(place_done, g + 1)
                link(nc.vector.tensor_tensor(place[:], pplace.rearrange("p (t e) -> p t e", e=NE),
                                             fill[:].unsqueeze(1).broadcast_to([P, GT, NE]), ALU.add))
                nc.vector.tensor_tensor(fill[:], fill[:], ptotal, ALU.add)
                nc.vector.tensor_tensor(first[:], first[:], place[:], ALU.mult)
                link(nc.vector.tensor_tensor(second[:], second[:], place[:], ALU.mult))
                nc.vector.tensor_reduce(slot_f[:, 0, :], first[:], AX.X, ALU.add)
                link(nc.vector.tensor_reduce(slot_f[:, 1, :], second[:], AX.X, ALU.add))
                nc.vector.tensor_copy(ia[u][:], slot_f[:, 0, :])
                nc.vector.tensor_copy(ib[u][:], slot_f[:, 1, :]).then_inc(slots_done, 1)
                dve.wait_ge(slots_done, g + 1)

            def step(k, u, before, next_loaded):
                fixed = isinstance(k, int)
                if not fixed or k >= 1:
                    shift(k - 1)
                if not fixed or k < NG:
                    update(k, u)
                if not fixed or k >= 1:
                    router(k - 1, 1 - u)
                if not fixed or k < NG:
                    norm(k, u, before)
                if not fixed or k >= 1:
                    route(k - 1, 1 - u)
                if not fixed or k < NG - 1:
                    base(k + 1, 1 - u, next_loaded)

            base(0, 0, 32)
            step(0, 0, 0, 32)
            step(1, 1, 0, 64)
            with dve.Fori(1, LOOPS) as i:
                for u in range(2):
                    step(i * 2 + u, u, i, i * 32 + (32 if u == 0 else 64))
            for k in range(NG - 1, NG + 1):
                step(k, k % 2, k // 2, None)


def experts(nc, fill, lists, results, w1, b1, w2, b2):
    with ExitStack() as ctx:
        a = Alloc(nc, ctx, "exp")
        count = a.sb("count", [P, NE])
        count_i = a.sb("count_i", [P, NE], I32)
        blocks_i = a.sb("blocks_i", [P, NE], I32)
        blocks_f = a.sb("blocks_f", [P, NE])
        packed = a.sb("packed", [P, NE])
        upto = a.sb("upto", [P, NE])
        nought = a.sb("nought", [P, NE])
        number = a.sb("number", [P, NE])
        table = a.sb("table", [P, NE, 2], I32)
        zeros = a.sb("zeros", [P, XT, DR])
        unread = a.sb("unread", [P, XT])
        ident = a.sb("ident", [P, P])
        w1f = [a.sb(f"w1f{i}", [P, DC, H]) for i in range(2)]
        w2f = [a.sb(f"w2f{i}", [P, HC, D]) for i in range(2)]
        w1hi = [a.sb(f"w1hi{i}", [P, DC, H], F32R) for i in range(2)]
        w1lo = [a.sb(f"w1lo{i}", [P, DC, H], F32R) for i in range(2)]
        w2hi = [a.sb(f"w2hi{i}", [P, HC, D], F32R) for i in range(2)]
        w2lo = [a.sb(f"w2lo{i}", [P, HC, D], F32R) for i in range(2)]
        b1c = a.sb("b1c", [P, NE, HC])
        b2c = a.sb("b2c", [P, NE, DC])
        rows = a.sb("rows", [P, XT, DR])
        behind_f = a.sb("behind_f", [P, XT, DR - D])
        behind_next = a.sb("behind_next", [P, XT, DR - D])
        is_first = a.sb("is_first", [P, XT])
        other = a.sb("other", [P, XT])
        part = a.sb("part", [P, XT])
        weight = a.sb("weight", [P, XT])
        target = a.sb("target", [P, XT])
        index = a.sb("index", [P, XT], I32)
        xhi, xlo = a.sb("xhi", [P, DC, XB], F32R), a.sb("xlo", [P, DC, XB], F32R)
        g = a.sb("g", [P, HC, XB])
        ghi, glo = a.sb("ghi", [P, HC, XB], F32R), a.sb("glo", [P, HC, XB], F32R)
        yt = a.sb("yt", [P, DC, XB])
        y = a.sb("y", [P, XT, D])
        px = a.ps("px", [P, 2, 512])
        pt = px[:].rearrange("p b n -> p (b n)").rearrange("p (c n) -> p c n", c=DC)
        py = px[:].rearrange("p b n -> p (b n)").rearrange("p (t d) -> p t d", d=D)
        p1 = a.ps("p1", [P, HC, XB])
        p2 = a.ps("p2", [P, DC, XB])

        consts_in = a.sem("consts_in")
        zero_done = a.sem("zero_done")
        ident_done = a.sem("ident_done")
        table_done = a.sem("table_done")
        tails_out = [a.sem(f"tails_out{i}") for i in range(2)]
        tails_seen = a.sem("tails_seen")
        w_in = [a.sem(f"w_in{i}") for i in range(2)]
        w_split = a.sem("w_split")
        rows_in = a.sem("rows_in")
        turned = a.sem("turned")
        xhi_done = a.sem("xhi_done")
        xlo_done = a.sem("xlo_done")
        l1_done = a.sem("l1_done")
        gelu_done = a.sem("gelu_done")
        ghi_done = a.sem("ghi_done")
        glo_done = a.sem("glo_done")
        l2_done = a.sem("l2_done")
        yt_done = a.sem("yt_done")
        returned = a.sem("returned")
        y_done = a.sem("y_done")
        y_seen = a.sem("y_seen")
        y_out = a.sem("y_out")
        y_free = a.sem("y_free")
        prep = a.sem("prep")
        taken = a.sem("taken")
        passed_on = a.sem("passed_on")
        rank_links = a.sem("rank_links")
        split_step = a.sem("split_step")
        block = ctx.enter_context(nc.Block())

        def entry(eng, e, column, most):
            return eng.value_load(table[0:1, bass.ds(e, 1), column:column + 1].rearrange("o s c -> o (s c)"),
                                  min_val=0, max_val=most)

        def blocks_of(eng, e):
            word = entry(eng, e, 0, ALL * LISTED + MOST)
            before = nc.s_assert_within(word // LISTED, 0, ALL, skip_runtime_bounds_check_because=WHY)
            blocks = nc.s_assert_within(word & (LISTED - 1), 0, MOST,
                                        skip_runtime_bounds_check_because="NPAD rows fill MOST blocks")
            return blocks, before

        def each_block(eng, blocks, before, body):
            with eng.If(blocks > 0):
                with eng.Fori(0, blocks) as q:
                    m = nc.s_assert_within(before + q, 0, ALL - 1, skip_runtime_bounds_check_because=WHY)
                    body(m, q)

        def all_blocks(eng):
            blocks, before = blocks_of(eng, NE - 1)
            return nc.s_assert_within(before + blocks, 0, ALL, skip_runtime_bounds_check_because=WHY)

        def two_on(e):
            return nc.s_assert_within((e + 2) & (NE - 1), 0, NE - 1,
                                      skip_runtime_bounds_check_because="it is a remainder by NE")

        @block.sync
        def _(sp):
            def tail(e, u):
                row = entry(sp, e, 1, NPAD)
                out = lists[bass.ds(row + e * LIST, XB), :].rearrange("(t p) d -> p t d", p=P)
                sp.dma_start(out, zeros[:]).then_inc(tails_out[u], 16)

            def load(m, row):
                sp.wait_ge(turned, m + 1)
                sp.wait_ge(taken, m + 1)
                sp.dma_start(rows[:], lists[bass.ds(row, XB), :].rearrange("(t p) d -> p t d", p=P))\
                    .then_inc(rows_in, 16)

            sp.wait_ge(zero_done, 3)
            sp.wait_ge(table_done, 1)
            for e in range(2):
                tail(e, e)
            with sp.Fori(0, NE // 2) as i:
                for u in range(2):
                    e = i * 2 + u
                    blocks, before = blocks_of(sp, e)
                    sp.wait_ge(tails_out[u], i * 16 + 16)
                    sp.sem_inc(tails_seen, 1)
                    each_block(sp, blocks, before, lambda m, q: load(m, e * LIST + q * XB))
                    tail(two_on(e), u)
            load(all_blocks(sp), 0)
            for u in range(2):
                sp.wait_ge(tails_out[u], 16 * (NE // 2 + 1))

        @block.gpsimd
        def _(pool):
            nc.gpsimd.memset(zeros[:], 0.0).then_inc(zero_done, 1)
            nc.gpsimd.iota(unread[:], pattern=[[P, XT]], base=0, channel_multiplier=1,
                           allow_small_or_imprecise_dtypes=True).then_inc(zero_done, 1)
            pool.wait_ge(zero_done, 2)
            nc.gpsimd.tensor_copy(zeros[:, :, D + 3], unread[:]).then_inc(zero_done, 1)
            nc.gpsimd.memset(ident[:], 0.0).then_inc(ident_done, 1)
            pool.wait_ge(ident_done, 1)
            nc.gpsimd.affine_select(out=ident[:], in_=ident[:], compare_op=ALU.not_equal, fill=1.0, base=0,
                                    pattern=[[-1, P]], channel_multiplier=1).then_inc(ident_done, 1)
            pool.sem_inc(y_free, 1)
            pool.wait_ge(table_done, 1)

            def store(m):
                pool.wait_ge(y_done, m + 2)
                pool.sem_inc(y_seen, 1)
                for t in range(XT):
                    nc.gpsimd.indirect_dma_start(
                        out=results, out_offset=bass.IndirectOffsetOnAxis(ap=index[:, t:t + 1], axis=0),
                        in_=y[:, t, :], in_offset=None).then_inc(y_out, 16)
                pool.wait_ge(y_out, m * (16 * XT) + 16 * XT)
                pool.sem_inc(y_free, 1)

            with pool.Fori(0, NE) as e:
                each_block(pool, *blocks_of(pool, e), lambda m, q: store(m))
            store(all_blocks(pool))

        @block.scalar
        def _(act):
            def weights(e, u):
                act.dma_start(w1f[u][:], w1[bass.ds(e * D, D), :].rearrange("(c p) n -> p c n", p=P))\
                    .then_inc(w_in[u], 16)
                act.dma_start(w2f[u][:], w2[bass.ds(e * H, H), :].rearrange("(c p) n -> p c n", p=P))\
                    .then_inc(w_in[u], 16)

            weights(0, 0)
            act.dma_start(b1c[:], b1).then_inc(consts_in, 16)
            act.dma_start(b2c[:], b2).then_inc(consts_in, 16)
            act.wait_ge(consts_in, 32)
            act.wait_ge(table_done, 1)

            def column(bias, e, c):
                return bias[:, bass.ds(e, 1), c:c + 1].rearrange("p o c -> p (o c)")

            def round_x(m):
                act.wait_ge(turned, m + 2)
                nc.scalar.activation(xhi[:], pt, ACT.Copy).then_inc(xhi_done, 1)

            def body(m, e):
                for j in range(HC):
                    act.wait_ge(l1_done, m * HC + j + 1)
                    act.wait_ge(glo_done, m * HC + 1)
                    nc.scalar.activation(g[:, j, :], p1[:, j, :], ACT.Gelu, bias=column(b1c, e, j))\
                        .then_inc(gelu_done, 1)
                round_x(m + 1)
                act.wait_ge(l2_done, m + 2)
                for c in range(DC):
                    last = nc.scalar.activation(yt[:, c, :], p2[:, c, :], ACT.Identity, bias=column(b2c, e, c))
                last.then_inc(yt_done, 1)

            act.wait_ge(w_split, 1)
            weights(1, 1)
            round_x(0)
            with act.Fori(0, NE // 2) as i:
                for u in range(2):
                    e = i * 2 + u
                    act.wait_ge(w_split, e + 1)
                    weights(two_on(e), u)
                    each_block(act, *blocks_of(act, e), lambda m, q: body(m, e))
            for u in range(2):
                act.wait_ge(w_in[u], 32 * (NE // 2 + 1))

        @block.vector
        def _(dve):
            n = [0]

            def chain(ins):
                n[0] += 1
                ins.then_inc(prep, 1)
                dve.wait_ge(prep, n[0])

            for e in range(NE):
                last = nc.vector.tensor_scalar(count[:, e:e + 1], fill[:, e:e + 1], float(e * LIST), None,
                                               ALU.subtract)
            nc.vector.memset(nought[:], 0.0)
            chain(last)
            nc.vector.tensor_copy(table[:, :, 1], count[:])
            chain(nc.vector.tensor_scalar(blocks_f[:], count[:], float(XB - 1), None, ALU.add))
            chain(nc.vector.tensor_copy(blocks_i[:], blocks_f[:]))
            chain(nc.vector.tensor_scalar(blocks_i[:], blocks_i[:], XB.bit_length() - 1, None,
                                          ALU.logical_shift_right))
            chain(nc.vector.tensor_copy(blocks_f[:], blocks_i[:]))
            chain(nc.vector.tensor_tensor_scan(upto[:], blocks_f[:], nought[:], 0.0, ALU.add, ALU.add))
            chain(nc.vector.tensor_tensor(upto[:], upto[:], blocks_f[:], ALU.subtract))
            chain(nc.vector.tensor_scalar(packed[:], upto[:], float(LISTED), None, ALU.mult))
            chain(nc.vector.tensor_tensor(packed[:], packed[:], blocks_f[:], ALU.add))
            nc.vector.tensor_copy(table[:, :, 0], packed[:]).then_inc(table_done, 1)
            nc.vector.memset(yt[:], 0.0).then_inc(yt_done, 1)
            for e in range(NE):
                nc.vector.memset(number[:, e:e + 1], float(e))
            nc.vector.memset(weight[:], 0.0)
            dve.wait_ge(zero_done, 3)
            chain(nc.vector.tensor_copy(target[:], unread[:]))
            for start in (xlo_done, glo_done, y_done, taken):
                dve.sem_inc(start, 1)
            dve.wait_ge(table_done, 1)

            def split(u, loaded, step):
                dve.wait_ge(w_in[u], loaded)
                nc.vector.tensor_copy(w1hi[u][:], w1f[u][:])
                nc.vector.tensor_copy(w2hi[u][:], w2f[u][:]).then_inc(split_step, 1)
                dve.wait_ge(split_step, step)
                nc.vector.tensor_tensor(w1lo[u][:], w1f[u][:], w1hi[u][:].bitcast(F32), ALU.subtract)
                nc.vector.tensor_tensor(w2lo[u][:], w2f[u][:], w2hi[u][:].bitcast(F32), ALU.subtract)\
                    .then_inc(w_split, 1)

            def x_low(m):
                dve.wait_ge(xhi_done, m + 1)
                nc.vector.tensor_tensor(xlo[:], pt, xhi[:].bitcast(F32), ALU.subtract).then_inc(xlo_done, 1)

            def leave(m):
                dve.wait_ge(returned, m + 1)
                dve.wait_ge(y_free, m + 1)
                nc.vector.tensor_copy(index[:], target[:])
                nc.vector.tensor_tensor(y[:], py, weight[:].unsqueeze(2).broadcast_to([P, XT, D]), ALU.mult)\
                    .then_inc(y_done, 1)

            def take(m):
                dve.wait_ge(rows_in, m * 16 + 16)
                nc.vector.tensor_copy(behind_next[:], rows[:, :, D:]).then_inc(taken, 1)
                dve.wait_ge(taken, m + 2)

            def ranks(m, e):
                n = [0]

                def link(ins):
                    n[0] += 1
                    ins.then_inc(rank_links, 1)
                    dve.wait_ge(rank_links, m * 4 + n[0])

                link(nc.vector.tensor_scalar(is_first[:], behind_f[:, :, 0],
                                             number[:, bass.ds(e, 1)], None, ALU.is_equal))
                link(nc.vector.tensor_scalar(other[:], is_first[:], -1.0, 1.0, ALU.mult, ALU.add))
                nc.vector.tensor_tensor(part[:], is_first[:], behind_f[:, :, 1], ALU.mult)
                nc.vector.scalar_tensor_tensor(out=target[:], in0=other[:], scalar=float(RANK),
                                               in1=behind_f[:, :, 3], op0=ALU.mult, op1=ALU.add)
                link(nc.vector.tensor_tensor(weight[:], other[:], behind_f[:, :, 2], ALU.mult))
                link(nc.vector.tensor_tensor(weight[:], weight[:], part[:], ALU.add))

            def body(m, e):
                nc.vector.tensor_copy(behind_f[:], behind_next[:]).then_inc(passed_on, 1)
                dve.wait_ge(passed_on, m + 1)
                take(m + 1)
                for j in range(HC):
                    dve.wait_ge(gelu_done, m * HC + j + 1)
                    nc.vector.tensor_copy(ghi[:, j, :], g[:, j, :]).then_inc(ghi_done, 1)
                    dve.wait_ge(ghi_done, m * HC + j + 1)
                    nc.vector.tensor_tensor(glo[:, j, :], g[:, j, :], ghi[:, j, :].bitcast(F32), ALU.subtract)\
                        .then_inc(glo_done, 1)
                x_low(m + 1)
                leave(m)
                ranks(m, e)

            split(0, 32, 1)
            take(0)
            x_low(0)
            with dve.Fori(0, NE // 2) as i:
                for u in range(2):
                    e = i * 2 + u
                    blocks, before = blocks_of(dve, e)
                    dve.wait_ge(l2_done, before + 1)
                    split(1 - u, i * 32 + (32 if u == 0 else 64), e + 2)
                    each_block(dve, blocks, before, lambda m, q: body(m, e))
            leave(all_blocks(dve))

        @block.tensor
        def _(pe):
            mm = nc.tensor.matmul
            pe.sem_inc(turned, 1)
            pe.sem_inc(l2_done, 1)
            pe.wait_ge(ident_done, 2)
            pe.wait_ge(table_done, 1)

            def turn(m):
                pe.wait_ge(rows_in, m * 16 + 16)
                if not isinstance(m, int):
                    pe.wait_ge(y_done, m)
                for c in range(DC):
                    for t in range(XT):
                        last = nc.tensor.transpose(pt[:, c, t * P:(t + 1) * P], rows[:, t, c * P:(c + 1) * P],
                                                   ident[:])
                last.then_inc(turned, 1)

            def turn_back(m):
                for t in range(XT):
                    for c in range(DC):
                        last = nc.tensor.transpose(py[:, t, c * P:(c + 1) * P], yt[:, c, t * P:(t + 1) * P],
                                                   ident[:])
                last.then_inc(returned, 1)

            def body(m, u):
                pe.wait_ge(xlo_done, m + 2)
                for j in range(HC):
                    for c in range(DC):
                        hi, lo = (w[u][:, c, j * P:(j + 1) * P] for w in (w1hi, w1lo))
                        mm(p1[:, j, :], hi, xhi[:, c, :], start=c == 0, stop=False)
                        mm(p1[:, j, :], hi, xlo[:, c, :], start=False, stop=False)
                        last = mm(p1[:, j, :], lo, xhi[:, c, :], start=False, stop=c == DC - 1)
                    last.then_inc(l1_done, 1)
                turn(m + 1)
                pe.wait_ge(yt_done, m + 1)
                for j in range(HC):
                    if j == HC - 1:
                        pe.wait_ge(xlo_done, m + 3)
                        turn_back(m)
                    pe.wait_ge(glo_done, m * HC + j + 2)
                    for c in range(DC):
                        hi, lo = (w[u][:, j, c * P:(c + 1) * P] for w in (w2hi, w2lo))
                        mm(p2[:, c, :], hi, ghi[:, j, :], start=j == 0, stop=False)
                        mm(p2[:, c, :], hi, glo[:, j, :], start=False, stop=False)
                        last = mm(p2[:, c, :], lo, ghi[:, j, :], start=False, stop=j == HC - 1)
                last.then_inc(l2_done, 1)

            turn(0)
            with pe.Fori(0, NE // 2) as i:
                for u in range(2):
                    e = i * 2 + u
                    blocks, before = blocks_of(pe, e)
                    pe.wait_ge(w_split, e + 1)
                    each_block(pe, blocks, before, lambda m, q: body(m, u))
            total = all_blocks(pe)
            pe.wait_ge(yt_done, total + 1)
            pe.wait_ge(xlo_done, total + 2)
            pe.wait_ge(y_done, total + 1)
            turn_back(total)


def combine(nc, aggr, results, out):
    with ExitStack() as ctx:
        a = Alloc(nc, ctx, "comb")
        ya = [a.sb(f"ya{i}", [P, GT, D]) for i in range(NG)]
        yb = [a.sb(f"yb{i}", [P, GT, D]) for i in range(NG)]
        rows_in = [a.sem(f"rows_in{i}") for i in range(NG)]
        half_done = a.sem("half_done")
        sum_done = a.sem("sum_done")
        sent = a.sem("sent")
        block = ctx.enter_context(nc.Block())

        def group(rows, g):
            return rows[g * GN:(g + 1) * GN, :].rearrange("(t p) d -> p t d", p=P)

        @block.sync
        def _(sp):
            for g in range(NG):
                sp.dma_start(ya[g][:], group(results[XB:], g)).then_inc(rows_in[g], 16)
                sp.dma_start(yb[g][:], group(results[RANK + XB:], g)).then_inc(rows_in[g], 16)

        @block.vector
        def _(dve):
            for g in range(NG):
                dve.wait_ge(rows_in[g], 32)
                first, second = x1_view(ya[g]), x1_view(yb[g])
                nc.vector.tensor_tensor(first, x1_place(aggr, g), first, ALU.add).then_inc(half_done, 1)
                dve.wait_ge(half_done, g + 1)
                nc.vector.tensor_tensor(first, first, second, ALU.add).then_inc(sum_done, 1)

        @block.scalar
        def _(act):
            for g in range(NG):
                act.wait_ge(sum_done, g + 1)
                act.dma_start(group(out, g), ya[g][:]).then_inc(sent, 16)
            act.wait_ge(sent, 16 * NG)


def build(nc, x, src_cols, dst_cols, dst_rows, rbf, w1, b1, w2, b2, u1, c1, u2, c2,
          gate_w, gate_b, ew1, eb1, ew2, eb2, out):
    scaled_h = nc.dram_tensor("scaled_h", (NPAD, D), F32, kind="Internal").ap()
    seg_scratch = nc.dram_tensor("seg_scratch", (NS, 2), I32, kind="Internal").ap()
    seg_table = nc.dram_tensor("seg_table", (1, NS, 4), I32, kind="Internal").ap()
    lists = nc.dram_tensor("lists", (NE * LIST, DR), F32, kind="Internal").ap()
    results = nc.dram_tensor("results", (2 * RANK, D), F32, kind="Internal").ap()
    with ExitStack() as ctx:
        a = Alloc(nc, ctx, "all")
        fill = a.sb("fill", [P, NE])
        aggr = ctx.enter_context(nc.sbuf_tensor("aggr", [P, DC, AW], F32))
        with nc.sbuf_tensor("node", [P, AW], F32) as node:
            normalise(nc, node, aggr, x, scaled_h, dst_rows, seg_scratch, seg_table)
            edges(nc, node, aggr, rbf, src_cols, dst_cols, scaled_h, seg_table, w1, b1, w2, b2)
        nodes(nc, aggr, fill, x, scaled_h, lists, u1, c1, u2, c2, gate_w, gate_b)
        experts(nc, fill, lists, results, ew1, eb1, ew2, eb2)
        combine(nc, aggr, results, out)


def kernel(**inputs):
    import concourse.bacc as bacc
    from concourse.bass_utils import run_bass_kernel_spmd

    v = {name: np.asarray(a) for name, a in inputs.items()}

    def padded(a, rows, value=0):
        return np.concatenate([a, np.full((rows - a.shape[0], *a.shape[1:]), value, a.dtype)])

    src = padded(v["src"], EPAD)
    dst = padded(v["dst"], EPAD, NPAD - 1)
    arrays = {
        "x": padded(v["x"], NPAD),
        "src_cols": src.reshape(NS * ST, P).T,
        "dst_cols": dst.reshape(NS * ST, P).T,
        "dst_rows": dst.reshape(2, HALF_S, SUP).transpose(1, 0, 2),
        "rbf": padded(v["edge_attr_64"], EPAD).T,
        "w1": v["L0_gnn_W1"],
        "b1": v["L0_gnn_b1"].reshape(DC, P).T,
        "w2": v["L0_gnn_W2"],
        "b2": v["L0_gnn_b2"].reshape(1, D),
        "u1": v["L0_gnn_U1"],
        "c1": v["L0_gnn_c1"].reshape(DC, P).T,
        "u2": v["L0_gnn_U2"],
        "c2": v["L0_gnn_c2"],
        "gate_w": v["L0_ffn_gate_w"],
        "gate_b": v["L0_ffn_gate_b"],
        "ew1": v["L0_ffn_W1"].reshape(NE * D, H),
        "eb1": v["L0_ffn_b1"].reshape(NE, HC, P).transpose(2, 0, 1),
        "ew2": v["L0_ffn_W2"].reshape(NE * H, D),
        "eb2": v["L0_ffn_b2"].reshape(NE, DC, P).transpose(2, 0, 1),
    }
    nc = bacc.Bacc("TRN2", target_bir_lowering=False, num_devices=1)
    feeds, args = {}, []
    for name, a in arrays.items():
        feeds[f"in_{name}"] = np.ascontiguousarray(a)
        args.append(nc.dram_tensor(f"in_{name}", a.shape, mybir.dt.from_np(a.dtype), kind="ExternalInput").ap())
    out = nc.dram_tensor("out", (NPAD, D), F32, kind="ExternalOutput").ap()
    build(nc, *args, out)
    result = run_bass_kernel_spmd(nc, [feeds], core_ids=[0])
    return result.results[0]["out"][:N_NODES]
```
